# Optimizing a Trainium2 kernel written in Bass

```python
import numpy as np
import jax
import jax.numpy as jnp

def _softmax(x, axis=-1):
    return jax.nn.softmax(x, axis=axis)

def _gelu(x):
    return jax.nn.gelu(x, approximate=True)

def _silu(x):
    return jax.nn.silu(x)

def _sigmoid(x):
    return jax.nn.sigmoid(x)

def _layernorm(x, axis=-1, eps=1e-05):
    m = jnp.mean(x, axis=axis, keepdims=True)
    v = jnp.var(x, axis=axis, keepdims=True)
    return (x - m) / jnp.sqrt(v + eps)

def _scatter_add(tgt, idx, src, axis=0):
    return tgt.at[idx].add(src)

def _segment_sum(src, seg, n):
    return jax.ops.segment_sum(src, seg, n)
kernel_name = 'mk_xattn_ffn_d2_seqx_r4_fc6c06'

def setup_inputs(seed: int=0):
    np.random.seed(seed)
    _w = jnp.asarray

    def _rec_inputs():
        import jax
        import jax.numpy as jnp
        _rk = jax.random.key(seed)
        x = -0.0002928 + 1 * jax.random.normal(jax.random.fold_in(_rk, 1), (128, 128, 256), jnp.float32)
        _lenS = 128 - jax.random.randint(jax.random.fold_in(_rk, 7), (128,), 0, max(1, 128 // 4) + 1, jnp.int32)
        _lenS2 = 128 - jax.random.randint(jax.random.fold_in(_rk, 8), (128,), 0, max(1, 128 // 4) + 1, jnp.int32)
        _ctx_1024P = jax.random.normal(jax.random.fold_in(_rk, 11), (128, 16, 256), jnp.float32)
        _ctx_1024c = jax.random.dirichlet(jax.random.fold_in(_rk, 511), 0.3 * jnp.ones((16,), jnp.float32), (128, 128))
        _ctx_1024t = jnp.einsum('bsk,bkd->bsd', _ctx_1024c, _ctx_1024P)
        _ctx_1024t = _ctx_1024t * jax.lax.rsqrt(jnp.mean(jnp.square(_ctx_1024t)) + 1e-12) * 0.953939
        ctx_1024 = -1.39393e-06 + 0.999914 * (_ctx_1024t + 0.3 * jax.random.normal(jax.random.fold_in(_rk, 611), (128, 128, 256), jnp.float32))
        _validS = jnp.arange(128)[None, :] < _lenS[:, None]
        _validS2 = jnp.arange(128)[None, :] < _lenS2[:, None]
        _causal = jnp.tril(jnp.ones((128, 128), dtype=bool))
        mask_1x1xSxS2_ik1 = jnp.where(jnp.broadcast_to(_validS2[0:1, None, None, :], (1, 1, 128, 128)), 1, 0).astype(jnp.int32)
        return (x, ctx_1024, mask_1x1xSxS2_ik1)
    x, ctx_1024, mask_1x1xSxS2_ik1 = _rec_inputs()

    def _L0_xattn_setup():
        import jax, jax.numpy as jnp
        import numpy as np
        HIDDEN = 256
        HEADS = 16
        D_K = HIDDEN // HEADS
        B, S = (2, 512)
        key = jax.random.key(seed)
        ks = jax.random.split(key, 11)
        sc = 1.0 / np.sqrt(HIDDEN)
        return {'query': jax.random.normal(ks[0], (B, S, HIDDEN), jnp.float32), 'key': jax.random.normal(ks[1], (B, S, HIDDEN), jnp.float32), 'value': jax.random.normal(ks[2], (B, S, HIDDEN), jnp.float32), 'w_q': jax.random.normal(ks[3], (HIDDEN, HIDDEN), jnp.float32) * sc, 'b_q': jax.random.normal(ks[4], (HIDDEN,), jnp.float32) * 0.02, 'w_k': jax.random.normal(ks[5], (HIDDEN, HIDDEN), jnp.float32) * sc, 'b_k': jax.random.normal(ks[6], (HIDDEN,), jnp.float32) * 0.02, 'w_v': jax.random.normal(ks[7], (HIDDEN, HIDDEN), jnp.float32) * sc, 'b_v': jax.random.normal(ks[8], (HIDDEN,), jnp.float32) * 0.02, 'w_o': jax.random.normal(ks[9], (HIDDEN, HIDDEN), jnp.float32) * sc, 'b_o': jax.random.normal(ks[10], (HIDDEN,), jnp.float32) * 0.02}
    _L0_xattn_all = _L0_xattn_setup()
    _L0_xattn_in = {k: v for k, v in _L0_xattn_all.items() if k in ('w_q', 'b_q', 'w_k', 'b_k', 'w_v', 'b_v', 'w_o', 'b_o')}
    del _L0_xattn_all

    def _L0_ffn_setup():
        import jax, jax.numpy as jnp
        import numpy as np
        B, S, D, H, E, TOP_K = (8, 512, 256, 1024, 8, 2)
        key = jax.random.key(seed)
        ks = jax.random.split(key, 7)
        scale = 0.02
        return {'x': jax.random.normal(ks[0], (B, S, D), dtype=jnp.float32), 'Wg': jax.random.normal(ks[1], (D, E), dtype=jnp.float32) * scale, 'bg': jnp.zeros((E,), dtype=jnp.float32), 'W1': jax.random.normal(ks[2], (E, D, H), dtype=jnp.float32) * scale, 'b1': jnp.zeros((E, H), dtype=jnp.float32), 'W2': jax.random.normal(ks[3], (E, H, D), dtype=jnp.float32) * scale, 'b2': jnp.zeros((E, D), dtype=jnp.float32)}
    _L0_ffn_all = _L0_ffn_setup()
    _L0_ffn_in = {k: v for k, v in _L0_ffn_all.items() if k in ('Wg', 'bg', 'W1', 'b1', 'W2', 'b2')}
    del _L0_ffn_all

    def _L1_xattn_setup():
        import jax, jax.numpy as jnp
        import numpy as np
        EMBED = 256
        HEADS = 16
        HEAD_DIM = EMBED // HEADS
        N, S = (2, 512)
        key = jax.random.key(seed)
        ks = jax.random.split(key, 9)
        values = jax.random.normal(ks[0], (N, S, EMBED), dtype=jnp.float32)
        keys_in = jax.random.normal(ks[1], (N, S, EMBED), dtype=jnp.float32)
        query = jax.random.normal(ks[2], (N, S, EMBED), dtype=jnp.float32)
        mask = jax.random.randint(ks[3], (1, 1, S, S), 0, 2, dtype=jnp.int32)
        sc = 1.0 / np.sqrt(HEAD_DIM)
        Wv = jax.random.normal(ks[4], (HEAD_DIM, HEAD_DIM), dtype=jnp.float32) * sc
        Wk = jax.random.normal(ks[5], (HEAD_DIM, HEAD_DIM), dtype=jnp.float32) * sc
        Wq = jax.random.normal(ks[6], (HEAD_DIM, HEAD_DIM), dtype=jnp.float32) * sc
        Wo = jax.random.normal(ks[7], (EMBED, EMBED), dtype=jnp.float32) * (1.0 / np.sqrt(EMBED))
        bo = jax.random.normal(ks[8], (EMBED,), dtype=jnp.float32) * 0.01
        return {'values': values, 'keys': keys_in, 'query': query, 'mask': mask, 'heads': HEADS, 'Wv': Wv, 'Wk': Wk, 'Wq': Wq, 'Wo': Wo, 'bo': bo}
    _L1_xattn_all = _L1_xattn_setup()
    _L1_xattn_in = {k: v for k, v in _L1_xattn_all.items() if k in ('Wv', 'Wk', 'Wq', 'Wo', 'bo')}
    del _L1_xattn_all

    def _L1_ffn_setup():
        import jax, jax.numpy as jnp
        import numpy as np
        import math
        BETA = 0.9
        THRESHOLD = 1.0
        NUM_STEPS = 5
        ALPHA = 2.0

        @jax.custom_vjp
        def spike_fn(u):
            return (u > 0).astype(u.dtype)

        def _spike_fwd(u):
            return (spike_fn(u), u)

        def _spike_bwd(u, g):
            s = jnp.pi / 2.0 * ALPHA * u
            return (g * (ALPHA / 2.0) / (1.0 + s * s),)
        spike_fn.defvjp(_spike_fwd, _spike_bwd)
        key = jax.random.key(seed)
        k1, k2, k3 = jax.random.split(key, 3)
        n_embd = 256
        x = jax.random.normal(k1, (4, 512, n_embd), dtype=jnp.float32)
        W_fc = jax.random.normal(k2, (4 * n_embd, n_embd), dtype=jnp.float32) / math.sqrt(n_embd)
        W_proj = jax.random.normal(k3, (n_embd, 4 * n_embd), dtype=jnp.float32) / math.sqrt(4 * n_embd)
        return {'x': x, 'W_fc': W_fc, 'W_proj': W_proj}
    _L1_ffn_all = _L1_ffn_setup()
    _L1_ffn_in = {k: v for k, v in _L1_ffn_all.items() if k in ('W_fc', 'W_proj')}
    del _L1_ffn_all
    return {'x': x, 'ctx_1024': ctx_1024, 'mask_1x1xSxS2_ik1': mask_1x1xSxS2_ik1, 'L0_xattn_w_q': _L0_xattn_in['w_q'], 'L0_xattn_b_q': _L0_xattn_in['b_q'], 'L0_xattn_w_k': _L0_xattn_in['w_k'], 'L0_xattn_b_k': _L0_xattn_in['b_k'], 'L0_xattn_w_v': _L0_xattn_in['w_v'], 'L0_xattn_b_v': _L0_xattn_in['b_v'], 'L0_xattn_w_o': _L0_xattn_in['w_o'], 'L0_xattn_b_o': _L0_xattn_in['b_o'], 'L0_ffn_Wg': _L0_ffn_in['Wg'], 'L0_ffn_bg': _L0_ffn_in['bg'], 'L0_ffn_W1': _L0_ffn_in['W1'], 'L0_ffn_b1': _L0_ffn_in['b1'], 'L0_ffn_W2': _L0_ffn_in['W2'], 'L0_ffn_b2': _L0_ffn_in['b2'], 'L1_xattn_Wv': _L1_xattn_in['Wv'], 'L1_xattn_Wk': _L1_xattn_in['Wk'], 'L1_xattn_Wq': _L1_xattn_in['Wq'], 'L1_xattn_Wo': _L1_xattn_in['Wo'], 'L1_xattn_bo': _L1_xattn_in['bo'], 'L1_ffn_W_fc': _L1_ffn_in['W_fc'], 'L1_ffn_W_proj': _L1_ffn_in['W_proj']}

def reference(x, ctx_1024, mask_1x1xSxS2_ik1, L0_xattn_w_q, L0_xattn_b_q, L0_xattn_w_k, L0_xattn_b_k, L0_xattn_w_v, L0_xattn_b_v, L0_xattn_w_o, L0_xattn_b_o, L0_ffn_Wg, L0_ffn_bg, L0_ffn_W1, L0_ffn_b1, L0_ffn_W2, L0_ffn_b2, L1_xattn_Wv, L1_xattn_Wk, L1_xattn_Wq, L1_xattn_Wo, L1_xattn_bo, L1_ffn_W_fc, L1_ffn_W_proj):
    import jax
    import jax.numpy as jnp

    def _L0_xattn_ref(query, key, value, w_q, b_q, w_k, b_k, w_v, b_v, w_o, b_o):
        import jax, jax.numpy as jnp
        import numpy as np
        HIDDEN = 256
        HEADS = 16
        D_K = HIDDEN // HEADS
        B, S = (2, 512)
        b, s, _ = query.shape
        q = query @ w_q.T + b_q
        k = key @ w_k.T + b_k
        v = value @ w_v.T + b_v
        q = q.reshape(b, s, HEADS, D_K).transpose(0, 2, 1, 3)
        k = k.reshape(b, s, HEADS, D_K).transpose(0, 2, 1, 3)
        v = v.reshape(b, s, HEADS, D_K).transpose(0, 2, 1, 3)
        scale = jnp.float32(1.0 / np.sqrt(D_K))
        scores = jnp.einsum('bhqd,bhkd->bhqk', q, k) * scale
        probs = jax.nn.softmax(scores, axis=-1)
        y = jnp.einsum('bhqk,bhkd->bhqd', probs, v)
        y = y.transpose(0, 2, 1, 3).reshape(b, s, HIDDEN)
        return y @ w_o.T + b_o

    def _L0_ffn_ref(x, Wg, bg, W1, b1, W2, b2):
        import jax, jax.numpy as jnp
        import numpy as np
        B, S, D, H, E, TOP_K = (8, 512, 256, 1024, 8, 2)
        batch = x.shape[0]
        gate_logits = jnp.einsum('bsd,de->bse', x, Wg) + bg
        top_vals, top_idx = jax.lax.top_k(gate_logits, TOP_K)
        gate_scores = jax.nn.softmax(top_vals, axis=-1)
        out = jnp.zeros_like(x)
        for i in range(TOP_K):
            e = top_idx[..., i].reshape(-1)[:batch]
            h = jax.nn.gelu(jnp.einsum('bsd,bdh->bsh', x, W1[e]) + b1[e][:, None, :], approximate=False)
            y = jnp.einsum('bsh,bhd->bsd', h, W2[e]) + b2[e][:, None, :]
            out = out + gate_scores[..., i:i + 1] * y
        return out

    def _L1_xattn_ref(values, keys, query, mask, heads, Wv, Wk, Wq, Wo, bo):
        import jax, jax.numpy as jnp
        import numpy as np
        EMBED = 256
        HEADS = 16
        HEAD_DIM = EMBED // HEADS
        N, S = (2, 512)
        n, q_len, embed = query.shape
        v_len, k_len = (values.shape[1], keys.shape[1])
        d = embed // heads
        v = values.reshape(n, v_len, heads, d)
        k = keys.reshape(n, k_len, heads, d)
        q = query.reshape(n, q_len, heads, d)
        v = jnp.einsum('nlhd,ed->nlhe', v, Wv)
        k = jnp.einsum('nlhd,ed->nlhe', k, Wk)
        q = jnp.einsum('nlhd,ed->nlhe', q, Wq)
        energy = jnp.einsum('nqhd,nkhd->nhqk', q, k)
        energy = jnp.where(mask == 0, jnp.float32(-1e+20), energy)
        attn = jax.nn.softmax(energy / jnp.sqrt(jnp.float32(embed)), axis=3)
        out = jnp.einsum('nhql,nlhd->nqhd', attn, v).reshape(n, q_len, embed)
        out = out @ Wo.T + bo
        return out

    def _L1_ffn_ref(x, W_fc, W_proj):
        import jax, jax.numpy as jnp
        import numpy as np
        import math
        BETA = 0.9
        THRESHOLD = 1.0
        NUM_STEPS = 5
        ALPHA = 2.0

        @jax.custom_vjp
        def spike_fn(u):
            return (u > 0).astype(u.dtype)

        def _spike_fwd(u):
            return (spike_fn(u), u)

        def _spike_bwd(u, g):
            s = jnp.pi / 2.0 * ALPHA * u
            return (g * (ALPHA / 2.0) / (1.0 + s * s),)
        spike_fn.defvjp(_spike_fwd, _spike_bwd)
        h = jnp.square(jax.nn.relu(jnp.einsum('bsd,fd->bsf', x, W_fc)))
        y = jnp.einsum('bsf,df->bsd', h, W_proj)

        def step(mem, _):
            reset = jax.lax.stop_gradient(spike_fn(mem - THRESHOLD))
            mem_new = BETA * mem + y - reset * THRESHOLD
            spk = spike_fn(mem_new - THRESHOLD)
            return (mem_new, spk)
        mem0 = jnp.zeros_like(y)
        _, spks = jax.lax.scan(step, mem0, None, length=NUM_STEPS)
        return jnp.sum(spks, axis=0) / NUM_STEPS
    x = x + _L0_xattn_ref(_layernorm(x, axis=-1), ctx_1024, ctx_1024, L0_xattn_w_q, L0_xattn_b_q, L0_xattn_w_k, L0_xattn_b_k, L0_xattn_w_v, L0_xattn_b_v, L0_xattn_w_o, L0_xattn_b_o)
    x = x + _L0_ffn_ref(_layernorm(x, axis=-1), L0_ffn_Wg, L0_ffn_bg, L0_ffn_W1, L0_ffn_b1, L0_ffn_W2, L0_ffn_b2)
    x = x + _L1_xattn_ref(ctx_1024, ctx_1024, _layernorm(x, axis=-1), mask_1x1xSxS2_ik1, 16, L1_xattn_Wv, L1_xattn_Wk, L1_xattn_Wq, L1_xattn_Wo, L1_xattn_bo)
    x = x + _L1_ffn_ref(_layernorm(x, axis=-1), L1_ffn_W_fc, L1_ffn_W_proj)
    return x

_drawn_inputs = setup_inputs


def setup_inputs(seed=0):
    import zlib

    import numpy as np

    out = dict(_drawn_inputs(seed))
    spreads = {'L0_ffn_bg': (0.0, 0.1), 'L0_ffn_b1': (0.0, 0.1), 'L0_ffn_b2': (0.0, 0.1)}
    factors = {'L0_xattn_b_q': 5.874, 'L0_xattn_b_k': 8.0, 'L1_xattn_bo': 3.766}
    for name, (base, spread) in spreads.items():
        noise = np.random.default_rng([zlib.crc32(name.encode()), seed]).standard_normal(out[name].shape)
        drawn = base * np.exp(spread * noise) if base else spread * noise
        out[name] = jnp.asarray(drawn.astype(out[name].dtype))
    for name, factor in factors.items():
        out[name] = (out[name] * factor).astype(out[name].dtype)
    return out
```

```python
from contextlib import ExitStack

import concourse.bass as bass
from concourse import mybir

F32 = mybir.dt.float32
F16 = mybir.dt.float16
BF16 = mybir.dt.bfloat16
I32 = mybir.dt.int32
U32 = mybir.dt.uint32
ALU = mybir.AluOpType
ACT = mybir.ActivationFunctionType
AX = mybir.AxisListType

P = 128
S = 128
D = 256
KB = D // P
HEADS = 16
DK = D // HEADS
PAIR = 2
QB = HEADS // 2
EXP = 8
HID = 1024
HB = HID // P
EPS = 1e-5

LN_X, CTX_X, W_X, QK_X, Y_X, H_X = 10, 6, 8, 6, 6, 6
PARTS = 3
CHUNKS = 4
CH = 4


def p2(e):
    return float(2.0 ** e)


class Unit:

    def __init__(self, base, off):
        self.base, self.off = base, off
        self.slot = off % 2
        static = isinstance(base, int)
        self.no = 2 * base + off if static else base * 2 + off
        self.turn = base + off // 2
        self.static = static

    def back(self, lag):
        return Unit(self.base, self.off - lag)


class Sig:

    def __init__(self, sem, per=1, count=None):
        self.sem, self.per, self.count = sem, per, count

    def wait(self, eng, unit, k=None):
        k = self.per if k is None else k
        v = unit.no * self.per + k
        if unit.static:
            if self.count is not None:
                v = min(v, self.count * self.per)
            if v <= 0:
                return
        eng.wait_ge(self.sem, v)


class DmaSig:

    def __init__(self, sems, n=1):
        self.sems, self.n = sems, n

    def inc(self, dma, unit):
        dma.then_inc(self.sems[unit.slot], 16)

    def wait(self, eng, unit):
        if unit.static and unit.no < 0:
            return
        eng.wait_ge(self.sems[unit.slot], (unit.turn + 1) * (16 * self.n))


def settle(eng, ticks):
    eng.sem_inc(ticks, 1)


def run_steps(eng, tasks, count, depth):
    peel = depth + 2 + depth % 2
    if count <= peel:
        for s in range(count + depth):
            for lag, task in tasks:
                if 0 <= s - lag < count:
                    task(Unit(0, s - lag))
        return
    assert count % 2 == 0
    for s in range(peel):
        for lag, task in tasks:
            if s - lag >= 0:
                task(Unit(0, s - lag))
    with eng.Fori(peel // 2, count // 2) as i:
        for k in range(2):
            for lag, task in tasks:
                task(Unit(i, k - lag))
    for s in range(count, count + depth):
        for lag, task in tasks:
            if s - lag < count:
                task(Unit(0, s - lag))


class Bank:

    def __init__(self, users, count):
        self.users, self.count = users, count

    def wait(self, eng, n, unit):
        step_off = unit.off + self.users[n][0]
        for d in range(1, 1 + 8 * len(self.users)):
            m = n - d
            lag, freed, k = self.users[m % len(self.users)]
            if lag == 9999:
                continue
            before = Unit(unit.base, step_off + m // len(self.users) - lag)
            if unit.static and not 0 <= before.off < self.count:
                continue
            freed.wait(eng, before, k)
            return


def split_dma(eng, dst, src):
    return eng.dma_start(dst, src)


class Kit:

    def __init__(self, nc, ctx, stage, whole=None):
        self.nc, self.ctx, self.stage, self.whole, self.sems = nc, ctx, stage, whole or self, []

    def sb(self, name, shape, dt):
        return self.ctx.enter_context(self.nc.sbuf_tensor(f"{self.stage}_{name}", shape, dt))

    def ps(self, name):
        return self.ctx.enter_context(self.nc.psum_tensor(f"{self.stage}_{name}", [P, 512], F32))

    def sem(self, name):
        self.whole.sems.append(self.nc.alloc_semaphore(name=f"{self.stage}_{name}"))
        return self.whole.sems[-1]

    def end_phase(self):
        self.nc.clear_and_free_semaphores(self.sems)
        self.nc.all_engine_barrier()

    def sig(self, name, per=1, count=None):
        return Sig(self.sem(name), per, count)

    def dsig(self, name, n=1):
        return DmaSig([self.sem(f"{name}_a"), self.sem(f"{name}_b")], n)


def three_passes(eng, out, l_hi, l_lo, r_hi, r_lo, start, stop):
    eng.matmul(out, l_hi, r_hi, start=start, stop=False)
    eng.matmul(out, l_hi, r_lo, start=False, stop=False)
    return eng.matmul(out, l_lo, r_hi, start=False, stop=stop)


def constants(nc, k, io):
    c = {}
    c["ident"] = k.sb("ident", [P, P], F32)
    c["identb"] = k.sb("identb", [P, P], BF16)
    c["sel"] = k.sb("sel", [P, HEADS, P], BF16)
    c["ones10"] = k.sb("ones10", [2, D], F16)
    c["ones6"] = k.sb("ones6", [2, D], F16)
    c["minus_half"] = k.sb("minus_half", [P, PAIR], F32)
    s = k.sem("s_const")
    with nc.Block() as block:
        @block.gpsimd
        def _(g):
            g.memset(c["ident"][:, :], 0.0).then_inc(s, 1)
            g.memset(c["identb"][:, :], 0.0).then_inc(s, 1)
            g.memset(c["sel"][:, :, :], 0.0).then_inc(s, 1)
            g.memset(c["ones10"][:, :], p2(LN_X)).then_inc(s, 1)
            g.memset(c["ones6"][:, :], p2(CTX_X)).then_inc(s, 1)
            g.memset(c["minus_half"][:, :], -0.5).then_inc(s, 1)
            g.wait_ge(s, 6)
            n = 6
            for m in ("ident", "identb"):
                g.affine_select(out=c[m][:, :], in_=c[m][:, :], compare_op=ALU.not_equal, fill=1.0,
                                base=0, pattern=[[-1, P]], channel_multiplier=1).then_inc(s, 1)
                n += 1
            for g0 in (0, 64):
                for part in range(PARTS):
                    g.affine_select(out=c["sel"][:, :, :], in_=c["sel"][:, :, :],
                                    compare_op=ALU.not_equal, fill=1.0, base=-(g0 + 16 * part),
                                    pattern=[[-1, HEADS], [0, P]], channel_multiplier=1).then_inc(s, 1)
                    n += 1
                    g.wait_ge(s, n)
    return c


def prepare_weights(nc, k, c, mats, rows):
    out = {}
    jobs = []
    for name, w, tr in mats:
        n_out, n_in = (w.shape[0], w.shape[1]) if tr else (w.shape[1], w.shape[0])
        hi = k.sb(f"{name}_hi", [P, n_in // P, n_out], F16)
        lo = k.sb(f"{name}_lo", [P, n_in // P, n_out], F16)
        out[name] = (hi, lo)
    for name, b in rows:
        out[name] = k.sb(f"{name}_rows", [2, b.shape[-1]], F16)
    with ExitStack() as tmp:
        kk = Kit(nc, tmp, f"{k.stage}_tmp", k.whole)
        bank = [kk.ps(f"prep_ps{i}") for i in range(2)]
        work = []
        loads = []
        for name, w, tr in mats:
            hi, lo = out[name]
            r, cc = w.shape
            raw = kk.sb(f"{name}_raw", [P, r // P, cc], F32) if r >= P else None
            loads.append((raw, w))
            if tr:
                for ib in range(cc // P):
                    for ob in range(0, r // P, 4):
                        nb = min(4, r // P - ob)
                        work.append(("t", raw, ib, ob, nb, hi[:, ib, ob * P:(ob + nb) * P],
                                     lo[:, ib, ob * P:(ob + nb) * P], len(loads)))
            else:
                for ib in range(r // P):
                    work.append(("c", raw, ib, 0, 0, hi[:, ib, :], lo[:, ib, :], len(loads)))
        rrow = {}
        for name, b in rows:
            n = b.shape[-1]
            raw = kk.sb(f"{name}_rawrow", [1, n], F32)
            parts = kk.sb(f"{name}_parts", [1, 2, n], F16)
            rrow[name] = (raw, parts, out[name])
            loads.append((raw, b))
        s_ld, s_t, s_hi, s_lo, s_row = (kk.sem(f"prep_{x}") for x in ("ld", "t", "hi", "lo", "row"))
        tw = [w for w in work if w[0] == "t"]
        with nc.Block() as block:
            @block.sync
            def _(sp):
                for raw, w in loads:
                    if raw.shape[0] == 1:
                        sp.dma_start(raw[:, :], w).then_inc(s_ld, 16)
                    else:
                        sp.dma_start(raw[:, :, :], w.rearrange("(b p) n -> p b n", p=P)).then_inc(s_ld, 16)
                sp.wait_ge(s_lo, len(work) + len(rows))
                for name, b in rows:
                    raw, parts, dst = rrow[name]
                    for i in range(2):
                        sp.dma_start(dst[i:i + 1, :], parts[:, i, :]).then_inc(s_row, 16)
                sp.wait_ge(s_row, 32 * len(rows))

            @block.tensor
            def _(pe):
                pe.wait_ge(s_ld, 16 * len(loads))
                for n, (_, raw, ib, ob, nb, hi, lo, _l) in enumerate(tw):
                    if n >= 2:
                        pe.wait_ge(s_lo, n - 1)
                    for j in range(nb):
                        m = pe.transpose(bank[n % 2][:, j * P:(j + 1) * P],
                                         raw[:, ob + j, ib * P:(ib + 1) * P], c["ident"][:, :])
                    m.then_inc(s_t, 1)

            ordered = tw + [w for w in work if w[0] == "c"]

            @block.scalar
            def _(act):
                act.wait_ge(s_ld, 16 * len(loads))
                for n, (kind, raw, ib, ob, nb, hi, lo, _l) in enumerate(ordered):
                    if kind == "t":
                        act.wait_ge(s_t, n + 1)
                        src = bank[n % 2][:, 0:nb * P]
                    else:
                        src = raw[:, ib, :]
                    act.activation(hi, src, ACT.Copy, scale=p2(W_X)).then_inc(s_hi, 1)
                for name, b in rows:
                    raw, parts, dst = rrow[name]
                    act.activation(parts[:, 0, :], raw[:, :], ACT.Copy, scale=p2(W_X)).then_inc(s_hi, 1)

            @block.vector
            def _(v):
                v.wait_ge(s_ld, 16 * len(loads))
                for n, (kind, raw, ib, ob, nb, hi, lo, _l) in enumerate(ordered):
                    v.wait_ge(s_hi, n + 1)
                    src = bank[n % 2][:, 0:nb * P] if kind == "t" else raw[:, ib, :]
                    v.scalar_tensor_tensor(out=lo, in0=src, scalar=p2(W_X), in1=hi, op0=ALU.mult,
                                           op1=ALU.subtract).then_inc(s_lo, 1)
                for n, (name, b) in enumerate(rows):
                    raw, parts, dst = rrow[name]
                    v.wait_ge(s_hi, len(ordered) + n + 1)
                    v.scalar_tensor_tensor(out=parts[:, 1, :], in0=raw[:, :], scalar=p2(W_X),
                                           in1=parts[:, 0, :], op0=ALU.mult,
                                           op1=ALU.subtract).then_inc(s_lo, 1)
    return out


class Norm:

    def __init__(self, k, name, c, ticks_v, ticks_g):
        self.c, self.ticks_v, self.ticks_g = c, ticks_v, ticks_g
        self.st = [k.sb(f"{name}_st{i}", [P, PAIR, 6], F32) for i in range(2)]
        self.mv = [k.sb(f"{name}_mv{i}", [P, PAIR, 2], F32) for i in range(2)]
        self.ve = [k.sb(f"{name}_ve{i}", [P, PAIR], F32) for i in range(2)]
        self.rs = [k.sb(f"{name}_rs{i}", [P, PAIR], F32) for i in range(2)]
        self.xn = [k.sb(f"{name}_xn{i}", [P, PAIR, D], F32) for i in range(2)]
        self.s_st = k.sig(f"{name}_s_st", PAIR)
        self.s_mv = k.sig(f"{name}_s_mv", PAIR)
        self.s_ve = k.sig(f"{name}_s_ve")
        self.s_rs = k.sig(f"{name}_s_rs")
        self.s_xn = k.sig(f"{name}_s_xn", PAIR)

    def stats(self, v, u, x):
        s = u.slot
        self.s_rs.wait(v, u.back(2))
        for a in range(PAIR):
            v.bn_stats(self.st[s][:, a, :], x[:, a, :]).then_inc(self.s_st.sem, 1)
        for a in range(PAIR):
            self.s_st.wait(v, u, a + 1)
            settle(v, self.ticks_v)
            v.bn_aggr(self.mv[s][:, a, :], self.st[s][:, a, :]).then_inc(self.s_mv.sem, 1)

    def rstd(self, g, u):
        s = u.slot
        self.s_mv.wait(g, u)
        self.s_xn.wait(g, u.back(2))
        settle(g, self.ticks_g)
        g.tensor_scalar(self.ve[s][:, :], self.mv[s][:, :, 1], EPS, p2(-2 * LN_X), ALU.add,
                        ALU.mult).then_inc(self.s_ve.sem, 1)
        self.s_ve.wait(g, u)
        g.tensor_tensor(self.rs[s][:, :], self.ve[s][:, :], self.c["minus_half"][:, :],
                        ALU.pow).then_inc(self.s_rs.sem, 1)

    def apply(self, v, u, x):
        s = u.slot
        self.s_rs.wait(v, u)
        for a in range(PAIR):
            v.tensor_scalar(self.xn[s][:, a, :], x[:, a, :], self.mv[s][:, a, 0:1],
                            self.rs[s][:, a:a + 1], ALU.subtract, ALU.mult).then_inc(self.s_xn.sem, 1)


def transpose_pair(pe, bank, x, ident):
    for kb in range(KB):
        for a in range(PAIR):
            at = (kb * PAIR + a) * P
            m = pe.transpose(bank[:, at:at + P], x[:, a, kb * P:(kb + 1) * P], ident)
    return m


def v4(t):
    return t.rearrange("p (b n) -> p b n", b=KB)


def attention(nc, k0, c, w, io, n_seq, first, glog_top=None, idx_d=None):
    units = n_seq // PAIR
    exp_scale = p2(-2 * QK_X) * (DK ** -0.5 if first else D ** -0.5)
    x_in, x_out, h_out = (io["x"], io["x1"], io["h"]) if first else (io["x2"], io["x3"], io["h3"])
    ctx = ExitStack()
    with ctx:
        k = Kit(nc, ctx, f"{k0.stage}_loop", k0.whole)
        two = lambda name, shape, dt: [k.sb(f"{name}{i}", shape, dt) for i in range(2)]
        xin = two("xin", [P, PAIR, D], F32)
        cin = two("cin", [P, PAIR, D], F32)
        xr = two("xr", [P, PAIR, D], F32)
        xT = two("xT", [P, 2, KB, PAIR * S], F16)
        cT = two("cT", [P, 2, KB, PAIR * S], F16)
        qk = two("qk", [P, 4, KB, PAIR * S], F16)
        qS = two("qS", [P, QB, PAIR * S], F16)
        kS = two("kS", [P, QB, PAIR * S], F16)
        vx = two("vx", [P, PAIR, HEADS, 2 * DK], F32)
        mx = two("mx", [P, PAIR, HEADS], F32)
        nm = two("nm", [P, PAIR, HEADS], F32)
        m3 = two("m3", [P, PAIR, P], BF16)
        mT = two("mT", [P, PAIR, S], BF16)
        pt = [k.sb(f"pt{i}", [P, CH, S], F32) for i in range(4)]
        yE = two("yE", [P, PAIR, 512], F32)
        rec = two("rec", [P, PAIR, HEADS], F32)
        yn = two("yn", [P, PAIR, D], F32)
        yT = two("yT", [P, 2, KB, PAIR * S], F16)
        x1 = two("x1", [P, PAIR, D], F32)
        hT = two("hT", [P, 2, KB, PAIR * S], F16)
        gl = two("gl", [P, PAIR, EXP], F32)
        g8 = two("g8", [P, PAIR, EXP], F32)
        i8 = k.sb("i8", [P, EXP], U32)
        qkd = [nc.dram_tensor(f"qk_scratch{int(first)}{i}", (4, D, PAIR * S), F16, kind="Internal").ap() for i in range(2)]
        ring = [k.ps(f"ring{i}") for i in range(3)]
        sb_ = [k.ps(f"score{i}") for i in range(2)]
        tb = [k.ps(f"scoreT{i}") for i in range(2)]
        avb = k.ps("av")

        tag = "a" if first else "b"
        s_init, N0 = k.sem("s_init"), 8
        ticks_v, ticks_g = k.sem("ticks_v"), k.sem("ticks_g")
        ln0, ln1 = (Norm(k, f"{n}{tag}", c, ticks_v, ticks_g) for n in ("ln0", "ln1"))
        d_x, d_c, d_xr = k.dsig("d_x"), k.dsig("d_c"), k.dsig("d_xr")
        d_qk, d_st, d_x1, d_h = k.dsig("d_qk"), k.dsig("d_st", 12), k.dsig("d_x1"), k.dsig("d_h")
        d_ct = k.dsig("d_ct")
        g = lambda name, per=1: k.sig(name, per)
        s_tx, s_tc, s_xh, s_xl, s_ch, s_cl = g("s_tx"), g("s_tc"), g("s_xh"), g("s_xl"), g("s_ch"), g("s_cl")
        s_q, s_k, s_v, s_qh, s_ql, s_kh, s_kl, s_ve = (g(n) for n in "s_q s_k s_v s_qh s_ql s_kh s_kl s_vev".split())
        NC = PAIR * CHUNKS
        s_s, s_mx, s_st, s_e, s_av = (g(n, NC) for n in "s_s s_mx s_st s_e s_av".split())
        s_ye, s_yt, s_rec, s_yn = (g(n, PAIR) for n in "s_ye s_yt s_rec s_yn".split())
        s_m3, s_mt, s_mte = g("s_m3", 7), g("s_mt"), g("s_mte")
        s_y2, s_yh, s_yl, s_o, s_x1, s_t1, s_hh, s_hl = (g(n) for n in "s_y2 s_yh s_yl s_o s_x1 s_t1 s_hh s_hl".split())
        s_g, s_gl, s_g8, s_gt = g("s_g"), g("s_gl"), g("s_g8", PAIR), g("s_gt")
        s_idx, s_idxd = k.sem("s_idx"), k.sem("s_idxd")
        if first:
            bank0 = Bank([(1, s_xl, 1), (4, s_mte, 1), (2, s_kl, 1), (4, s_yn, 2)], units)
            bank1 = Bank([(1, s_cl, 1), (6, s_gl, 1), (2, s_ve, 1), (5, s_hl, 1)], units)
        else:
            bank0 = Bank([(1, s_xl, 1), (4, s_mte, 1), (9999, s_kl, 1), (4, s_yn, 2)], units)
            bank1 = Bank([(9999, s_cl, 1), (9999, s_gl, 1), (9999, s_ve, 1), (5, s_hl, 1)], units)
        bank2 = Bank([(5, s_x1, 1), (2, s_ql, 1), (4, s_yn, 1), (4, s_yl, 1)], units)

        xv = x_in.rearrange("(u a) s d -> u s a d", a=PAIR)
        cv = io["ctx"].rearrange("(u a) s d -> u s a d", a=PAIR)
        x1v = x_out.rearrange("(u a) s d -> u s a d", a=PAIR)

        with nc.Block() as block:
            @block.sync
            def _(sp):
                def load(u):
                    s = u.slot
                    ln0.s_xn.wait(sp, u.back(2))
                    d_x.inc(sp.dma_start(xin[s][:, :, :], xv[u.no]), u)
                    (s_tc if first else s_ve).wait(sp, u.back(2))
                    d_c.inc(sp.dma_start(cin[s][:, :, :], cv[u.no]), u)

                def store_x1(u):
                    s_x1.wait(sp, u)
                    d_x1.inc(sp.dma_start(x1v[u.no], x1[u.slot][:, :, :]), u)

                def store_h(u):
                    s_hl.wait(sp, u)
                    s_hh.wait(sp, u)
                    d_h.inc(sp.dma_start(h_out[u.no], hT[u.slot][:, :, :, :]), u)

                def reload_x(u):
                    s_x1.wait(sp, u.back(2))
                    d_xr.inc(sp.dma_start(xr[u.slot][:, :, :], xv[u.no]), u)

                def store_ct(u):
                    s_cl.wait(sp, u)
                    s_ch.wait(sp, u)
                    d_ct.inc(sp.dma_start(io["ct"][u.no].rearrange("w (b p) n -> p w b n", p=P),
                                          cT[u.slot][:, :, :, :]), u)

                def stacks(u):
                    s = u.slot
                    s_ql.wait(sp, u)
                    if first:
                        s_kl.wait(sp, u)
                    d_st.wait(sp, u.back(2))
                    n = 4 if first else 2
                    d_qk.inc(sp.dma_start(qkd[s][0:n].rearrange("w (b p) n -> p w b n", p=P), qk[s][:, 0:n, :, :]), u)
                    d_qk.wait(sp, u)
                    s_st.wait(sp, u.back(2))
                    s_s.wait(sp, u.back(2))
                    for dst, order in ((qS, (0, 0, 1)), (kS, (2, 3, 2))):
                        for hh in range(2):
                            for part, which in enumerate(order):
                                src = qkd[s][which] if first or which < 2 else io["ct"][u.no][which - 2]
                                src = src.rearrange("(b h d) n -> h d b n", h=2, d=DK)[hh]
                                at = 64 * hh + DK * part
                                d_st.inc(sp.dma_start(dst[s][at:at + DK, :, :], src), u)

                tasks = [(0, load), (5, store_x1), (6, store_h), (4, reload_x)] + [(2, store_ct)] * first
                run_steps(sp, tasks + [(2, stacks)], units, 6)
                for s in range(2):
                    last = Unit(0, units - 2 + s)
                    d_x1.wait(sp, last)
                    d_h.wait(sp, last)
                    if first:
                        d_ct.wait(sp, last)
                if first:
                    sp.wait_ge(s_idx, 1)
                    sp.dma_start(idx_d, i8[0:n_seq, 0:2]).then_inc(s_idxd, 16)
                    sp.wait_ge(s_idxd, 16)

            @block.gpsimd
            def _(p):
                for s in range(2):
                    p.memset(m3[s][:, :, :], 0.0).then_inc(s_init, 1)
                    p.memset(vx[s][:, :, :, :], 1.0).then_inc(s_init, 1)
                    p.memset(qS[s][:, :, :], 0.0).then_inc(s_init, 1)
                    p.memset(kS[s][:, :, :], 0.0).then_inc(s_init, 1)
                p.wait_ge(s_init, N0)

                def maxima(u):
                    s = u.slot
                    s_mx.wait(p, u)
                    s_mt.wait(p, u.back(2))
                    settle(p, ticks_g)
                    part = [m3[s][:, :, 16 * i:16 * i + 16] for i in range(PARTS)]
                    n = [0]

                    def then(ins):
                        n[0] += 1
                        ins.then_inc(s_m3.sem, 1)
                        s_m3.wait(p, u, n[0])
                        settle(p, ticks_g)
                    then(p.tensor_scalar(nm[s][:, :, :], mx[s][:, :, :], -1.0, None, ALU.mult))
                    then(p.tensor_copy(part[0], nm[s][:, :, :]))
                    then(p.tensor_tensor(nm[s][:, :, :], nm[s][:, :, :], part[0], ALU.subtract))
                    then(p.tensor_copy(part[1], nm[s][:, :, :]))
                    then(p.tensor_tensor(nm[s][:, :, :], nm[s][:, :, :], part[1], ALU.subtract))
                    then(p.tensor_copy(part[2], nm[s][:, :, :]))
                    p.tensor_copy(m3[s][:, :, 64:112], m3[s][:, :, 0:48]).then_inc(s_m3.sem, 1)

                def ctx_as_v(u):
                    d_c.wait(p, u)
                    s_av.wait(p, u.back(2))
                    settle(p, ticks_g)
                    p.tensor_copy(vx[u.slot][:, :, :, 0:DK],
                                  cin[u.slot][:, :, :].rearrange("p a (h d) -> p a h d", d=DK)).then_inc(s_ve.sem, 1)

                tasks = [(5, lambda u: ln1.rstd(p, u)), (0, lambda u: ln0.rstd(p, u))]
                tasks += [] if first else [(2, ctx_as_v)]
                run_steps(p, tasks + [(3, maxima)], units, 6)

            @block.tensor
            def _(pe):
                pe.wait_ge(s_init, N0)
                ident = c["ident"][:, :]

                def t_x(u):
                    ln0.s_xn.wait(pe, u)
                    bank0.wait(pe, 0, u)
                    transpose_pair(pe, ring[0], ln0.xn[u.slot], ident).then_inc(s_tx.sem, 1)

                def t_c(u):
                    d_c.wait(pe, u)
                    bank1.wait(pe, 0, u)
                    transpose_pair(pe, ring[1], cin[u.slot], ident).then_inc(s_tc.sem, 1)

                def project(u, bank, src, name, bias, ones):
                    hi, lo = w[name]
                    x = src[u.slot]
                    for mb in range(KB):
                        o = bank[:, mb * 256:(mb + 1) * 256]
                        for kb in range(KB):
                            three_passes(pe, o, hi[:, kb, mb * P:(mb + 1) * P], lo[:, kb, mb * P:(mb + 1) * P],
                                         x[:, 0, kb, :], x[:, 1, kb, :], kb == 0, False)
                        m = pe.matmul(o, w[bias][:, mb * P:(mb + 1) * P], ones[:, :], start=False, stop=True)
                    return m

                def fold_q(u):
                    s_xl.wait(pe, u)
                    bank2.wait(pe, 1, u)
                    hi, lo = w["wa"]
                    x = xT[u.slot]
                    for kb in range(KB):
                        m = three_passes(pe, ring[2][:, kb * 256:(kb + 1) * 256], hi[:, 0, :], lo[:, 0, :],
                                         x[:, 0, kb, :], x[:, 1, kb, :], True, True)
                    m.then_inc(s_q.sem, 1)

                def project_rows(u, bank, src, name, bias, ones):
                    hi, lo = w[name]
                    x = src[u.slot]
                    for a in range(PAIR):
                        o = bank[:, a * D:(a + 1) * D]
                        at = slice(a * S, (a + 1) * S)
                        for kb in range(KB):
                            three_passes(pe, o, x[:, 0, kb, at], x[:, 1, kb, at], hi[:, kb, :], lo[:, kb, :],
                                         kb == 0, False)
                        m = pe.matmul(o, ones[:, 0:S], w[bias][:, :], start=False, stop=True)
                    return m

                def q(u):
                    s_xl.wait(pe, u)
                    bank2.wait(pe, 1, u)
                    project(u, ring[2], xT, "wq", "bq", c["ones10"]).then_inc(s_q.sem, 1)

                def kk(u):
                    s_cl.wait(pe, u)
                    bank0.wait(pe, 2, u)
                    project(u, ring[0], cT, "wk", "bk", c["ones6"]).then_inc(s_k.sem, 1)

                def vv(u):
                    s_cl.wait(pe, u)
                    bank1.wait(pe, 2, u)
                    project_rows(u, ring[1], cT, "wv", "bv", c["ones6"]).then_inc(s_v.sem, 1)

                def score(n):
                    a, ch = n // CHUNKS, n % CHUNKS
                    hh, g4 = ch // 2, ch % 2
                    rows = slice(64 * hh, 64 * hh + 3 * DK)
                    at = slice(a * S, (a + 1) * S)

                    def go(u):
                        if n == 0:
                            d_st.wait(pe, u)
                        s_mx.wait(pe, u, n - 1)
                        for j in range(CH):
                            b = 4 * g4 + j
                            m = pe.matmul(sb_[n % 2][:, j * S:(j + 1) * S], qS[u.slot][rows, b, at],
                                          kS[u.slot][rows, b, at], start=first or j == 0, stop=first,
                                          skip_group_check=not first)
                        if not first:
                            m = pe.matmul(sb_[n % 2][:, :], c["identb"][:, :], w["mask"][:, :], start=False, stop=True,
                                          skip_group_check=True)
                        m.then_inc(s_s.sem, 1)
                    return go

                def t_max(u):
                    s_m3.wait(pe, u)
                    bank0.wait(pe, 1, u)
                    o = ring[0][:, 0:S].bitcast(BF16)
                    for a in range(PAIR):
                        m = pe.transpose(o[:, a * S:(a + 1) * S], m3[u.slot][:, a, :], c["identb"][:, :])
                    m.then_inc(s_mt.sem, 1)

                def score_t(n):
                    a, ch = n // CHUNKS, n % CHUNKS
                    hh, g4 = ch // 2, ch % 2
                    rows = slice(64 * hh, 64 * hh + 3 * DK)
                    at = slice(a * S, (a + 1) * S)

                    def go(u):
                        s_e.wait(pe, u, n - 1)
                        s_mte.wait(pe, u)
                        o = tb[n % 2][:, :].rearrange("p (j n) -> p j n", j=CH)
                        for j in range(CH):
                            b = 4 * g4 + j
                            pe.matmul(o[:, j, :], kS[u.slot][rows, b, at], qS[u.slot][rows, b, at], start=j == 0,
                                      stop=False, skip_group_check=True)
                        if not first:
                            pe.matmul(tb[n % 2][:, :], c["identb"][:, :], w["maskT"][:, :], start=False, stop=False,
                                      skip_group_check=True)
                        for j in range(CH):
                            m = pe.matmul(o[:, j, :], c["sel"][rows, 8 * hh + 4 * g4 + j, :], mT[u.slot][rows, a, :],
                                          start=False, stop=j == CH - 1, skip_group_check=True)
                        m.then_inc(s_st.sem, 1)
                    return go

                def av(n):
                    a, ch = n // CHUNKS, n % CHUNKS
                    hh, g4 = ch // 2, ch % 2

                    def go(u):
                        s_e.wait(pe, u, n + 1)
                        if n == 0:
                            s_ve.wait(pe, u)
                        if ch == 0:
                            s_ye.wait(pe, u, a)
                        for j in range(CH):
                            head = 2 * (4 * g4 + j) + hh
                            m = pe.matmul(avb[32 * j:32 * j + 32, ch * S:(ch + 1) * S], vx[u.slot][:, a, head, :],
                                          pt[n % 4][:, j, :], start=True, stop=True)
                        m.then_inc(s_av.sem, 1)
                    return go

                def y_rows(a):
                    def go(u):
                        s_ye.wait(pe, u, a + 1)
                        if a == 0:
                            bank2.wait(pe, 2, u)
                        else:
                            bank0.wait(pe, 3, u)
                        for ch in range(CHUNKS):
                            at = slice(ch * P, (ch + 1) * P)
                            m = pe.transpose(ring[2 if a == 0 else 0][:, at], yE[u.slot][:, a, at], ident)
                        m.then_inc(s_yt.sem, 1)
                    return go

                def t_y(u):
                    s_yn.wait(pe, u)
                    bank2.wait(pe, 3, u)
                    transpose_pair(pe, ring[2], yn[u.slot], ident).then_inc(s_y2.sem, 1)

                def o(u):
                    s_yl.wait(pe, u)
                    bank2.wait(pe, 0, u)
                    project_rows(u, ring[2], yT, "wo", "bo", c["ones6"]).then_inc(s_o.sem, 1)

                def t_1(u):
                    ln1.s_xn.wait(pe, u)
                    bank1.wait(pe, 3, u)
                    transpose_pair(pe, ring[1], ln1.xn[u.slot], ident).then_inc(s_t1.sem, 1)

                def gate(u):
                    s_hl.wait(pe, u)
                    bank1.wait(pe, 1, u)
                    hi, lo = w["wg"]
                    for a in range(PAIR):
                        out = ring[1][:, a * EXP:(a + 1) * EXP]
                        at = slice(a * S, (a + 1) * S)
                        for kb in range(KB):
                            three_passes(pe, out, hT[u.slot][:, 0, kb, at], hT[u.slot][:, 1, kb, at], hi[:, kb, :],
                                         lo[:, kb, :], kb == 0, False)
                        m = pe.matmul(out, c["ones10"][:, 0:S], w["bg"][:, :], start=False, stop=True)
                    m.then_inc(s_g.sem, 1)

                tasks = [(1, t_x)] + [(1, t_c)] * first + [(5, o), (4, t_max), (4, score_t(0))] + [(6, gate)] * first
                for n in range(1, NC):
                    tasks += [(4, score_t(n)), (4, av(n - 1))]
                tasks += [(2, q if first else fold_q), (4, av(NC - 1)), (3, score(0)), (3, score(1))]
                tasks += [(2, kk)] * first + [(3, score(2)), (3, score(3))] + [(2, vv)] * first
                tasks += [(3, score(4)), (4, y_rows(0)), (3, score(5)), (4, y_rows(1)), (3, score(6)),
                          (3, score(7)), (5, t_1), (4, t_y)]
                run_steps(pe, tasks, units, 6)

            @block.scalar
            def _(act):
                act.wait_ge(s_init, N0)

                def hi_part(done, src, dst, after, freed, scale):
                    def go(u):
                        after.wait(act, u)
                        for f in freed:
                            f.wait(act, u.back(2))
                        act.activation(dst[u.slot][:, 0, :, :], v4(src), ACT.Copy, scale=scale).then_inc(done.sem, 1)
                    return go

                hi_x = hi_part(s_xh, ring[0][:, :], xT, s_tx, [s_q], 1.0)
                hi_c = hi_part(s_ch, ring[1][:, :], cT, s_tc, [s_v, d_ct], p2(CTX_X))
                hi_y = hi_part(s_yh, ring[2][:, :], yT, s_y2, [s_o], p2(Y_X))
                hi_h = hi_part(s_hh, ring[1][:, :], hT, s_t1, [s_g] * first + [d_h], 1.0)

                def hi_q(u):
                    s_q.wait(act, u)
                    d_qk.wait(act, u.back(2))
                    act.activation(qk[u.slot][:, 0, :, :], v4(ring[2][:, :]), ACT.Copy,
                                   scale=p2(QK_X - LN_X - W_X)).then_inc(s_qh.sem, 1)

                def hi_k(u):
                    s_k.wait(act, u)
                    d_qk.wait(act, u.back(2))
                    act.activation(qk[u.slot][:, 2, :, :], v4(ring[0][:, :]), ACT.Copy,
                                   scale=p2(QK_X - CTX_X - W_X)).then_inc(s_kh.sem, 1)

                def copy_v(u):
                    s_v.wait(act, u)
                    s_av.wait(act, u.back(2))
                    act.activation(vx[u.slot][:, :, :, 0:DK],
                                   ring[1][:, :].rearrange("p (a h d) -> p a h d", a=PAIR, d=DK), ACT.Copy,
                                   scale=p2(-CTX_X - W_X)).then_inc(s_ve.sem, 1)

                def copy_max(u):
                    s_mt.wait(act, u)
                    s_st.wait(act, u.back(2))
                    act.activation(mT[u.slot][:, :, :], ring[0][:, 0:S].bitcast(BF16).rearrange("p (a n) -> p a n", a=PAIR),
                                   ACT.Copy).then_inc(s_mte.sem, 1)

                def expo(n):
                    def go(u):
                        s_st.wait(act, u, n + 1)
                        s_av.wait(act, u, n - 3)
                        act.activation(pt[n % 4][:, :, :], tb[n % 2][:, :].rearrange("p (j n) -> p j n", j=CH),
                                       ACT.Exp, scale=exp_scale).then_inc(s_e.sem, 1)
                    return go

                def copy_y(a):
                    def go(u):
                        s_av.wait(act, u, CHUNKS * (a + 1))
                        s_yt.wait(act, u.back(2), a + 1)
                        act.activation(yE[u.slot][:, a, :], avb[:, :], ACT.Copy).then_inc(s_ye.sem, 1)
                    return go

                def copy_gate(u):
                    s_g.wait(act, u)
                    s_g8.wait(act, u.back(2))
                    act.activation(gl[u.slot][:, :, :], ring[1][:, 0:PAIR * EXP].rearrange("p (a n) -> p a n", a=PAIR),
                                   ACT.Copy, scale=p2(-LN_X - W_X)).then_inc(s_gl.sem, 1)

                tasks = [(1, hi_x)] + [(1, hi_c)] * first + [(4, copy_max)]
                for n in range(NC):
                    tasks.append((4, expo(n)))
                    if n == 1 and first:
                        tasks.append((6, copy_gate))
                    if n == CHUNKS:
                        tasks.append((4, copy_y(0)))
                tasks += [(2, hi_q), (4, copy_y(1))] + [(2, hi_k), (2, copy_v)] * first + [(5, hi_h), (4, hi_y)]
                run_steps(act, tasks, units, 6)

            @block.vector
            def _(v):
                v.wait_ge(s_init, N0)

                def lo_part(done, src, dst, w0, after, freed, scale):
                    def go(u):
                        after.wait(v, u)
                        for f in freed:
                            f.wait(v, u.back(2))
                        v.scalar_tensor_tensor(out=dst[u.slot][:, w0 + 1, :, :], in0=v4(src), scalar=scale,
                                               in1=dst[u.slot][:, w0, :, :], op0=ALU.mult,
                                               op1=ALU.subtract).then_inc(done.sem, 1)
                    return go

                lo_x = lo_part(s_xl, ring[0][:, :], xT, 0, s_xh, [s_q], 1.0)
                lo_c = lo_part(s_cl, ring[1][:, :], cT, 0, s_ch, [s_v, d_ct], p2(CTX_X))
                lo_q = lo_part(s_ql, ring[2][:, :], qk, 0, s_qh, [d_qk], p2(QK_X - LN_X - W_X))
                lo_k = lo_part(s_kl, ring[0][:, :], qk, 2, s_kh, [d_qk], p2(QK_X - CTX_X - W_X))
                lo_y = lo_part(s_yl, ring[2][:, :], yT, 0, s_yh, [s_o], p2(Y_X))
                lo_h = lo_part(s_hl, ring[1][:, :], hT, 0, s_hh, [s_g] * first + [d_h], 1.0)

                def norm0_stats(u):
                    d_x.wait(v, u)
                    ln0.stats(v, u, xin[u.slot])

                def norm0(u):
                    s_tx.wait(v, u.back(2))
                    ln0.apply(v, u, xin[u.slot])

                def add_x(u):
                    s_o.wait(v, u)
                    d_xr.wait(v, u)
                    d_x1.wait(v, u.back(2))
                    v.scalar_tensor_tensor(out=x1[u.slot][:, :, :],
                                           in0=ring[2][:, :].rearrange("p (a n) -> p a n", a=PAIR),
                                           scalar=p2(-Y_X - W_X), in1=xr[u.slot][:, :, :], op0=ALU.mult,
                                           op1=ALU.add).then_inc(s_x1.sem, 1)

                def norm1_stats(u):
                    s_x1.wait(v, u)
                    ln1.stats(v, u, x1[u.slot])

                def norm1(u):
                    s_t1.wait(v, u.back(2))
                    ln1.apply(v, u, x1[u.slot])

                def row_max(n):
                    a, ch = n // CHUNKS, n % CHUNKS

                    def go(u):
                        s_s.wait(v, u, n + 1)
                        if n == 0:
                            s_m3.wait(v, u.back(2))
                        v.tensor_reduce(mx[u.slot][:, a, CH * ch:CH * ch + CH],
                                        sb_[n % 2][:, :].rearrange("p (j n) -> p j n", j=CH), AX.X,
                                        ALU.max).then_inc(s_mx.sem, 1)
                    return go

                def norm_y(a):
                    def go(u):
                        s_yt.wait(v, u, a + 1)
                        s_y2.wait(v, u.back(2))
                        bank = ring[2 if a == 0 else 0]
                        y = bank[:, :].rearrange("p (h n) -> p h n", n=2 * DK)
                        v.reciprocal(rec[u.slot][:, a, :], y[:, :, DK]).then_inc(s_rec.sem, 1)
                        s_rec.wait(v, u, a + 1)
                        r = rec[u.slot][:, a, :].rearrange("p (hh b) -> p hh b", hh=2).unsqueeze(3)
                        v.tensor_tensor(yn[u.slot][:, a, :].rearrange("p (b hh d) -> p hh b d", hh=2, d=DK),
                                        y[:, :, 0:DK].rearrange("p (hh b) d -> p hh b d", hh=2),
                                        r.to_broadcast([P, 2, QB, DK]), ALU.mult).then_inc(s_yn.sem, 1)
                    return go

                def top(u):
                    s_gl.wait(v, u)
                    s_gt.wait(v, u.back(2))
                    settle(v, ticks_v)
                    for a in range(PAIR):
                        v.max(g8[u.slot][:, a, :], gl[u.slot][:, a, :]).then_inc(s_g8.sem, 1)
                    s_g8.wait(v, u)
                    if u.static and u.no == 0:
                        v.max_index(i8[:, :], g8[0][:, 0, :], gl[0][:, 0, :]).then_inc(s_idx, 1)
                    v.tensor_copy(glog_top[:, bass.ts(u.no, PAIR), :], g8[u.slot][:, :, 0:2]).then_inc(s_gt.sem, 1)

                tasks = [(1, lo_x)] + [(1, lo_c)] * first + [(5, add_x), (5, norm1_stats), (0, norm0_stats)]
                tasks += [(6, top)] * first + [(5, norm1), (0, norm0), (2, lo_q), (3, row_max(0)), (3, row_max(1))]
                tasks += [(2, lo_k)] * first + [(3, row_max(2)), (3, row_max(3)), (3, row_max(4)), (4, norm_y(0)), (3, row_max(5)),
                         (4, norm_y(1)), (3, row_max(6)), (3, row_max(7)), (5, lo_h), (4, lo_y)]
                run_steps(v, tasks, units, 6)


def gates(nc, k, top, gate, n_seq):
    with ExitStack() as tmp:
        kk = Kit(nc, tmp, f"{k.stage}_tmp", k.whole)
        e = kk.sb("gate_e", [P, n_seq], F32)
        d = kk.sb("gate_d", [P, n_seq], F32)
        s = kk.sem("s_gate")
        with nc.Block() as block:
            @block.vector
            def _(v):
                v.tensor_tensor(d[:, :], top[:, :, 1], top[:, :, 0], ALU.subtract).then_inc(s, 1)
                v.wait_ge(s, 2)
                v.tensor_scalar(d[:, :], e[:, :], 1.0, None, ALU.add).then_inc(s, 1)
                v.wait_ge(s, 3)
                v.reciprocal(d[:, :], d[:, :]).then_inc(s, 1)
                v.wait_ge(s, 4)
                v.tensor_scalar(gate[:, :, 0], d[:, :], p2(-H_X - W_X), None, ALU.mult).then_inc(s, 1)
                v.wait_ge(s, 5)
                v.tensor_tensor(gate[:, :, 1], gate[:, :, 0], e[:, :], ALU.mult).then_inc(s, 1)

            @block.scalar
            def _(act):
                act.wait_ge(s, 1)
                act.activation(e[:, :], d[:, :], ACT.Exp).then_inc(s, 1)


def prepare_experts(nc, k, c, io, idx_d, n_seq):
    w = {"w1_hi": k.sb("w1_hi", [P, EXP, KB, HID], F16), "w1_lo": k.sb("w1_lo", [P, EXP, KB, HID], F16),
         "w2_hi": k.sb("w2_hi", [P, EXP, HB, D], F16), "w2_lo": k.sb("w2_lo", [P, EXP, HB, D], F16),
         "b1": k.sb("b1T", [P, EXP * HB], F32), "idx": k.sb("idx", [1, 2 * n_seq], U32)}
    jobs = []
    for e in range(EXP):
        jobs.append((io["L0_ffn_W1"][e].rearrange("(b p) n -> p b n", p=P), "w1", e))
        jobs.append((io["L0_ffn_W2"][e].rearrange("(b p) n -> p b n", p=P), "w2", e))
    N = len(jobs)
    with ExitStack() as tmp:
        kk = Kit(nc, tmp, f"{k.stage}_expert", k.whole)
        raw = [kk.sb(f"expert_raw{i}", [P, KB * HID], F32) for i in range(3)]
        b1r = kk.sb("b1_raw", [EXP * HB, P], F32)
        bank = kk.ps("b1_ps")
        s_ld = [kk.sem(f"expert_ld{i}") for i in range(3)]
        s_hi, s_lo, s_b, s_t, s_i = (kk.sem(f"expert_{x}") for x in ("hi", "lo", "b", "t", "i"))

        def view(i, name):
            return raw[i % 3][:, :].rearrange("p (b n) -> p b n", b=KB if name == "w1" else HB)
        with nc.Block() as block:
            @block.sync
            def _(sp):
                sp.dma_start(b1r[:, :], io["L0_ffn_b1"].rearrange("e (b p) -> (e b) p", p=P)).then_inc(s_b, 16)
                sp.dma_start(w["idx"][:, :], idx_d.rearrange("(o t) n -> o (t n)", o=1)).then_inc(s_i, 16)
                for i, (src, name, e) in enumerate(jobs):
                    if i >= 3:
                        sp.wait_ge(s_lo, i - 2)
                    sp.dma_start(view(i, name), src).then_inc(s_ld[i % 3], 16)
                sp.wait_ge(s_i, 16)

            @block.tensor
            def _(pe):
                pe.wait_ge(s_b, 16)
                pe.transpose(bank[:, 0:EXP * HB], b1r[:, :], c["ident"][0:EXP * HB, 0:EXP * HB]).then_inc(s_t, 1)

            @block.scalar
            def _(act):
                for i, (src, name, e) in enumerate(jobs):
                    act.wait_ge(s_ld[i % 3], 16 * (i // 3 + 1))
                    act.activation(w[f"{name}_hi"][:, e, :, :], view(i, name), ACT.Copy, scale=p2(W_X)).then_inc(s_hi, 1)

            @block.vector
            def _(v):
                v.wait_ge(s_t, 1)
                v.tensor_copy(w["b1"][:, :], bank[:, 0:EXP * HB])
                for i, (src, name, e) in enumerate(jobs):
                    v.wait_ge(s_hi, i + 1)
                    hi = w[f"{name}_hi"][:, e, :, :]
                    v.scalar_tensor_tensor(out=w[f"{name}_lo"][:, e, :, :], in0=view(i, name), scalar=p2(W_X), in1=hi,
                                           op0=ALU.mult, op1=ALU.subtract).then_inc(s_lo, 1)
    return w


def experts(nc, k0, c, w, io, n_seq, gate):
    units = n_seq // PAIR
    NC = PAIR * 2 * 2
    with ExitStack() as ctx:
        k = Kit(nc, ctx, f"{k0.stage}_loop", k0.whole)
        two = lambda name, shape, dt: [k.sb(f"{name}{i}", shape, dt) for i in range(2)]
        hT = two("moe_h", [P, 2, KB, PAIR * S], F16)
        x1 = two("moe_x1", [P, PAIR, D], F32)
        x2 = two("moe_x2", [P, PAIR, D], F32)
        t2 = two("moe_t2", [P, PAIR, D], F32)
        NH = 4
        hf = [k.sb(f"hf{i}", [P, 4, S], F32) for i in range(NH)]
        hh = [k.sb(f"hh{i}", [P, 4, S], F16) for i in range(NH)]
        hl = [k.sb(f"hl{i}", [P, 4, S], F16) for i in range(NH)]
        hb_ = [k.ps(f"hid{i}") for i in range(4)]
        yb = [k.ps(f"moe_y{i}") for i in range(2)]
        d_h, d_x, d_o = k.dsig("m_h"), k.dsig("m_x"), k.dsig("m_o")
        s_m1, s_ge, s_hi, s_lo, s_m2 = (k.sig(f"m_{n}", NC) for n in "m1 ge hi lo m2".split())
        s_t2, s_x2 = k.sig("m_t2", PAIR), k.sig("m_x2", PAIR)
        x1v = io["x1"].rearrange("(u a) s d -> u s a d", a=PAIR)
        x2v = io["x2"].rearrange("(u a) s d -> u s a d", a=PAIR)

        with nc.Block() as block:
            @block.sync
            def _(sp):
                def load(u):
                    s_m1.wait(sp, u.back(2))
                    d_h.inc(sp.dma_start(hT[u.slot][:, :, :, :], io["h"][u.no]), u)
                    s_t2.wait(sp, u.back(2))
                    d_x.inc(sp.dma_start(x1[u.slot][:, :, :], x1v[u.no]), u)

                def store(u):
                    s_x2.wait(sp, u)
                    d_o.inc(sp.dma_start(x2v[u.no], x2[u.slot][:, :, :]), u)
                run_steps(sp, [(0, load), (3, store)], units, 3)
                for s in range(2):
                    d_o.wait(sp, Unit(0, units - 2 + s))

            @block.tensor
            def _(pe):
                e_now, e_before = {}, {}

                def read_experts(into):
                    def go(u):
                        for n in range(2 * PAIR):
                            into[n] = pe.value_load(w["idx"][0:1, bass.ds(u.no * (2 * PAIR) + n, 1)], min_val=0,
                                                    max_val=EXP - 1)
                    return go

                def up(n):
                    a, ex, half = n // 4, n // 2 % 2, n % 2

                    def go(u):
                        if n == 0:
                            d_h.wait(pe, u)
                        s_ge.wait(pe, u, n - 3)
                        at = slice(a * S, (a + 1) * S)
                        e = e_now[2 * a + ex]
                        for j in range(4):
                            cols = slice((4 * half + j) * P, (4 * half + j + 1) * P)
                            for kb in range(KB):
                                m = three_passes(pe, hb_[n % 4][:, j * S:(j + 1) * S],
                                                 w["w1_hi"][:, bass.ds(e, 1), kb, cols].rearrange("p o n -> p (o n)"),
                                                 w["w1_lo"][:, bass.ds(e, 1), kb, cols].rearrange("p o n -> p (o n)"),
                                                 hT[u.slot][:, 0, kb, at], hT[u.slot][:, 1, kb, at], kb == 0,
                                                 kb == KB - 1)
                        m.then_inc(s_m1.sem, 1)
                    return go

                def down(n, table):
                    a, ex, half = n // 4, n // 2 % 2, n % 2

                    def go(u):
                        s_lo.wait(pe, u, n + 1)
                        if n % 4 == 0:
                            s_x2.wait(pe, u.back(1), a + 1)
                        e = table[2 * a + ex]
                        o = yb[a][:, ex * D:(ex + 1) * D]
                        for j in range(4):
                            m = three_passes(pe, o, hh[n % NH][:, j, :], hl[n % NH][:, j, :],
                                             w["w2_hi"][:, bass.ds(e, 1), 4 * half + j, :].rearrange("p o n -> p (o n)"),
                                             w["w2_lo"][:, bass.ds(e, 1), 4 * half + j, :].rearrange("p o n -> p (o n)"),
                                             half == 0 and j == 0, False)
                        if half == 1:
                            m = pe.matmul(o, c["ones6"][:, 0:S], w["b2"][:, bass.ds(e * D, D)], start=False, stop=True)
                        m.then_inc(s_m2.sem, 1)
                    return go

                tasks = [(2, read_experts(e_before)), (1, read_experts(e_now))]
                for n in range(NC):
                    tasks.append((1, up(n)))
                    tasks.append((1, down(n - 3, e_now)) if n >= 3 else (2, down(n + NC - 3, e_before)))
                run_steps(pe, tasks, units, 3)

            @block.scalar
            def _(act):
                e_now = {}

                def read_experts(u):
                    for n in range(2 * PAIR):
                        e_now[n] = act.value_load(w["idx"][0:1, bass.ds(u.no * (2 * PAIR) + n, 1)], min_val=0,
                                                  max_val=EXP - 1)

                def gelu(n):
                    a, ex, half = n // 4, n // 2 % 2, n % 2

                    def go(u):
                        s_m1.wait(act, u, n + 1)
                        s_lo.wait(act, u, n + 1 - NH)
                        e = e_now[2 * a + ex]
                        for j in range(4):
                            i = act.activation(hf[n % NH][:, j, :], hb_[n % 4][:, j * S:(j + 1) * S], ACT.Gelu,
                                               bias=w["b1"][:, bass.ds(e * HB + (4 * half + j), 1)],
                                               scale=p2(-LN_X - W_X))
                        i.then_inc(s_ge.sem, 1)
                    return go
                run_steps(act, [(1, read_experts)] + [(1, gelu(n)) for n in range(NC)], units, 3)

            @block.vector
            def _(v):
                def split(n):
                    def go(u):
                        s_ge.wait(v, u, n + 1)
                        s_m2.wait(v, u, n + 1 - NH)
                        v.tensor_scalar(hh[n % NH][:, :, :], hf[n % NH][:, :, :], p2(H_X), None, ALU.mult)\
                         .then_inc(s_hi.sem, 1)
                        s_hi.wait(v, u, n + 1)
                        v.scalar_tensor_tensor(out=hl[n % NH][:, :, :], in0=hf[n % NH][:, :, :], scalar=p2(H_X),
                                               in1=hh[n % NH][:, :, :], op0=ALU.mult, op1=ALU.subtract)\
                         .then_inc(s_lo.sem, 1)
                    return go

                def add(a):
                    def go(u):
                        s_m2.wait(v, u, 4 * (a + 1))
                        if a == 0:
                            d_x.wait(v, u)
                            d_o.wait(v, u.back(2))
                        s = u.slot
                        g = [gate[:, bass.ds(u.no * PAIR + a, 1), ex] for ex in range(2)]
                        v.scalar_tensor_tensor(out=t2[s][:, a, :], in0=yb[a][:, 0:D], scalar=g[0], in1=x1[s][:, a, :],
                                               op0=ALU.mult, op1=ALU.add).then_inc(s_t2.sem, 1)
                        s_t2.wait(v, u, a + 1)
                        v.scalar_tensor_tensor(out=x2[s][:, a, :], in0=yb[a][:, D:2 * D], scalar=g[1],
                                               in1=t2[s][:, a, :], op0=ALU.mult, op1=ALU.add).then_inc(s_x2.sem, 1)
                    return go

                tasks = []
                for n in range(NC):
                    tasks.append((1, split(n)))
                    if n == 2:
                        tasks.append((2, add(1)))
                    if n == NC - 1:
                        tasks.append((1, add(0)))
                run_steps(v, tasks, units, 3)


def prepare_shared_heads(nc, k, c, io, w):
    for name, n in (("wa", P), ("wo", D)):
        nb = 1 if name == "wa" else KB
        w[name] = (k.sb(f"{name}2_hi", [P, nb, n], F16), k.sb(f"{name}2_lo", [P, nb, n], F16))
    w["mask"] = k.sb("mask4", [P, CH * S], BF16)
    w["maskT"] = k.sb("maskT4", [P, CH * S], BF16)
    masked = -1e20 * p2(2 * QK_X)
    with ExitStack() as tmp:
        kk = Kit(nc, tmp, f"{k.stage}_shared", k.whole)
        bd = [kk.sb(f"bd{i}", [P, P], F32) for i in range(3)]
        wo = kk.sb("wo_raw2", [P, KB, D], F32)
        woT = kk.sb("woT2", [P, KB, D], F32)
        mi = kk.sb("mask_int", [P, S], I32)
        mf = kk.sb("mask_f", [P, S], F32)
        b1, b2, b3, b4 = (kk.ps(f"sh_ps{i}") for i in range(4))
        s_z, s_ld, s_mk, s_pe, s_v, s_a = (kk.sem(f"sh_{x}") for x in ("z", "ld", "mk", "pe", "v", "a"))
        with nc.Block() as block:
            @block.gpsimd
            def _(g):
                for t in bd:
                    g.memset(t[:, :], 0.0).then_inc(s_z, 1)

            @block.sync
            def _(sp):
                sp.dma_start(mi[:, :], io["mask"].rearrange("a b s n -> (a b s) n")).then_inc(s_mk, 16)
                sp.wait_ge(s_z, 3)
                for t, name in zip(bd, ("Wq", "Wk", "Wv")):
                    for h in range(P // DK):
                        at = slice(h * DK, (h + 1) * DK)
                        sp.dma_start(t[at, at], io[f"L1_xattn_{name}"]).then_inc(s_ld, 16)
                sp.dma_start(wo[:, :, :], io["L1_xattn_Wo"].rearrange("(b p) n -> p b n", p=P)).then_inc(s_ld, 16)

            @block.tensor
            def _(pe):
                pe.wait_ge(s_ld, 16 * (3 * (P // DK) + 1))
                pe.matmul(b1[:, 0:P], bd[0][:, :], bd[1][:, :], start=True, stop=True).then_inc(s_pe, 1)
                for ib in range(KB):
                    for ob in range(KB):
                        m = pe.transpose(b2[:, ib * D + ob * P:ib * D + (ob + 1) * P], wo[:, ob, ib * P:(ib + 1) * P],
                                         c["ident"][:, :])
                m.then_inc(s_pe, 1)
                pe.wait_ge(s_v, 1)
                for ib in range(KB):
                    m = pe.matmul(b3[:, ib * D:(ib + 1) * D], bd[2][:, :], woT[:, ib, :], start=True, stop=True)
                m.then_inc(s_pe, 1)
                pe.wait_ge(s_v, 6)
                pe.transpose(b4[:, 0:S // 2].bitcast(BF16), w["mask"][:, 0:S], c["identb"][:, :]).then_inc(s_pe, 1)

            @block.scalar
            def _(act):
                act.wait_ge(s_pe, 1)
                act.activation(w["wa"][0][:, 0, :], b1[:, 0:P], ACT.Copy, scale=p2(W_X)).then_inc(s_a, 1)
                act.wait_ge(s_pe, 3)
                act.activation(w["wo"][0][:, :, :], v4(b3[:, :]), ACT.Copy, scale=p2(W_X)).then_inc(s_a, 1)

            @block.vector
            def _(v):
                v.wait_ge(s_pe, 2)
                v.tensor_copy(woT[:, :, :], v4(b2[:, :])).then_inc(s_v, 1)
                v.wait_ge(s_mk, 16)
                v.tensor_scalar(mf[:, :], mi[:, :], 0.0, masked, ALU.is_equal, ALU.mult).then_inc(s_v, 1)
                v.wait_ge(s_v, 2)
                for j in range(CH):
                    v.tensor_copy(w["mask"][:, j * S:(j + 1) * S], mf[:, :]).then_inc(s_v, 1)
                v.wait_ge(s_a, 1)
                v.scalar_tensor_tensor(out=w["wa"][1][:, 0, :], in0=b1[:, 0:P], scalar=p2(W_X), in1=w["wa"][0][:, 0, :],
                                       op0=ALU.mult, op1=ALU.subtract)
                v.wait_ge(s_a, 2)
                v.scalar_tensor_tensor(out=w["wo"][1][:, :, :], in0=v4(b3[:, :]), scalar=p2(W_X),
                                       in1=w["wo"][0][:, :, :], op0=ALU.mult, op1=ALU.subtract)
                v.wait_ge(s_pe, 4)
                for j in range(CH):
                    v.tensor_copy(w["maskT"][:, j * S:(j + 1) * S], b4[:, 0:S // 2].bitcast(BF16))


F_X = 4


def spiking(nc, k0, c, w, io, n_seq):
    units = n_seq // PAIR
    NC = HB // 2
    STEPS, BETA = 5, 0.9
    with ExitStack() as ctx:
        k = Kit(nc, ctx, f"{k0.stage}_loop", k0.whole)
        two = lambda name, shape, dt: [k.sb(f"{name}{i}", shape, dt) for i in range(2)]
        hT = two("sp_h", [P, 2, KB, PAIR * S], F16)
        x3 = two("sp_x3", [P, PAIR, D], F32)
        out = two("sp_out", [P, PAIR, D], F32)
        y = two("sp_y", [P, PAIR, D], F32)
        mem, pot, cnt = (k.sb(f"sp_{n}", [P, PAIR, D], F32) for n in ("mem", "pot", "cnt"))
        r = [k.sb(f"sp_r{i}", [P, 2, PAIR * S], F32) for i in range(4)]
        q = [k.sb(f"sp_q{i}", [P, 2, PAIR * S], F32) for i in range(4)]
        fh = [k.sb(f"sp_fh{i}", [P, 2, PAIR * S], F16) for i in range(4)]
        fl = [k.sb(f"sp_fl{i}", [P, 2, PAIR * S], F16) for i in range(4)]
        hb_ = [k.ps(f"sp_hid{i}") for i in range(4)]
        yb = [k.ps(f"sp_yb{i}") for i in range(2)]
        d_h, d_x, d_o = k.dsig("p_h"), k.dsig("p_x"), k.dsig("p_o")
        s_m1, s_r, s_q, s_hi, s_lo, s_m2 = (k.sig(f"p_{n}", NC) for n in "m1 r q hi lo m2".split())
        s_y, s_out = k.sig("p_y"), k.sig("p_out")
        s_sp = k.sig("p_sp", 1 + 3 * (STEPS - 1))
        x3v = io["x3"].rearrange("(u a) s d -> u s a d", a=PAIR)
        outv = io["out"].rearrange("(u a) s d -> u s a d", a=PAIR)

        with nc.Block() as block:
            @block.sync
            def _(sp):
                def load(u):
                    s_m1.wait(sp, u.back(2))
                    d_h.inc(sp.dma_start(hT[u.slot][:, :, :, :], io["h3"][u.no]), u)
                    s_out.wait(sp, u.back(2))
                    d_x.inc(sp.dma_start(x3[u.slot][:, :, :], x3v[u.no]), u)

                def store(u):
                    s_out.wait(sp, u)
                    d_o.inc(sp.dma_start(outv[u.no], out[u.slot][:, :, :]), u)
                run_steps(sp, [(0, load), (3, store)], units, 3)
                for s in range(2):
                    d_o.wait(sp, Unit(0, units - 2 + s))

            @block.tensor
            def _(pe):
                def up(n):
                    def go(u):
                        if n == 0:
                            d_h.wait(pe, u)
                        s_r.wait(pe, u, n - 3)
                        hi, lo = w["wf"]
                        for j in range(2):
                            cols = slice((2 * n + j) * P, (2 * n + j + 1) * P)
                            for kb in range(KB):
                                m = three_passes(pe, hb_[n % 4][:, j * 256:(j + 1) * 256], hi[:, kb, cols], lo[:, kb, cols],
                                                 hT[u.slot][:, 0, kb, :], hT[u.slot][:, 1, kb, :], kb == 0, kb == KB - 1)
                        m.then_inc(s_m1.sem, 1)
                    return go

                def down(n):
                    def go(u):
                        s_lo.wait(pe, u, n + 1)
                        if n == 0:
                            s_y.wait(pe, u.back(2))
                        hi, lo = w["wp"]
                        for j in range(2):
                            for a in range(PAIR):
                                o = yb[u.slot][:, a * D:(a + 1) * D]
                                at = slice(a * S, (a + 1) * S)
                                hb = 2 * n + j
                                st, sto = hb == 0 and a == 0, hb == HB - 1 and a == PAIR - 1
                                for i, (l, rr) in enumerate(((fh, hi), (fh, lo), (fl, hi))):
                                    m = pe.matmul(o, l[n % 4][:, j, at], rr[:, hb, :], start=st and i == 0,
                                                  stop=sto and i == 2, skip_group_check=True)
                        m.then_inc(s_m2.sem, 1)
                    return go
                tasks = []
                for n in range(NC):
                    tasks.append((1, up(n)))
                    tasks.append((1, down(n - 2)) if n >= 2 else (2, down(n + NC - 2)))
                run_steps(pe, tasks, units, 3)

            @block.scalar
            def _(act):
                def relu(n):
                    def go(u):
                        s_m1.wait(act, u, n + 1)
                        s_q.wait(act, u.back(1), n + 1)
                        act.activation(r[n][:, :, :], v4(hb_[n][:, :]), ACT.Relu, scale=p2(-LN_X - W_X)).then_inc(s_r.sem, 1)
                    return go

                def square(n):
                    def go(u):
                        s_r.wait(act, u, n + 1)
                        s_m2.wait(act, u.back(1), n + 1)
                        act.activation(fh[n][:, :, :], r[n][:, :, :], ACT.Square, scale=p2(F_X // 2)).then_inc(s_hi.sem, 1)
                    return go

                def copy_y(u):
                    s_m2.wait(act, u)
                    s_out.wait(act, u.back(2))
                    act.activation(y[u.slot][:, :, :], yb[u.slot][:, :].rearrange("p (a n) -> p a n", a=PAIR), ACT.Copy,
                                   scale=p2(-F_X - W_X)).then_inc(s_y.sem, 1)
                tasks = []
                for n in range(NC):
                    tasks += [(1, relu(n)), (1, square(n))]
                    if n == 1:
                        tasks.append((2, copy_y))
                run_steps(act, tasks, units, 3)

            @block.gpsimd
            def _(g):
                def sq(n):
                    def go(u):
                        s_r.wait(g, u, n + 1)
                        s_lo.wait(g, u.back(1), n + 1)
                        g.tensor_tensor(q[n][:, :, :], r[n][:, :, :], r[n][:, :, :], ALU.mult).then_inc(s_q.sem, 1)
                    return go
                run_steps(g, [(1, sq(n)) for n in range(NC)], units, 3)

            @block.vector
            def _(v):
                def low(n):
                    def go(u):
                        s_hi.wait(v, u, n + 1)
                        s_q.wait(v, u, n + 1)
                        v.scalar_tensor_tensor(out=fl[n][:, :, :], in0=q[n][:, :, :], scalar=p2(F_X), in1=fh[n][:, :, :],
                                               op0=ALU.mult, op1=ALU.subtract).then_inc(s_lo.sem, 1)
                    return go

                def fire(first_step, last_step):
                    def go(u):
                        yy = y[u.slot][:, :, :]
                        if first_step == 1:
                            s_y.wait(v, u)
                            s_out.wait(v, u.back(1))
                            v.tensor_scalar(cnt[:, :, :], yy, 1.0, None, ALU.is_gt).then_inc(s_sp.sem, 1)
                        for n in range(max(first_step, 2), last_step + 1):
                            m = yy if n == 2 else mem[:, :, :]
                            at = 1 + 3 * (n - 2)
                            s_sp.wait(v, u, at)
                            v.scalar_tensor_tensor(out=pot[:, :, :], in0=m, scalar=BETA, in1=yy, op0=ALU.mult,
                                                   op1=ALU.add).then_inc(s_sp.sem, 1)
                            s_sp.wait(v, u, at + 1)
                            v.scalar_tensor_tensor(out=mem[:, :, :], in0=m, scalar=1.0, in1=pot[:, :, :], op0=ALU.is_gt,
                                                   op1=ALU.subtract, reverse1=True).then_inc(s_sp.sem, 1)
                            s_sp.wait(v, u, at + 2)
                            v.scalar_tensor_tensor(out=cnt[:, :, :], in0=mem[:, :, :], scalar=1.0, in1=cnt[:, :, :],
                                                   op0=ALU.is_gt, op1=ALU.add).then_inc(s_sp.sem, 1)
                        if last_step == STEPS:
                            d_x.wait(v, u)
                            d_o.wait(v, u.back(2))
                            s_sp.wait(v, u)
                            v.scalar_tensor_tensor(out=out[u.slot][:, :, :], in0=cnt[:, :, :], scalar=1.0 / STEPS,
                                                   in1=x3[u.slot][:, :, :], op0=ALU.mult, op1=ALU.add).then_inc(s_out.sem, 1)
                    return go
                run_steps(v, [(1, low(0)), (2, fire(1, 2)), (1, low(1)), (2, fire(3, 3)), (1, low(2)), (2, fire(4, 4)),
                              (1, low(3)), (2, fire(5, 5))], units, 3)


def build(nc, io, n_seq=128):
    with ExitStack() as ctx:
        k = Kit(nc, ctx, "all")
        c = constants(nc, k, io)
        for name in ("x1", "x2", "x3"):
            io[name] = nc.dram_tensor(f"{name}_scratch", (n_seq, S, D), F32, kind="Internal").ap()
        for name in ("h", "h3"):
            io[name] = nc.dram_tensor(f"{name}_scratch", (n_seq // PAIR, P, 2, KB, PAIR * S), F16, kind="Internal").ap()
        io["ct"] = nc.dram_tensor("ct_scratch", (n_seq // PAIR, 2, D, PAIR * S), F16, kind="Internal").ap()
        idx_d = nc.dram_tensor("idx_scratch", (n_seq, 2), U32, kind="Internal").ap()
        top = k.sb("top", [P, n_seq, 2], F32)
        gate = k.sb("gate", [P, n_seq, 2], F32)
        with ExitStack() as c1:
            k1 = Kit(nc, c1, "phase1")
            w = prepare_weights(nc, k1, c, [("wq", io["L0_xattn_w_q"], True), ("wk", io["L0_xattn_w_k"], True),
                                            ("wv", io["L0_xattn_w_v"], True), ("wo", io["L0_xattn_w_o"], True),
                                            ("wg", io["L0_ffn_Wg"], False)],
                                [("bq", io["L0_xattn_b_q"]), ("bk", io["L0_xattn_b_k"]), ("bv", io["L0_xattn_b_v"]),
                                 ("bo", io["L0_xattn_b_o"]), ("bg", io["L0_ffn_bg"])])
            attention(nc, k1, c, w, io, n_seq, True, top, idx_d)
            k1.end_phase()
        gates(nc, k, top, gate, n_seq)
        with ExitStack() as c2:
            k2 = Kit(nc, c2, "phase2")
            w = prepare_weights(nc, k2, c, [], [("b2", io["L0_ffn_b2"])])
            w.update(prepare_experts(nc, k2, c, io, idx_d, n_seq))
            experts(nc, k2, c, w, io, n_seq, gate)
            k2.end_phase()
        with ExitStack() as c3:
            k3 = Kit(nc, c3, "phase3")
            w = prepare_weights(nc, k3, c, [], [("bo", io["L1_xattn_bo"])])
            prepare_shared_heads(nc, k3, c, io, w)
            attention(nc, k3, c, w, io, n_seq, False)
            k3.end_phase()
        with ExitStack() as c4:
            k4 = Kit(nc, c4, "phase4")
            w = prepare_weights(nc, k4, c, [("wf", io["L1_ffn_W_fc"], True), ("wp", io["L1_ffn_W_proj"], True)], [])
            spiking(nc, k4, c, w, io, n_seq)


_ROWS = ("L0_xattn_b_q", "L0_xattn_b_k", "L0_xattn_b_v", "L0_xattn_b_o", "L0_ffn_bg", "L1_xattn_bo", "L0_ffn_b2")


def kernel(**inputs):
    import numpy as _np
    import concourse.bacc as _bacc
    from concourse.bass_utils import run_bass_kernel_spmd as _run

    nc = _bacc.Bacc("TRN2", target_bir_lowering=False, num_devices=1)
    arrays, io = {}, {}
    short = {"ctx_1024": "ctx", "mask_1x1xSxS2_ik1": "mask"}
    for name, value in inputs.items():
        a = _np.ascontiguousarray(value)
        if name in _ROWS:
            a = a.reshape(1, -1)
        key = short.get(name, name)
        arrays[f"in_{key}"] = a
        io[key] = nc.dram_tensor(f"in_{key}", a.shape, mybir.dt.from_np(a.dtype), kind="ExternalInput").ap()
    n_seq = io["x"].shape[0]
    io["out"] = nc.dram_tensor("out_x", tuple(io["x"].shape), F32, kind="ExternalOutput").ap()
    build(nc, io, n_seq)
    r = _run(nc, [arrays], core_ids=[0])
    return r.results[0]["out_x"]
```

```python
from contextlib import ExitStack

import concourse.bass as bass
from concourse import mybir

F32 = mybir.dt.float32
F16 = mybir.dt.float16
BF16 = mybir.dt.bfloat16
I32 = mybir.dt.int32
U32 = mybir.dt.uint32
ALU = mybir.AluOpType
ACT = mybir.ActivationFunctionType
AX = mybir.AxisListType

P = 128
S = 128
D = 256
KB = D // P
HEADS = 16
DK = D // HEADS
PAIR = 2
QB = HEADS // 2
EXP = 8
HID = 1024
HB = HID // P
EPS = 1e-5

LN_X, CTX_X, W_X, QK_X, Y_X, H_X = 10, 6, 8, 6, 6, 6
PARTS = 3
CHUNKS = 4
CH = 4
LOOP = 4


def p2(e):
    return float(2.0 ** e)


class Unit:

    def __init__(self, base, off):
        self.base, self.off = base, off
        self.slot, self.slot4 = off % 2, off % 4
        self.static = isinstance(base, int)
        self.no = base * LOOP + off
        self.turn = base * (LOOP // 2) + off // 2

    def back(self, lag):
        return Unit(self.base, self.off - lag)


class Sig:

    def __init__(self, sem, per=1, count=None):
        self.sem, self.per, self.count = sem, per, count

    def wait(self, eng, unit, k=None):
        k = self.per if k is None else k
        v = unit.no * self.per + k
        if unit.static:
            if self.count is not None:
                v = min(v, self.count * self.per)
            if v <= 0:
                return
        eng.wait_ge(self.sem, v)


class DmaSig:

    def __init__(self, sems, n=1):
        self.sems, self.n = sems, n

    def inc(self, dma, unit):
        dma.then_inc(self.sems[unit.slot], 16)

    def wait(self, eng, unit):
        if unit.static and unit.no < 0:
            return
        eng.wait_ge(self.sems[unit.slot], (unit.turn + 1) * (16 * self.n))


def settle(eng, ticks):
    eng.sem_inc(ticks, 1)


def run_steps(eng, tasks, count, depth):
    peel = -(-(depth + 2) // LOOP) * LOOP
    if count <= peel:
        for s in range(count + depth):
            for lag, task in tasks:
                if 0 <= s - lag < count:
                    task(Unit(0, s - lag))
        return
    assert count % LOOP == 0
    for s in range(peel):
        for lag, task in tasks:
            if s - lag >= 0:
                task(Unit(0, s - lag))
    with eng.Fori(peel // LOOP, count // LOOP) as i:
        for k in range(LOOP):
            for lag, task in tasks:
                task(Unit(i, k - lag))
    for s in range(count, count + depth):
        for lag, task in tasks:
            if s - lag < count:
                task(Unit(0, s - lag))


class Bank:

    def __init__(self, users, count):
        self.users, self.count = users, count
        self.at = {u[0]: i for i, u in enumerate(users)}

    def wait(self, eng, name, unit):
        n = self.at[name]
        step = unit.off + self.users[n][1]
        for m in range(n - 1, n - 1 - 8 * len(self.users), -1):
            _, lag, freed, k = self.users[m % len(self.users)]
            before = Unit(unit.base, step + m // len(self.users) - lag)
            if unit.static and not 0 <= before.off < self.count:
                continue
            freed.wait(eng, before, k)
            return


class Kit:

    def __init__(self, nc, ctx, stage, whole=None):
        self.nc, self.ctx, self.stage, self.whole, self.sems = nc, ctx, stage, whole or self, []

    def sb(self, name, shape, dt):
        return self.ctx.enter_context(self.nc.sbuf_tensor(f"{self.stage}_{name}", shape, dt))

    def ps(self, name):
        return self.ctx.enter_context(self.nc.psum_tensor(f"{self.stage}_{name}", [P, 512], F32))

    def sem(self, name):
        self.whole.sems.append(self.nc.alloc_semaphore(name=f"{self.stage}_{name}"))
        return self.whole.sems[-1]

    def end_phase(self):
        self.nc.clear_and_free_semaphores(self.sems)
        self.nc.all_engine_barrier()

    def sig(self, name, per=1, count=None):
        return Sig(self.sem(name), per, count)

    def dsig(self, name, n=1):
        return DmaSig([self.sem(f"{name}_a"), self.sem(f"{name}_b")], n)


def three_passes(eng, out, l_hi, l_lo, r_hi, r_lo, start, stop):
    eng.matmul(out, l_hi, r_hi, start=start, stop=False)
    eng.matmul(out, l_hi, r_lo, start=False, stop=False)
    return eng.matmul(out, l_lo, r_hi, start=False, stop=stop)


def constants(nc, k, io):
    c = {}
    c["ident"] = k.sb("ident", [P, P], F32)
    c["identb"] = k.sb("identb", [P, P], BF16)
    c["sel"] = k.sb("sel", [P, HEADS, P], BF16)
    c["ones10"] = k.sb("ones10", [2, D], F16)
    c["ones6"] = k.sb("ones6", [2, D], F16)
    c["minus_half"] = k.sb("minus_half", [P, PAIR], F32)
    s = k.sem("s_const")
    with nc.Block() as block:
        @block.gpsimd
        def _(g):
            g.memset(c["ident"][:, :], 0.0).then_inc(s, 1)
            g.memset(c["identb"][:, :], 0.0).then_inc(s, 1)
            g.memset(c["sel"][:, :, :], 0.0).then_inc(s, 1)
            g.memset(c["ones10"][:, :], p2(LN_X)).then_inc(s, 1)
            g.memset(c["ones6"][:, :], p2(CTX_X)).then_inc(s, 1)
            g.memset(c["minus_half"][:, :], -0.5).then_inc(s, 1)
            g.wait_ge(s, 6)
            n = 6
            for m in ("ident", "identb"):
                g.affine_select(out=c[m][:, :], in_=c[m][:, :], compare_op=ALU.not_equal, fill=1.0,
                                base=0, pattern=[[-1, P]], channel_multiplier=1).then_inc(s, 1)
                n += 1
            for g0 in (0, 64):
                for part in range(PARTS):
                    g.affine_select(out=c["sel"][:, :, :], in_=c["sel"][:, :, :],
                                    compare_op=ALU.not_equal, fill=1.0, base=-(g0 + 16 * part),
                                    pattern=[[-1, HEADS], [0, P]], channel_multiplier=1).then_inc(s, 1)
                    n += 1
                    g.wait_ge(s, n)
    return c


def prepare_weights(nc, k, c, mats, rows):
    out = {}
    jobs = []
    for name, w, tr in mats:
        n_out, n_in = (w.shape[0], w.shape[1]) if tr else (w.shape[1], w.shape[0])
        hi = k.sb(f"{name}_hi", [P, n_in // P, n_out], F16)
        lo = k.sb(f"{name}_lo", [P, n_in // P, n_out], F16)
        out[name] = (hi, lo)
    for name, b in rows:
        out[name] = k.sb(f"{name}_rows", [2, b.shape[-1]], F16)
    with ExitStack() as tmp:
        kk = Kit(nc, tmp, f"{k.stage}_tmp", k.whole)
        bank = [kk.ps(f"prep_ps{i}") for i in range(2)]
        work = []
        loads = []
        for name, w, tr in mats:
            hi, lo = out[name]
            r, cc = w.shape
            raw = kk.sb(f"{name}_raw", [P, r // P, cc], F32) if r >= P else None
            loads.append((raw, w))
            if tr:
                for ib in range(cc // P):
                    for ob in range(0, r // P, 4):
                        nb = min(4, r // P - ob)
                        work.append(("t", raw, ib, ob, nb, hi[:, ib, ob * P:(ob + nb) * P],
                                     lo[:, ib, ob * P:(ob + nb) * P], len(loads)))
            else:
                for ib in range(r // P):
                    work.append(("c", raw, ib, 0, 0, hi[:, ib, :], lo[:, ib, :], len(loads)))
        rrow = {}
        for name, b in rows:
            n = b.shape[-1]
            raw = kk.sb(f"{name}_rawrow", [1, n], F32)
            parts = kk.sb(f"{name}_parts", [1, 2, n], F16)
            rrow[name] = (raw, parts, out[name])
            loads.append((raw, b))
        s_ld, s_t, s_hi, s_lo, s_row = (kk.sem(f"prep_{x}") for x in ("ld", "t", "hi", "lo", "row"))
        tw = [w for w in work if w[0] == "t"]
        with nc.Block() as block:
            @block.sync
            def _(sp):
                for raw, w in loads:
                    if raw.shape[0] == 1:
                        sp.dma_start(raw[:, :], w).then_inc(s_ld, 16)
                    else:
                        sp.dma_start(raw[:, :, :], w.rearrange("(b p) n -> p b n", p=P)).then_inc(s_ld, 16)
                sp.wait_ge(s_lo, len(work) + len(rows))
                for name, b in rows:
                    raw, parts, dst = rrow[name]
                    for i in range(2):
                        sp.dma_start(dst[i:i + 1, :], parts[:, i, :]).then_inc(s_row, 16)
                sp.wait_ge(s_row, 32 * len(rows))

            @block.tensor
            def _(pe):
                pe.wait_ge(s_ld, 16 * len(loads))
                for n, (_, raw, ib, ob, nb, hi, lo, _l) in enumerate(tw):
                    if n >= 2:
                        pe.wait_ge(s_lo, n - 1)
                    for j in range(nb):
                        m = pe.transpose(bank[n % 2][:, j * P:(j + 1) * P],
                                         raw[:, ob + j, ib * P:(ib + 1) * P], c["ident"][:, :])
                    m.then_inc(s_t, 1)

            ordered = tw + [w for w in work if w[0] == "c"]

            @block.scalar
            def _(act):
                act.wait_ge(s_ld, 16 * len(loads))
                for n, (kind, raw, ib, ob, nb, hi, lo, _l) in enumerate(ordered):
                    if kind == "t":
                        act.wait_ge(s_t, n + 1)
                        src = bank[n % 2][:, 0:nb * P]
                    else:
                        src = raw[:, ib, :]
                    act.activation(hi, src, ACT.Copy, scale=p2(W_X)).then_inc(s_hi, 1)
                for name, b in rows:
                    raw, parts, dst = rrow[name]
                    act.activation(parts[:, 0, :], raw[:, :], ACT.Copy, scale=p2(W_X)).then_inc(s_hi, 1)

            @block.vector
            def _(v):
                v.wait_ge(s_ld, 16 * len(loads))
                for n, (kind, raw, ib, ob, nb, hi, lo, _l) in enumerate(ordered):
                    v.wait_ge(s_hi, n + 1)
                    src = bank[n % 2][:, 0:nb * P] if kind == "t" else raw[:, ib, :]
                    v.scalar_tensor_tensor(out=lo, in0=src, scalar=p2(W_X), in1=hi, op0=ALU.mult,
                                           op1=ALU.subtract).then_inc(s_lo, 1)
                for n, (name, b) in enumerate(rows):
                    raw, parts, dst = rrow[name]
                    v.wait_ge(s_hi, len(ordered) + n + 1)
                    v.scalar_tensor_tensor(out=parts[:, 1, :], in0=raw[:, :], scalar=p2(W_X),
                                           in1=parts[:, 0, :], op0=ALU.mult,
                                           op1=ALU.subtract).then_inc(s_lo, 1)
    return out


class Norm:

    def __init__(self, k, name, c, ticks_v, ticks_g):
        self.c, self.ticks_v, self.ticks_g = c, ticks_v, ticks_g
        self.st = [k.sb(f"{name}_st{i}", [P, PAIR, 6], F32) for i in range(2)]
        self.mv = [k.sb(f"{name}_mv{i}", [P, PAIR, 2], F32) for i in range(2)]
        self.ve = [k.sb(f"{name}_ve{i}", [P, PAIR], F32) for i in range(2)]
        self.rs = [k.sb(f"{name}_rs{i}", [P, PAIR], F32) for i in range(2)]
        self.xn = [k.sb(f"{name}_xn{i}", [P, PAIR, D], F32) for i in range(2)]
        self.s_st = k.sig(f"{name}_s_st", PAIR)
        self.s_mv = k.sig(f"{name}_s_mv", PAIR)
        self.s_ve = k.sig(f"{name}_s_ve")
        self.s_rs = k.sig(f"{name}_s_rs")
        self.s_xn = k.sig(f"{name}_s_xn", PAIR)

    def stats(self, v, u, x):
        s = u.slot
        self.s_rs.wait(v, u.back(2))
        for a in range(PAIR):
            v.bn_stats(self.st[s][:, a, :], x[:, a, :]).then_inc(self.s_st.sem, 1)
        for a in range(PAIR):
            self.s_st.wait(v, u, a + 1)
            settle(v, self.ticks_v)
            v.bn_aggr(self.mv[s][:, a, :], self.st[s][:, a, :]).then_inc(self.s_mv.sem, 1)

    def rstd(self, g, u):
        s = u.slot
        self.s_mv.wait(g, u)
        self.s_xn.wait(g, u.back(2))
        settle(g, self.ticks_g)
        g.tensor_scalar(self.ve[s][:, :], self.mv[s][:, :, 1], EPS, p2(-2 * LN_X), ALU.add,
                        ALU.mult).then_inc(self.s_ve.sem, 1)
        self.s_ve.wait(g, u)
        g.tensor_tensor(self.rs[s][:, :], self.ve[s][:, :], self.c["minus_half"][:, :],
                        ALU.pow).then_inc(self.s_rs.sem, 1)

    def apply(self, v, u, x):
        s = u.slot
        self.s_rs.wait(v, u)
        for a in range(PAIR):
            v.tensor_scalar(self.xn[s][:, a, :], x[:, a, :], self.mv[s][:, a, 0:1],
                            self.rs[s][:, a:a + 1], ALU.subtract, ALU.mult).then_inc(self.s_xn.sem, 1)


def transpose_pair(pe, bank, x, ident):
    for kb in range(KB):
        for a in range(PAIR):
            at = (kb * PAIR + a) * P
            m = pe.transpose(bank[:, at:at + P], x[:, a, kb * P:(kb + 1) * P], ident)
    return m


T_FIRST = 5




def lag_t(n):
    return 4 if n < T_FIRST else 5


def slot_of(buffers, u):
    return buffers[u.slot if len(buffers) == 2 else u.slot4]


def v4(t):
    return t.rearrange("p (b n) -> p b n", b=KB)


def attention(nc, k0, c, w, io, n_seq, first, glog_top=None, idx_d=None):
    units = n_seq // PAIR
    exp_scale = p2(-2 * QK_X) * (DK ** -0.5 if first else D ** -0.5)
    x_in, x_out, h_out = (io["x"], io["x1"], io["h"]) if first else (io["x2"], io["x3"], io["h3"])
    ctx = ExitStack()
    with ctx:
        k = Kit(nc, ctx, f"{k0.stage}_loop", k0.whole)
        two = lambda name, shape, dt: [k.sb(f"{name}{i}", shape, dt) for i in range(2)]
        four = lambda name, shape, dt: [k.sb(f"{name}{i}", shape, dt) for i in range(4)]
        xin = two("xin", [P, PAIR, D], F32)
        cin = two("cin", [P, PAIR, D], F32)
        xr = two("xr", [P, PAIR, D], F32)
        xT = two("xT", [P, 2, KB, PAIR * S], F16)
        cT = four("cT", [P, 2, KB, PAIR * S], F16)
        qk = two("qk", [P, 4, KB, PAIR * S], F16)
        qS = four("qS", [P, QB, PAIR * S], F16)
        kS = four("kS", [P, QB, PAIR * S], F16)
        vx = four("vx", [P, PAIR, HEADS, 2 * DK], F32)
        mx = two("mx", [P, PAIR, HEADS], F32)
        nm = two("nm", [P, PAIR, HEADS], F32)
        m3 = two("m3", [P, PAIR, P], BF16)
        mT = two("mT", [P, PAIR, S], BF16)
        pt = [k.sb(f"pt{i}", [P, CH, S], F32) for i in range(4)]
        yE = two("yE", [P, PAIR, 512], F32)
        rec = two("rec", [P, PAIR, HEADS], F32)
        yn = two("yn", [P, PAIR, D], F32)
        yT = two("yT", [P, 2, KB, PAIR * S], F16)
        x1 = two("x1", [P, PAIR, D], F32)
        hT = two("hT", [P, 2, KB, PAIR * S], F16)
        gl = two("gl", [P, PAIR, EXP], F32)
        g8 = two("g8", [P, PAIR, EXP], F32)
        i8 = k.sb("i8", [P, EXP], U32)
        qkd = [nc.dram_tensor(f"qk_scratch{int(first)}{i}", (4, D, PAIR * S), F16, kind="Internal").ap() for i in range(2)]
        ring = [k.ps(f"ring{i}") for i in range(3)]
        sb_ = [k.ps(f"score{i}") for i in range(2)]
        tb = [k.ps(f"scoreT{i}") for i in range(2)]
        avb = k.ps("av")

        tag = "a" if first else "b"
        s_init, N0 = k.sem("s_init"), 14
        ticks_v, ticks_g, ticks_s = (k.sem(f"ticks_{e}") for e in "vgs")
        ln0, ln1 = (Norm(k, f"{n}{tag}", c, ticks_v, ticks_g) for n in ("ln0", "ln1"))
        d_x, d_c, d_xr = k.dsig("d_x"), k.dsig("d_c"), k.dsig("d_xr")
        d_q, d_k, d_x1, d_h = k.dsig("d_q"), k.dsig("d_k"), k.dsig("d_x1"), k.dsig("d_h")
        d_stq, d_stk = k.dsig("d_stq", 6), k.dsig("d_stk", 6)
        d_ct = k.dsig("d_ct")
        g = lambda name, per=1: k.sig(name, per)
        s_tx, s_tc, s_xh, s_xl, s_ch, s_cl = g("s_tx"), g("s_tc"), g("s_xh"), g("s_xl"), g("s_ch"), g("s_cl")
        s_q, s_k, s_v, s_qh, s_ql, s_kh, s_kl, s_ve = (g(n) for n in "s_q s_k s_v s_qh s_ql s_kh s_kl s_vev".split())
        NC = PAIR * CHUNKS
        DEPTH = 7
        s_s, s_mx, s_st, s_e, s_av = (g(n, NC) for n in "s_s s_mx s_st s_e s_av".split())
        s_ye, s_yt, s_rec, s_yn = (g(n, PAIR) for n in "s_ye s_yt s_rec s_yn".split())
        s_m3, s_mt, s_mte = g("s_m3", 7), g("s_mt"), g("s_mte")
        s_y2, s_yh, s_yl, s_o, s_x1, s_t1, s_hh, s_hl = (g(n) for n in "s_y2 s_yh s_yl s_o s_x1 s_t1 s_hh s_hl".split())
        s_g, s_gl, s_g8, s_gt = g("s_g"), g("s_gl"), g("s_g8", PAIR), g("s_gt")
        s_idx, s_idxd = k.sem("s_idx"), k.sem("s_idxd")
        only_first = lambda *users: list(users) if first else []
        banks = [Bank([("y0", 5, s_yn, 1)] + only_first(("k", 2, s_kl, 1)) + [("y1", 5, s_yn, 2), ("t_y", 5, s_yl, 1)], units),
                 Bank([("o", 6, s_x1, 1), ("t_max", 4, s_mte, 1), ("t_x", 1, s_xl, 1), ("t_1", 6, s_hl, 1)]
                      + only_first(("gate", 6, s_gl, 1)), units),
                 Bank([("q", 2, s_ql, 1)] + only_first(("t_c", 1, s_cl, 1), ("v", 2, s_ve, 1)), units)]

        xv = x_in.rearrange("(u a) s d -> u s a d", a=PAIR)
        cv = io["ctx"].rearrange("(u a) s d -> u s a d", a=PAIR)
        x1v = x_out.rearrange("(u a) s d -> u s a d", a=PAIR)

        with nc.Block() as block:
            @block.sync
            def _(sp):
                def load(u):
                    s = u.slot
                    ln0.s_xn.wait(sp, u.back(2))
                    d_x.inc(sp.dma_start(xin[s][:, :, :], xv[u.no]), u)
                    (s_tc if first else s_ve).wait(sp, u.back(2))
                    d_c.inc(sp.dma_start(cin[s][:, :, :], cv[u.no]), u)

                def store_x1(u):
                    s_x1.wait(sp, u)
                    d_x1.inc(sp.dma_start(x1v[u.no], x1[u.slot][:, :, :]), u)

                def store_h(u):
                    s_hl.wait(sp, u)
                    s_hh.wait(sp, u)
                    d_h.inc(sp.dma_start(h_out[u.no], hT[u.slot][:, :, :, :]), u)

                def reload_x(u):
                    s_x1.wait(sp, u.back(2))
                    d_xr.inc(sp.dma_start(xr[u.slot][:, :, :], xv[u.no]), u)

                def store_ct(u):
                    s_cl.wait(sp, u)
                    s_ch.wait(sp, u)
                    d_ct.inc(sp.dma_start(io["ct"][u.no].rearrange("w (b p) n -> p w b n", p=P),
                                          cT[u.slot4][:, :, :, :]), u)

                def store_q(u):
                    s_ql.wait(sp, u)
                    settle(sp, ticks_s)
                    d_stq.wait(sp, u.back(2))
                    d_q.inc(sp.dma_start(scratch(u, 0), qk[u.slot][:, 0:2, :, :]), u)

                def store_k(u):
                    s_kl.wait(sp, u)
                    d_stk.wait(sp, u.back(2))
                    d_k.inc(sp.dma_start(scratch(u, 2), qk[u.slot][:, 2:4, :, :]), u)

                def scratch(u, at):
                    return qkd[u.slot][at:at + 2].rearrange("w (b p) n -> p w b n", p=P)

                def stack(u, done, dst, parts):
                    for hh in range(2):
                        for i, part in enumerate(parts):
                            src = part.rearrange("(b h d) n -> h d b n", h=2, d=DK)[hh]
                            at = 64 * hh + DK * i
                            done.inc(sp.dma_start(dst[u.slot4][at:at + DK, :, :], src), u)

                def stack_q(u):
                    d_q.wait(sp, u)
                    s_st.wait(sp, u.back(4))
                    hi, lo = qkd[u.slot][0], qkd[u.slot][1]
                    stack(u, d_stq, qS, (hi, hi, lo))

                def stack_k(u):
                    if first:
                        d_k.wait(sp, u)
                        hi, lo = qkd[u.slot][2], qkd[u.slot][3]
                    else:
                        hi, lo = io["ct"][u.no][0], io["ct"][u.no][1]
                    s_st.wait(sp, u.back(4))
                    stack(u, d_stk, kS, (hi, lo, hi))

                if first:
                    tasks = [(2, store_ct), (0, load), (6, store_x1), (2, store_q), (5, reload_x), (2, store_k),
                             (2, stack_q), (2, stack_k), (6, store_h)]
                else:
                    tasks = [(2, stack_k), (0, load), (6, store_x1), (2, store_q), (5, reload_x), (2, stack_q),
                             (6, store_h)]
                sp.wait_ge(s_init, N0)
                run_steps(sp, tasks, units, DEPTH)
                for s in range(2):
                    last = Unit(0, units - 2 + s)
                    d_x1.wait(sp, last)
                    d_h.wait(sp, last)
                    if first:
                        d_ct.wait(sp, last)
                if first:
                    sp.wait_ge(s_idx, 1)
                    sp.dma_start(idx_d, i8[0:n_seq, 0:2]).then_inc(s_idxd, 16)
                    sp.wait_ge(s_idxd, 16)

            @block.gpsimd
            def _(p):
                for t in m3:
                    p.memset(t[:, :, :], 0.0).then_inc(s_init, 1)
                for t in vx:
                    p.memset(t[:, :, :, :], 1.0).then_inc(s_init, 1)
                for t in qS + kS:
                    p.memset(t[:, :, :], 0.0).then_inc(s_init, 1)
                p.wait_ge(s_init, N0)

                def maxima(u):
                    s = u.slot
                    s_mx.wait(p, u)
                    s_mt.wait(p, u.back(2))
                    settle(p, ticks_g)
                    part = [m3[s][:, :, 16 * i:16 * i + 16] for i in range(PARTS)]
                    n = [0]

                    def then(ins):
                        n[0] += 1
                        ins.then_inc(s_m3.sem, 1)
                        s_m3.wait(p, u, n[0])
                        settle(p, ticks_g)
                    then(p.tensor_scalar(nm[s][:, :, :], mx[s][:, :, :], -1.0, None, ALU.mult))
                    then(p.tensor_copy(part[0], nm[s][:, :, :]))
                    then(p.tensor_tensor(nm[s][:, :, :], nm[s][:, :, :], part[0], ALU.subtract))
                    then(p.tensor_copy(part[1], nm[s][:, :, :]))
                    then(p.tensor_tensor(nm[s][:, :, :], nm[s][:, :, :], part[1], ALU.subtract))
                    then(p.tensor_copy(part[2], nm[s][:, :, :]))
                    p.tensor_copy(m3[s][:, :, 64:112], m3[s][:, :, 0:48]).then_inc(s_m3.sem, 1)

                def ctx_as_v(u):
                    d_c.wait(p, u)
                    s_av.wait(p, u.back(4))
                    settle(p, ticks_g)
                    p.tensor_copy(vx[u.slot4][:, :, :, 0:DK],
                                  cin[u.slot][:, :, :].rearrange("p a (h d) -> p a h d", d=DK)).then_inc(s_ve.sem, 1)

                def rstd0(u):
                    ln0.rstd(p, u)

                def rstd1(u):
                    ln1.rstd(p, u)

                run_steps(p, [(4, maxima), (6, rstd1)] + ([] if first else [(2, ctx_as_v)]) + [(0, rstd0)], units, DEPTH)

            @block.tensor
            def _(pe):
                pe.wait_ge(s_init, N0)
                ident = c["ident"][:, :]

                def t_x(u):
                    ln0.s_xn.wait(pe, u)
                    banks[1].wait(pe, "t_x", u)
                    transpose_pair(pe, ring[1], ln0.xn[u.slot], ident).then_inc(s_tx.sem, 1)

                def t_c(u):
                    d_c.wait(pe, u)
                    banks[2].wait(pe, "t_c", u)
                    transpose_pair(pe, ring[2], cin[u.slot], ident).then_inc(s_tc.sem, 1)

                def project(u, bank, src, name, bias, ones):
                    hi, lo = w[name]
                    x = src(u)
                    for mb in range(KB):
                        o = bank[:, mb * 256:(mb + 1) * 256]
                        for kb in range(KB):
                            three_passes(pe, o, hi[:, kb, mb * P:(mb + 1) * P], lo[:, kb, mb * P:(mb + 1) * P],
                                         x[:, 0, kb, :], x[:, 1, kb, :], kb == 0, False)
                        m = pe.matmul(o, w[bias][:, mb * P:(mb + 1) * P], ones[:, :], start=False, stop=True)
                    return m

                def fold_q(u):
                    s_xl.wait(pe, u)
                    banks[2].wait(pe, "q", u)
                    hi, lo = w["wa"]
                    x = xT[u.slot]
                    for kb in range(KB):
                        m = three_passes(pe, ring[2][:, kb * 256:(kb + 1) * 256], hi[:, 0, :], lo[:, 0, :],
                                         x[:, 0, kb, :], x[:, 1, kb, :], True, True)
                    m.then_inc(s_q.sem, 1)

                def project_rows(u, bank, src, name, bias, ones):
                    hi, lo = w[name]
                    x = src(u)
                    for a in range(PAIR):
                        o = bank[:, a * D:(a + 1) * D]
                        at = slice(a * S, (a + 1) * S)
                        for kb in range(KB):
                            three_passes(pe, o, x[:, 0, kb, at], x[:, 1, kb, at], hi[:, kb, :], lo[:, kb, :],
                                         kb == 0, False)
                        m = pe.matmul(o, ones[:, 0:S], w[bias][:, :], start=False, stop=True)
                    return m

                def q(u):
                    s_xl.wait(pe, u)
                    banks[2].wait(pe, "q", u)
                    project(u, ring[2], lambda u: xT[u.slot], "wq", "bq", c["ones10"]).then_inc(s_q.sem, 1)

                def kk(u):
                    s_cl.wait(pe, u)
                    banks[0].wait(pe, "k", u)
                    project(u, ring[0], lambda u: cT[u.slot4], "wk", "bk", c["ones6"]).then_inc(s_k.sem, 1)

                def vv(u):
                    s_cl.wait(pe, u)
                    banks[2].wait(pe, "v", u)
                    project_rows(u, ring[2], lambda u: cT[u.slot4], "wv", "bv", c["ones6"]).then_inc(s_v.sem, 1)

                def score(n):
                    a, ch = n // CHUNKS, n % CHUNKS
                    hh, g4 = ch // 2, ch % 2
                    rows = slice(64 * hh, 64 * hh + 3 * DK)
                    at = slice(a * S, (a + 1) * S)

                    def go(u):
                        if n == 0:
                            d_stq.wait(pe, u)
                            d_stk.wait(pe, u)
                        s_mx.wait(pe, u, n - 1)
                        for j in range(CH):
                            b = 4 * g4 + j
                            m = pe.matmul(sb_[n % 2][:, j * S:(j + 1) * S], qS[u.slot4][rows, b, at],
                                          kS[u.slot4][rows, b, at], start=first or j == 0, stop=first,
                                          skip_group_check=not first)
                        if not first:
                            m = pe.matmul(sb_[n % 2][:, :], c["identb"][:, :], w["mask"][:, :], start=False, stop=True,
                                          skip_group_check=True)
                        m.then_inc(s_s.sem, 1)
                    return go

                def t_max(u):
                    s_m3.wait(pe, u)
                    banks[1].wait(pe, "t_max", u)
                    o = ring[1][:, 0:S].bitcast(BF16)
                    for a in range(PAIR):
                        m = pe.transpose(o[:, a * S:(a + 1) * S], m3[u.slot][:, a, :], c["identb"][:, :])
                    m.then_inc(s_mt.sem, 1)

                def score_t(n):
                    a, ch = n // CHUNKS, n % CHUNKS
                    hh, g4 = ch // 2, ch % 2
                    rows = slice(64 * hh, 64 * hh + 3 * DK)
                    at = slice(a * S, (a + 1) * S)

                    def go(u):
                        s_e.wait(pe, u, n - 1)
                        s_mte.wait(pe, u)
                        o = tb[n % 2][:, :].rearrange("p (j n) -> p j n", j=CH)
                        for j in range(CH):
                            b = 4 * g4 + j
                            pe.matmul(o[:, j, :], kS[u.slot4][rows, b, at], qS[u.slot4][rows, b, at], start=j == 0,
                                      stop=False, skip_group_check=True)
                        if not first:
                            pe.matmul(tb[n % 2][:, :], c["identb"][:, :], w["maskT"][:, :], start=False, stop=False,
                                      skip_group_check=True)
                        for j in range(CH):
                            m = pe.matmul(o[:, j, :], c["sel"][rows, 8 * hh + 4 * g4 + j, :], mT[u.slot][rows, a, :],
                                          start=False, stop=j == CH - 1, skip_group_check=True)
                        m.then_inc(s_st.sem, 1)
                    return go

                def av(n):
                    a, ch = n // CHUNKS, n % CHUNKS
                    hh, g4 = ch // 2, ch % 2

                    def go(u):
                        s_e.wait(pe, u, n + 1)
                        if n == 0:
                            s_ve.wait(pe, u)
                        if ch == 0:
                            s_ye.wait(pe, u, a)
                        for j in range(CH):
                            head = 2 * (4 * g4 + j) + hh
                            m = pe.matmul(avb[32 * j:32 * j + 32, ch * S:(ch + 1) * S], vx[u.slot4][:, a, head, :],
                                          pt[n % 4][:, j, :], start=True, stop=True)
                        m.then_inc(s_av.sem, 1)
                    return go

                def y_rows(a):
                    def go(u):
                        s_ye.wait(pe, u, a + 1)
                        banks[0].wait(pe, f"y{a}", u)
                        for ch in range(CHUNKS):
                            at = slice(ch * P, (ch + 1) * P)
                            m = pe.transpose(ring[0][:, at], yE[u.slot][:, a, at], ident)
                        m.then_inc(s_yt.sem, 1)
                    return go

                def t_y(u):
                    s_yn.wait(pe, u)
                    banks[0].wait(pe, "t_y", u)
                    transpose_pair(pe, ring[0], yn[u.slot], ident).then_inc(s_y2.sem, 1)

                def o(u):
                    s_yl.wait(pe, u)
                    banks[1].wait(pe, "o", u)
                    project_rows(u, ring[1], lambda u: yT[u.slot], "wo", "bo", c["ones6"]).then_inc(s_o.sem, 1)

                def t_1(u):
                    ln1.s_xn.wait(pe, u)
                    banks[1].wait(pe, "t_1", u)
                    transpose_pair(pe, ring[1], ln1.xn[u.slot], ident).then_inc(s_t1.sem, 1)

                def gate(u):
                    s_hl.wait(pe, u)
                    banks[1].wait(pe, "gate", u)
                    hi, lo = w["wg"]
                    for a in range(PAIR):
                        out = ring[1][:, a * EXP:(a + 1) * EXP]
                        at = slice(a * S, (a + 1) * S)
                        for kb in range(KB):
                            three_passes(pe, out, hT[u.slot][:, 0, kb, at], hT[u.slot][:, 1, kb, at], hi[:, kb, :],
                                         lo[:, kb, :], kb == 0, False)
                        m = pe.matmul(out, c["ones10"][:, 0:S], w["bg"][:, :], start=False, stop=True)
                    m.then_inc(s_g.sem, 1)

                items = [[(6, o)], [(5, y_rows(0)), (2, q if first else fold_q)], [(4, t_max)] + [(2, kk)] * first,
                         [(1, t_x)] + [(1, t_c)] * first, [(5, y_rows(1)), (6, t_1)], [(2, vv)] * first,
                         [(5, t_y)], [(6, gate)] * first]
                tasks = []
                for part in range(NC):
                    n = (part + T_FIRST) % NC
                    before = (n - 1) % NC
                    tasks += [(lag_t(n), score_t(n)), (4 if before < T_FIRST - 1 else 5, av(before))]
                    tasks += items[part] + [(3, score(part))]
                run_steps(pe, tasks, units, DEPTH)

            @block.scalar
            def _(act):
                act.wait_ge(s_init, N0)

                def hi_part(done, src, dst, after, freed, scale):
                    def go(u):
                        after.wait(act, u)
                        for f, ago in freed:
                            f.wait(act, u.back(ago))
                        act.activation(slot_of(dst, u)[:, 0, :, :], v4(src), ACT.Copy, scale=scale).then_inc(done.sem, 1)
                    return go

                hi_x = hi_part(s_xh, ring[1][:, :], xT, s_tx, [(s_q, 2)], 1.0)
                hi_c = hi_part(s_ch, ring[2][:, :], cT, s_tc, [(s_v, 4), (d_ct, 4)], p2(CTX_X))
                hi_y = hi_part(s_yh, ring[0][:, :], yT, s_y2, [(s_o, 2)], p2(Y_X))
                hi_h = hi_part(s_hh, ring[1][:, :], hT, s_t1, [(s_g, 2)] * first + [(d_h, 2)], 1.0)

                def hi_q(u):
                    s_q.wait(act, u)
                    d_q.wait(act, u.back(2))
                    act.activation(qk[u.slot][:, 0, :, :], v4(ring[2][:, :]), ACT.Copy,
                                   scale=p2(QK_X - LN_X - W_X)).then_inc(s_qh.sem, 1)

                def hi_k(u):
                    s_k.wait(act, u)
                    d_k.wait(act, u.back(2))
                    act.activation(qk[u.slot][:, 2, :, :], v4(ring[0][:, :]), ACT.Copy,
                                   scale=p2(QK_X - CTX_X - W_X)).then_inc(s_kh.sem, 1)

                def copy_v(u):
                    s_v.wait(act, u)
                    s_av.wait(act, u.back(4))
                    act.activation(vx[u.slot4][:, :, :, 0:DK],
                                   ring[2][:, :].rearrange("p (a h d) -> p a h d", a=PAIR, d=DK), ACT.Copy,
                                   scale=p2(-CTX_X - W_X)).then_inc(s_ve.sem, 1)

                def copy_max(u):
                    s_mt.wait(act, u)
                    s_st.wait(act, u.back(2))
                    act.activation(mT[u.slot][:, :, :], ring[1][:, 0:S].bitcast(BF16).rearrange("p (a n) -> p a n", a=PAIR),
                                   ACT.Copy).then_inc(s_mte.sem, 1)

                def expo(n):
                    def go(u):
                        s_st.wait(act, u, n + 1)
                        s_av.wait(act, u, n - 3)
                        act.activation(pt[n % 4][:, :, :], tb[n % 2][:, :].rearrange("p (j n) -> p j n", j=CH),
                                       ACT.Exp, scale=exp_scale).then_inc(s_e.sem, 1)
                    return go

                def copy_y(a):
                    def go(u):
                        s_av.wait(act, u, CHUNKS * (a + 1))
                        s_yt.wait(act, u.back(2), a + 1)
                        act.activation(yE[u.slot][:, a, :], avb[:, :], ACT.Copy).then_inc(s_ye.sem, 1)
                    return go

                def copy_gate(u):
                    s_g.wait(act, u)
                    s_g8.wait(act, u.back(2))
                    act.activation(gl[u.slot][:, :, :], ring[1][:, 0:PAIR * EXP].rearrange("p (a n) -> p a n", a=PAIR),
                                   ACT.Copy, scale=p2(-LN_X - W_X)).then_inc(s_gl.sem, 1)

                items = [[], [(2, hi_q)], [(4, copy_max)] + [(2, hi_k)] * first,
                         [(5, copy_y(1)), (1, hi_x)] + [(1, hi_c)] * first, [(6, hi_h)], [(2, copy_v)] * first,
                         [(5, hi_y)], [(4, copy_y(0))] + [(6, copy_gate)] * first]
                tasks = []
                for part in range(NC):
                    n = (part + T_FIRST) % NC
                    tasks += [(lag_t(n), expo(n))] + items[part]
                run_steps(act, tasks, units, DEPTH)

            @block.vector
            def _(v):
                v.wait_ge(s_init, N0)

                def lo_part(done, src, dst, w0, after, freed, scale):
                    def go(u):
                        after.wait(v, u)
                        for f, ago in freed:
                            f.wait(v, u.back(ago))
                        v.scalar_tensor_tensor(out=slot_of(dst, u)[:, w0 + 1, :, :], in0=v4(src), scalar=scale,
                                               in1=slot_of(dst, u)[:, w0, :, :], op0=ALU.mult,
                                               op1=ALU.subtract).then_inc(done.sem, 1)
                    return go

                lo_x = lo_part(s_xl, ring[1][:, :], xT, 0, s_xh, [(s_q, 2)], 1.0)
                lo_c = lo_part(s_cl, ring[2][:, :], cT, 0, s_ch, [(s_v, 4), (d_ct, 4)], p2(CTX_X))
                lo_q = lo_part(s_ql, ring[2][:, :], qk, 0, s_qh, [(d_q, 2)], p2(QK_X - LN_X - W_X))
                lo_k = lo_part(s_kl, ring[0][:, :], qk, 2, s_kh, [(d_k, 2)], p2(QK_X - CTX_X - W_X))
                lo_y = lo_part(s_yl, ring[0][:, :], yT, 0, s_yh, [(s_o, 2)], p2(Y_X))
                lo_h = lo_part(s_hl, ring[1][:, :], hT, 0, s_hh, [(s_g, 2)] * first + [(d_h, 2)], 1.0)

                def norm0_stats(u):
                    d_x.wait(v, u)
                    ln0.stats(v, u, xin[u.slot])

                def norm0(u):
                    s_tx.wait(v, u.back(2))
                    ln0.apply(v, u, xin[u.slot])

                def add_x(u):
                    s_o.wait(v, u)
                    d_xr.wait(v, u)
                    d_x1.wait(v, u.back(2))
                    v.scalar_tensor_tensor(out=x1[u.slot][:, :, :],
                                           in0=ring[1][:, :].rearrange("p (a n) -> p a n", a=PAIR),
                                           scalar=p2(-Y_X - W_X), in1=xr[u.slot][:, :, :], op0=ALU.mult,
                                           op1=ALU.add).then_inc(s_x1.sem, 1)

                def norm1_stats(u):
                    s_x1.wait(v, u)
                    ln1.stats(v, u, x1[u.slot])

                def norm1(u):
                    s_t1.wait(v, u.back(2))
                    ln1.apply(v, u, x1[u.slot])

                def row_max(n):
                    a, ch = n // CHUNKS, n % CHUNKS

                    def go(u):
                        s_s.wait(v, u, n + 1)
                        if n == 0:
                            s_m3.wait(v, u.back(2))
                        v.tensor_reduce(mx[u.slot][:, a, CH * ch:CH * ch + CH],
                                        sb_[n % 2][:, :].rearrange("p (j n) -> p j n", j=CH), AX.X,
                                        ALU.max).then_inc(s_mx.sem, 1)
                    return go

                def norm_y(a):
                    def go(u):
                        s_yt.wait(v, u, a + 1)
                        s_y2.wait(v, u.back(2))
                        y = ring[0][:, :].rearrange("p (h n) -> p h n", n=2 * DK)
                        v.reciprocal(rec[u.slot][:, a, :], y[:, :, DK]).then_inc(s_rec.sem, 1)
                        s_rec.wait(v, u, a + 1)
                        r = rec[u.slot][:, a, :].rearrange("p (hh b) -> p hh b", hh=2).unsqueeze(3)
                        v.tensor_tensor(yn[u.slot][:, a, :].rearrange("p (b hh d) -> p hh b d", hh=2, d=DK),
                                        y[:, :, 0:DK].rearrange("p (hh b) d -> p hh b d", hh=2),
                                        r.to_broadcast([P, 2, QB, DK]), ALU.mult).then_inc(s_yn.sem, 1)
                    return go

                def top(u):
                    s_gl.wait(v, u)
                    s_gt.wait(v, u.back(2))
                    settle(v, ticks_v)
                    for a in range(PAIR):
                        v.max(g8[u.slot][:, a, :], gl[u.slot][:, a, :]).then_inc(s_g8.sem, 1)
                    s_g8.wait(v, u)
                    if u.static and u.no == 0:
                        v.max_index(i8[:, :], g8[0][:, 0, :], gl[0][:, 0, :]).then_inc(s_idx, 1)
                    v.tensor_copy(glog_top[:, bass.ts(u.no, PAIR), :], g8[u.slot][:, :, 0:2]).then_inc(s_gt.sem, 1)

                items = [[(6, add_x)], [(6, norm1_stats), (5, norm_y(0))], [(2, lo_q), (6, norm1)],
                         [(2, lo_k)] * first + [(1, lo_x)], [(1, lo_c)] * first + [(5, norm_y(1))],
                         [(6, lo_h), (0, norm0_stats)], [], [(5, lo_y), (0, norm0)]]
                tasks = []
                for part in range(NC):
                    tasks += items[part] + [(3, row_max(part))]
                tasks += [(6, top)] * first
                run_steps(v, tasks, units, DEPTH)


def gates(nc, k, top, gate, n_seq):
    with ExitStack() as tmp:
        kk = Kit(nc, tmp, f"{k.stage}_tmp", k.whole)
        e = kk.sb("gate_e", [P, n_seq], F32)
        d = kk.sb("gate_d", [P, n_seq], F32)
        s = kk.sem("s_gate")
        with nc.Block() as block:
            @block.vector
            def _(v):
                v.tensor_tensor(d[:, :], top[:, :, 1], top[:, :, 0], ALU.subtract).then_inc(s, 1)
                v.wait_ge(s, 2)
                v.tensor_scalar(d[:, :], e[:, :], 1.0, None, ALU.add).then_inc(s, 1)
                v.wait_ge(s, 3)
                v.reciprocal(d[:, :], d[:, :]).then_inc(s, 1)
                v.wait_ge(s, 4)
                v.tensor_scalar(gate[:, :, 0], d[:, :], p2(-H_X - W_X), None, ALU.mult).then_inc(s, 1)
                v.wait_ge(s, 5)
                v.tensor_tensor(gate[:, :, 1], gate[:, :, 0], e[:, :], ALU.mult).then_inc(s, 1)

            @block.scalar
            def _(act):
                act.wait_ge(s, 1)
                act.activation(e[:, :], d[:, :], ACT.Exp).then_inc(s, 1)


def prepare_experts(nc, k, c, io, idx_d, n_seq):
    w = {"w1_hi": k.sb("w1_hi", [P, EXP, KB, HID], F16), "w1_lo": k.sb("w1_lo", [P, EXP, KB, HID], F16),
         "w2": k.sb("w2", [P, EXP, HB, 2, D], F16),
         "b1": k.sb("b1T", [P, EXP * HB], F32), "idx": k.sb("idx", [1, 2 * n_seq], U32)}
    jobs = []
    for e in range(EXP):
        jobs.append((io["L0_ffn_W1"][e].rearrange("(b p) n -> p b n", p=P), "w1", e))
        jobs.append((io["L0_ffn_W2"][e].rearrange("(b p) n -> p b n", p=P), "w2", e))
    N = len(jobs)
    with ExitStack() as tmp:
        kk = Kit(nc, tmp, f"{k.stage}_expert", k.whole)
        raw = [kk.sb(f"expert_raw{i}", [P, KB * HID], F32) for i in range(3)]
        b1r = kk.sb("b1_raw", [EXP * HB, P], F32)
        bank = kk.ps("b1_ps")
        s_ld = [kk.sem(f"expert_ld{i}") for i in range(3)]
        s_hi, s_lo, s_b, s_t, s_i = (kk.sem(f"expert_{x}") for x in ("hi", "lo", "b", "t", "i"))

        def part(name, e, i):
            return w["w2"][:, e, :, i, :] if name == "w2" else w["w1_lo" if i else "w1_hi"][:, e, :, :]

        def view(i, name):
            return raw[i % 3][:, :].rearrange("p (b n) -> p b n", b=KB if name == "w1" else HB)
        with nc.Block() as block:
            @block.sync
            def _(sp):
                sp.dma_start(b1r[:, :], io["L0_ffn_b1"].rearrange("e (b p) -> (e b) p", p=P)).then_inc(s_b, 16)
                sp.dma_start(w["idx"][:, :], idx_d.rearrange("(o t) n -> o (t n)", o=1)).then_inc(s_i, 16)
                for i, (src, name, e) in enumerate(jobs):
                    if i >= 3:
                        sp.wait_ge(s_lo, i - 2)
                    sp.dma_start(view(i, name), src).then_inc(s_ld[i % 3], 16)

            @block.tensor
            def _(pe):
                pe.wait_ge(s_b, 16)
                pe.transpose(bank[:, 0:EXP * HB], b1r[:, :], c["ident"][0:EXP * HB, 0:EXP * HB]).then_inc(s_t, 1)

            @block.scalar
            def _(act):
                for i, (src, name, e) in enumerate(jobs):
                    act.wait_ge(s_ld[i % 3], 16 * (i // 3 + 1))
                    act.activation(part(name, e, 0), view(i, name), ACT.Copy, scale=p2(W_X)).then_inc(s_hi, 1)

            @block.vector
            def _(v):
                v.wait_ge(s_t, 1)
                v.tensor_copy(w["b1"][:, :], bank[:, 0:EXP * HB])
                v.wait_ge(s_i, 16)
                v.tensor_scalar(w["idx"][:, :], w["idx"][:, :], EXP - 1, None, ALU.min)
                for i, (src, name, e) in enumerate(jobs):
                    v.wait_ge(s_hi, i + 1)
                    v.scalar_tensor_tensor(out=part(name, e, 1), in0=view(i, name), scalar=p2(W_X),
                                           in1=part(name, e, 0), op0=ALU.mult, op1=ALU.subtract).then_inc(s_lo, 1)
    return w


def read_experts(nc, eng, idx, u, first):
    at = idx[0:1, bass.ds(u.no * (2 * PAIR) + first, 2 * PAIR - first)]
    _, values = nc.values_load_multi_w_load_instructions(at, engines=[eng.engine], min_val=0, max_val=EXP - 1,
                                                           skip_runtime_bounds_check_because="VectorE has clamped them")
    return dict(enumerate(values, first))


def experts(nc, k0, c, w, io, n_seq, gate):
    units = n_seq // PAIR
    NC = PAIR * 2 * 2
    with ExitStack() as ctx:
        k = Kit(nc, ctx, f"{k0.stage}_loop", k0.whole)
        two = lambda name, shape, dt: [k.sb(f"{name}{i}", shape, dt) for i in range(2)]
        hT = two("moe_h", [P, 2, KB, PAIR * S], F16)
        x1 = two("moe_x1", [P, PAIR, D], F32)
        x2 = two("moe_x2", [P, PAIR, D], F32)
        sums = [k.sb(f"moe_t{i}", [P, PAIR, D], F32) for i in range(3)]
        NH = 4
        hf = [k.sb(f"hf{i}", [P, 4, S], F32) for i in range(NH)]
        hh = [k.sb(f"hh{i}", [P, 4, S], F16) for i in range(NH)]
        hl = [k.sb(f"hl{i}", [P, 4, S], F16) for i in range(NH)]
        hb_ = [k.ps(f"hid{i}") for i in range(4)]
        yb = [[k.ps(f"moe_y{a}{ex}") for ex in range(2)] for a in range(PAIR)]
        d_h, d_x, d_o = k.dsig("m_h"), k.dsig("m_x"), k.dsig("m_o")
        s_m1, s_ge, s_hi, s_lo, s_m2 = (k.sig(f"m_{n}", NC) for n in "m1 ge hi lo m2".split())
        s_t, s_x2 = k.sig("m_t", 3 * PAIR), k.sig("m_x2", PAIR)
        x1v = io["x1"].rearrange("(u a) s d -> u s a d", a=PAIR)
        x2v = io["x2"].rearrange("(u a) s d -> u s a d", a=PAIR)

        with nc.Block() as block:
            @block.sync
            def _(sp):
                def load(u):
                    s_m1.wait(sp, u.back(2))
                    d_h.inc(sp.dma_start(hT[u.slot][:, :, :, :], io["h"][u.no]), u)
                    s_t.wait(sp, u.back(2))
                    d_x.inc(sp.dma_start(x1[u.slot][:, :, :], x1v[u.no]), u)

                def store(u):
                    s_x2.wait(sp, u)
                    d_o.inc(sp.dma_start(x2v[u.no], x2[u.slot][:, :, :]), u)
                run_steps(sp, [(0, load), (3, store)], units, 3)
                for s in range(2):
                    d_o.wait(sp, Unit(0, units - 2 + s))

            @block.tensor
            def _(pe):
                e_now, e_before = {}, {}

                def read(into, first):
                    def go(u):
                        into.update(read_experts(nc, pe, w["idx"], u, first))
                    return go

                def up(n):
                    a, ex, half = n // 4, n // 2 % 2, n % 2

                    def go(u):
                        if n == 0:
                            d_h.wait(pe, u)
                        s_ge.wait(pe, u, n - 3)
                        at = slice(a * S, (a + 1) * S)
                        e = e_now[2 * a + ex]
                        for j in range(4):
                            cols = slice((4 * half + j) * P, (4 * half + j + 1) * P)
                            for kb in range(KB):
                                m = three_passes(pe, hb_[n % 4][:, j * S:(j + 1) * S],
                                                 w["w1_hi"][:, bass.ds(e, 1), kb, cols].rearrange("p o n -> p (o n)"),
                                                 w["w1_lo"][:, bass.ds(e, 1), kb, cols].rearrange("p o n -> p (o n)"),
                                                 hT[u.slot][:, 0, kb, at], hT[u.slot][:, 1, kb, at], kb == 0,
                                                 kb == KB - 1)
                        m.then_inc(s_m1.sem, 1)
                    return go

                def down(n, table):
                    a, ex, half = n // 4, n // 2 % 2, n % 2

                    def go(u):
                        s_lo.wait(pe, u, n + 1)
                        if n % 4 == 0:
                            s_x2.wait(pe, u.back(1), a + 1)
                        e = table[2 * a + ex]
                        o = yb[a][ex]
                        for j in range(4):
                            row = w["w2"][:, bass.ds(e, 1), 4 * half + j, :, :].rearrange("p o t n -> p (o t n)")
                            pe.matmul(o[:, :], hh[n % NH][:, j, :], row, start=half == 0 and j == 0, stop=False,
                                      skip_group_check=True)
                            m = pe.matmul(o[:, 0:D], hl[n % NH][:, j, :], row[:, 0:D], start=False, stop=False,
                                          skip_group_check=True)
                        if half == 1:
                            m = pe.matmul(o[:, 0:D], c["ones6"][:, 0:S], w["b2"][:, bass.ds(e * D, D)], start=False,
                                          stop=True, skip_group_check=True)
                        m.then_inc(s_m2.sem, 1)
                    return go

                tasks = [(1, read(e_now, 0))]
                for n in range(NC):
                    tasks.append((1, up(n)))
                    if n == 0:
                        tasks.append((2, read(e_before, PAIR)))
                    tasks.append((1, down(n - 3, e_now)) if n >= 3 else (2, down(n + NC - 3, e_before)))
                run_steps(pe, tasks, units, 3)

            @block.scalar
            def _(act):
                e_now = {}

                def read(u):
                    e_now.update(read_experts(nc, act, w["idx"], u, 0))

                def gelu(n):
                    a, ex, half = n // 4, n // 2 % 2, n % 2

                    def go(u):
                        s_m1.wait(act, u, n + 1)
                        s_lo.wait(act, u, n + 1 - NH)
                        e = e_now[2 * a + ex]
                        for j in range(4):
                            i = act.activation(hf[n % NH][:, j, :], hb_[n % 4][:, j * S:(j + 1) * S], ACT.Gelu,
                                               bias=w["b1"][:, bass.ds(e * HB + (4 * half + j), 1)],
                                               scale=p2(-LN_X - W_X))
                        i.then_inc(s_ge.sem, 1)
                    return go
                run_steps(act, [(1, read)] + [(1, gelu(n)) for n in range(NC)], units, 3)

            @block.vector
            def _(v):
                def split(n):
                    def go(u):
                        s_ge.wait(v, u, n + 1)
                        s_m2.wait(v, u, n + 1 - NH)
                        v.tensor_scalar(hh[n % NH][:, :, :], hf[n % NH][:, :, :], p2(H_X), None, ALU.mult)\
                         .then_inc(s_hi.sem, 1)
                        s_hi.wait(v, u, n + 1)
                        v.scalar_tensor_tensor(out=hl[n % NH][:, :, :], in0=hf[n % NH][:, :, :], scalar=p2(H_X),
                                               in1=hh[n % NH][:, :, :], op0=ALU.mult, op1=ALU.subtract)\
                         .then_inc(s_lo.sem, 1)
                    return go

                def add(a):
                    def go(u):
                        s_m2.wait(v, u, 4 * (a + 1))
                        if a == 0:
                            d_x.wait(v, u)
                            d_o.wait(v, u.back(2))
                        at = x1[u.slot][:, a, :]
                        for i in range(4):
                            ex, part = i // 2, i % 2
                            to, done = (sums[i][:, a, :], s_t) if i < 3 else (x2[u.slot][:, a, :], s_x2)
                            v.scalar_tensor_tensor(out=to, in0=yb[a][ex][:, part * D:(part + 1) * D],
                                                   scalar=gate[:, bass.ds(u.no * PAIR + a, 1), ex], in1=at,
                                                   op0=ALU.mult, op1=ALU.add).then_inc(done.sem, 1)
                            if i < 3:
                                s_t.wait(v, u, 3 * a + i + 1)
                            at = to
                    return go

                tasks = []
                for n in range(NC):
                    tasks.append((1, split(n)))
                    if n == 2:
                        tasks.append((2, add(1)))
                    if n == NC - 1:
                        tasks.append((1, add(0)))
                run_steps(v, tasks, units, 3)


def prepare_shared_heads(nc, k, c, io, w):
    for name, n in (("wa", P), ("wo", D)):
        nb = 1 if name == "wa" else KB
        w[name] = (k.sb(f"{name}2_hi", [P, nb, n], F16), k.sb(f"{name}2_lo", [P, nb, n], F16))
    w["mask"] = k.sb("mask4", [P, CH * S], BF16)
    w["maskT"] = k.sb("maskT4", [P, CH * S], BF16)
    masked = -1e20 * p2(2 * QK_X)
    with ExitStack() as tmp:
        kk = Kit(nc, tmp, f"{k.stage}_shared", k.whole)
        bd = [kk.sb(f"bd{i}", [P, P], F32) for i in range(3)]
        wo = kk.sb("wo_raw2", [P, KB, D], F32)
        woT = kk.sb("woT2", [P, KB, D], F32)
        mi = kk.sb("mask_int", [P, S], I32)
        mf = kk.sb("mask_f", [P, S], F32)
        b1, b2, b3, b4 = (kk.ps(f"sh_ps{i}") for i in range(4))
        s_z, s_ld, s_mk, s_pe, s_v, s_a = (kk.sem(f"sh_{x}") for x in ("z", "ld", "mk", "pe", "v", "a"))
        with nc.Block() as block:
            @block.gpsimd
            def _(g):
                for t in bd:
                    g.memset(t[:, :], 0.0).then_inc(s_z, 1)

            @block.sync
            def _(sp):
                sp.dma_start(mi[:, :], io["mask"].rearrange("a b s n -> (a b s) n")).then_inc(s_mk, 16)
                sp.wait_ge(s_z, 3)
                for t, name in zip(bd, ("Wq", "Wk", "Wv")):
                    for h in range(P // DK):
                        at = slice(h * DK, (h + 1) * DK)
                        sp.dma_start(t[at, at], io[f"L1_xattn_{name}"]).then_inc(s_ld, 16)
                sp.dma_start(wo[:, :, :], io["L1_xattn_Wo"].rearrange("(b p) n -> p b n", p=P)).then_inc(s_ld, 16)

            @block.tensor
            def _(pe):
                pe.wait_ge(s_ld, 16 * (3 * (P // DK) + 1))
                pe.matmul(b1[:, 0:P], bd[0][:, :], bd[1][:, :], start=True, stop=True).then_inc(s_pe, 1)
                for ib in range(KB):
                    for ob in range(KB):
                        m = pe.transpose(b2[:, ib * D + ob * P:ib * D + (ob + 1) * P], wo[:, ob, ib * P:(ib + 1) * P],
                                         c["ident"][:, :])
                m.then_inc(s_pe, 1)
                pe.wait_ge(s_v, 1)
                for ib in range(KB):
                    m = pe.matmul(b3[:, ib * D:(ib + 1) * D], bd[2][:, :], woT[:, ib, :], start=True, stop=True)
                m.then_inc(s_pe, 1)
                pe.wait_ge(s_v, 6)
                pe.transpose(b4[:, 0:S // 2].bitcast(BF16), w["mask"][:, 0:S], c["identb"][:, :]).then_inc(s_pe, 1)

            @block.scalar
            def _(act):
                act.wait_ge(s_pe, 1)
                act.activation(w["wa"][0][:, 0, :], b1[:, 0:P], ACT.Copy, scale=p2(W_X)).then_inc(s_a, 1)
                act.wait_ge(s_pe, 3)
                act.activation(w["wo"][0][:, :, :], v4(b3[:, :]), ACT.Copy, scale=p2(W_X)).then_inc(s_a, 1)

            @block.vector
            def _(v):
                v.wait_ge(s_pe, 2)
                v.tensor_copy(woT[:, :, :], v4(b2[:, :])).then_inc(s_v, 1)
                v.wait_ge(s_mk, 16)
                v.tensor_scalar(mf[:, :], mi[:, :], 0.0, masked, ALU.is_equal, ALU.mult).then_inc(s_v, 1)
                v.wait_ge(s_v, 2)
                for j in range(CH):
                    v.tensor_copy(w["mask"][:, j * S:(j + 1) * S], mf[:, :]).then_inc(s_v, 1)
                v.wait_ge(s_a, 1)
                v.scalar_tensor_tensor(out=w["wa"][1][:, 0, :], in0=b1[:, 0:P], scalar=p2(W_X), in1=w["wa"][0][:, 0, :],
                                       op0=ALU.mult, op1=ALU.subtract)
                v.wait_ge(s_a, 2)
                v.scalar_tensor_tensor(out=w["wo"][1][:, :, :], in0=v4(b3[:, :]), scalar=p2(W_X),
                                       in1=w["wo"][0][:, :, :], op0=ALU.mult, op1=ALU.subtract)
                v.wait_ge(s_pe, 4)
                for j in range(CH):
                    v.tensor_copy(w["maskT"][:, j * S:(j + 1) * S], b4[:, 0:S // 2].bitcast(BF16))


F_X = 4


def spiking(nc, k0, c, w, io, n_seq):
    units = n_seq // PAIR
    NC = HB // 2
    STEPS, BETA = 5, 0.9
    with ExitStack() as ctx:
        k = Kit(nc, ctx, f"{k0.stage}_loop", k0.whole)
        two = lambda name, shape, dt: [k.sb(f"{name}{i}", shape, dt) for i in range(2)]
        hT = two("sp_h", [P, 2, KB, PAIR * S], F16)
        x3 = two("sp_x3", [P, PAIR, D], F32)
        out = two("sp_out", [P, PAIR, D], F32)
        y = two("sp_y", [P, PAIR, D], F32)
        mem, pot, cnt = (k.sb(f"sp_{n}", [P, PAIR, D], F32) for n in ("mem", "pot", "cnt"))
        r = [k.sb(f"sp_r{i}", [P, 2, PAIR * S], F32) for i in range(4)]
        q = [k.sb(f"sp_q{i}", [P, 2, PAIR * S], F32) for i in range(4)]
        fh = [k.sb(f"sp_fh{i}", [P, 2, PAIR * S], F16) for i in range(4)]
        fl = [k.sb(f"sp_fl{i}", [P, 2, PAIR * S], F16) for i in range(4)]
        hb_ = [k.ps(f"sp_hid{i}") for i in range(4)]
        yb = [k.ps(f"sp_yb{i}") for i in range(2)]
        d_h, d_x, d_o = k.dsig("p_h"), k.dsig("p_x"), k.dsig("p_o")
        s_m1, s_r, s_q, s_hi, s_lo, s_m2 = (k.sig(f"p_{n}", NC) for n in "m1 r q hi lo m2".split())
        s_y, s_out = k.sig("p_y"), k.sig("p_out")
        s_sp = k.sig("p_sp", 1 + 3 * (STEPS - 1))
        x3v = io["x3"].rearrange("(u a) s d -> u s a d", a=PAIR)
        outv = io["out"].rearrange("(u a) s d -> u s a d", a=PAIR)

        with nc.Block() as block:
            @block.sync
            def _(sp):
                def load(u):
                    s_m1.wait(sp, u.back(2))
                    d_h.inc(sp.dma_start(hT[u.slot][:, :, :, :], io["h3"][u.no]), u)
                    s_out.wait(sp, u.back(2))
                    d_x.inc(sp.dma_start(x3[u.slot][:, :, :], x3v[u.no]), u)

                def store(u):
                    s_out.wait(sp, u)
                    d_o.inc(sp.dma_start(outv[u.no], out[u.slot][:, :, :]), u)
                run_steps(sp, [(0, load), (3, store)], units, 3)
                for s in range(2):
                    d_o.wait(sp, Unit(0, units - 2 + s))

            @block.tensor
            def _(pe):
                def up(n):
                    def go(u):
                        if n == 0:
                            d_h.wait(pe, u)
                        s_r.wait(pe, u, n - 3)
                        hi, lo = w["wf"]
                        for j in range(2):
                            cols = slice((2 * n + j) * P, (2 * n + j + 1) * P)
                            for kb in range(KB):
                                m = three_passes(pe, hb_[n % 4][:, j * 256:(j + 1) * 256], hi[:, kb, cols], lo[:, kb, cols],
                                                 hT[u.slot][:, 0, kb, :], hT[u.slot][:, 1, kb, :], kb == 0, kb == KB - 1)
                        m.then_inc(s_m1.sem, 1)
                    return go

                def down(n):
                    def go(u):
                        s_lo.wait(pe, u, n + 1)
                        if n == 0:
                            s_y.wait(pe, u.back(2))
                        hi, lo = w["wp"]
                        for j in range(2):
                            for a in range(PAIR):
                                o = yb[u.slot][:, a * D:(a + 1) * D]
                                at = slice(a * S, (a + 1) * S)
                                hb = 2 * n + j
                                st, sto = hb == 0 and a == 0, hb == HB - 1 and a == PAIR - 1
                                for i, (l, rr) in enumerate(((fh, hi), (fh, lo), (fl, hi))):
                                    m = pe.matmul(o, l[n % 4][:, j, at], rr[:, hb, :], start=st and i == 0,
                                                  stop=sto and i == 2, skip_group_check=True)
                        m.then_inc(s_m2.sem, 1)
                    return go
                tasks = []
                for n in range(NC):
                    tasks.append((1, up(n)))
                    tasks.append((1, down(n - 2)) if n >= 2 else (2, down(n + NC - 2)))
                run_steps(pe, tasks, units, 3)

            @block.scalar
            def _(act):
                def relu(n):
                    def go(u):
                        s_m1.wait(act, u, n + 1)
                        s_q.wait(act, u.back(1), n + 1)
                        act.activation(r[n][:, :, :], v4(hb_[n][:, :]), ACT.Relu, scale=p2(-LN_X - W_X)).then_inc(s_r.sem, 1)
                    return go

                def square(n):
                    def go(u):
                        s_r.wait(act, u, n + 1)
                        s_m2.wait(act, u.back(1), n + 1)
                        act.activation(fh[n][:, :, :], r[n][:, :, :], ACT.Square, scale=p2(F_X // 2)).then_inc(s_hi.sem, 1)
                    return go

                def copy_y(u):
                    s_m2.wait(act, u)
                    s_out.wait(act, u.back(2))
                    act.activation(y[u.slot][:, :, :], yb[u.slot][:, :].rearrange("p (a n) -> p a n", a=PAIR), ACT.Copy,
                                   scale=p2(-F_X - W_X)).then_inc(s_y.sem, 1)
                tasks = []
                for n in range(NC):
                    tasks += [(1, relu(n)), (1, square(n))]
                    if n == 1:
                        tasks.append((2, copy_y))
                run_steps(act, tasks, units, 3)

            @block.gpsimd
            def _(g):
                def sq(n):
                    def go(u):
                        s_r.wait(g, u, n + 1)
                        s_lo.wait(g, u.back(1), n + 1)
                        g.tensor_tensor(q[n][:, :, :], r[n][:, :, :], r[n][:, :, :], ALU.mult).then_inc(s_q.sem, 1)
                    return go
                run_steps(g, [(1, sq(n)) for n in range(NC)], units, 3)

            @block.vector
            def _(v):
                def low(n):
                    def go(u):
                        s_hi.wait(v, u, n + 1)
                        s_q.wait(v, u, n + 1)
                        v.scalar_tensor_tensor(out=fl[n][:, :, :], in0=q[n][:, :, :], scalar=p2(F_X), in1=fh[n][:, :, :],
                                               op0=ALU.mult, op1=ALU.subtract).then_inc(s_lo.sem, 1)
                    return go

                def fire(first_step, last_step):
                    def go(u):
                        yy = y[u.slot][:, :, :]
                        if first_step == 1:
                            s_y.wait(v, u)
                            s_out.wait(v, u.back(1))
                            v.tensor_scalar(cnt[:, :, :], yy, 1.0, None, ALU.is_gt).then_inc(s_sp.sem, 1)
                        for n in range(max(first_step, 2), last_step + 1):
                            m = yy if n == 2 else mem[:, :, :]
                            at = 1 + 3 * (n - 2)
                            s_sp.wait(v, u, at)
                            v.scalar_tensor_tensor(out=pot[:, :, :], in0=m, scalar=BETA, in1=yy, op0=ALU.mult,
                                                   op1=ALU.add).then_inc(s_sp.sem, 1)
                            s_sp.wait(v, u, at + 1)
                            v.scalar_tensor_tensor(out=mem[:, :, :], in0=m, scalar=1.0, in1=pot[:, :, :], op0=ALU.is_gt,
                                                   op1=ALU.subtract, reverse1=True).then_inc(s_sp.sem, 1)
                            s_sp.wait(v, u, at + 2)
                            v.scalar_tensor_tensor(out=cnt[:, :, :], in0=mem[:, :, :], scalar=1.0, in1=cnt[:, :, :],
                                                   op0=ALU.is_gt, op1=ALU.add).then_inc(s_sp.sem, 1)
                        if last_step == STEPS:
                            d_x.wait(v, u)
                            d_o.wait(v, u.back(2))
                            s_sp.wait(v, u)
                            v.scalar_tensor_tensor(out=out[u.slot][:, :, :], in0=cnt[:, :, :], scalar=1.0 / STEPS,
                                                   in1=x3[u.slot][:, :, :], op0=ALU.mult, op1=ALU.add).then_inc(s_out.sem, 1)
                    return go
                run_steps(v, [(1, low(0)), (2, fire(1, 2)), (1, low(1)), (2, fire(3, 3)), (1, low(2)), (2, fire(4, 4)),
                              (1, low(3)), (2, fire(5, 5))], units, 3)


def build(nc, io, n_seq=128):
    with ExitStack() as ctx:
        k = Kit(nc, ctx, "all")
        c = constants(nc, k, io)
        for name in ("x1", "x2", "x3"):
            io[name] = nc.dram_tensor(f"{name}_scratch", (n_seq, S, D), F32, kind="Internal").ap()
        for name in ("h", "h3"):
            io[name] = nc.dram_tensor(f"{name}_scratch", (n_seq // PAIR, P, 2, KB, PAIR * S), F16, kind="Internal").ap()
        io["ct"] = nc.dram_tensor("ct_scratch", (n_seq // PAIR, 2, D, PAIR * S), F16, kind="Internal").ap()
        idx_d = nc.dram_tensor("idx_scratch", (n_seq, 2), U32, kind="Internal").ap()
        top = k.sb("top", [P, n_seq, 2], F32)
        gate = k.sb("gate", [P, n_seq, 2], F32)
        with ExitStack() as c1:
            k1 = Kit(nc, c1, "phase1")
            w = prepare_weights(nc, k1, c, [("wq", io["L0_xattn_w_q"], True), ("wk", io["L0_xattn_w_k"], True),
                                            ("wv", io["L0_xattn_w_v"], True), ("wo", io["L0_xattn_w_o"], True),
                                            ("wg", io["L0_ffn_Wg"], False)],
                                [("bq", io["L0_xattn_b_q"]), ("bk", io["L0_xattn_b_k"]), ("bv", io["L0_xattn_b_v"]),
                                 ("bo", io["L0_xattn_b_o"]), ("bg", io["L0_ffn_bg"])])
            attention(nc, k1, c, w, io, n_seq, True, top, idx_d)
            k1.end_phase()
        gates(nc, k, top, gate, n_seq)
        with ExitStack() as c2:
            k2 = Kit(nc, c2, "phase2")
            w = prepare_weights(nc, k2, c, [], [("b2", io["L0_ffn_b2"])])
            w.update(prepare_experts(nc, k2, c, io, idx_d, n_seq))
            experts(nc, k2, c, w, io, n_seq, gate)
            k2.end_phase()
        with ExitStack() as c3:
            k3 = Kit(nc, c3, "phase3")
            w = prepare_weights(nc, k3, c, [], [("bo", io["L1_xattn_bo"])])
            prepare_shared_heads(nc, k3, c, io, w)
            attention(nc, k3, c, w, io, n_seq, False)
            k3.end_phase()
        with ExitStack() as c4:
            k4 = Kit(nc, c4, "phase4")
            w = prepare_weights(nc, k4, c, [("wf", io["L1_ffn_W_fc"], True), ("wp", io["L1_ffn_W_proj"], True)], [])
            spiking(nc, k4, c, w, io, n_seq)


_ROWS = ("L0_xattn_b_q", "L0_xattn_b_k", "L0_xattn_b_v", "L0_xattn_b_o", "L0_ffn_bg", "L1_xattn_bo", "L0_ffn_b2")


def kernel(**inputs):
    import numpy as _np
    import concourse.bacc as _bacc
    from concourse.bass_utils import run_bass_kernel_spmd as _run

    nc = _bacc.Bacc("TRN2", target_bir_lowering=False, num_devices=1)
    arrays, io = {}, {}
    short = {"ctx_1024": "ctx", "mask_1x1xSxS2_ik1": "mask"}
    for name, value in inputs.items():
        a = _np.ascontiguousarray(value)
        if name in _ROWS:
            a = a.reshape(1, -1)
        key = short.get(name, name)
        arrays[f"in_{key}"] = a
        io[key] = nc.dram_tensor(f"in_{key}", a.shape, mybir.dt.from_np(a.dtype), kind="ExternalInput").ap()
    n_seq = io["x"].shape[0]
    io["out"] = nc.dram_tensor("out_x", tuple(io["x"].shape), F32, kind="ExternalOutput").ap()
    build(nc, io, n_seq)
    r = _run(nc, [arrays], core_ids=[0])
    return r.results[0]["out_x"]
```

```python
from contextlib import ExitStack

import concourse.bass as bass
from concourse import mybir

F32 = mybir.dt.float32
F16 = mybir.dt.float16
BF16 = mybir.dt.bfloat16
I32 = mybir.dt.int32
U32 = mybir.dt.uint32
ALU = mybir.AluOpType
ACT = mybir.ActivationFunctionType
AX = mybir.AxisListType

P = 128
S = 128
D = 256
KB = D // P
HEADS = 16
DK = D // HEADS
PAIR = 2
QB = HEADS // 2
EXP = 8
HID = 1024
HB = HID // P
EPS = 1e-5

LN_X, CTX_X, W_X, QK_X, Y_X, H_X = 10, 6, 8, 6, 6, 6
PARTS = 3
CHUNKS = 4
CH = 4
M_X = 15
LOOP = 4


def p2(e):
    return float(2.0 ** e)


class Unit:

    def __init__(self, base, off):
        self.base, self.off = base, off
        self.slot, self.slot4 = off % 2, off % 4
        self.static = isinstance(base, int)
        self.no = base * LOOP + off
        self.turn = base * (LOOP // 2) + off // 2

    def back(self, lag):
        return Unit(self.base, self.off - lag)


class Sig:

    def __init__(self, sem, per=1):
        self.sem, self.per = sem, per

    def wait(self, eng, unit, k=None):
        k = self.per if k is None else k
        v = unit.no * self.per + k
        if unit.static and v <= 0:
            return
        eng.wait_ge(self.sem, v)


class DmaSig:

    def __init__(self, sems, n=1):
        self.sems, self.n = sems, n

    def inc(self, dma, unit):
        dma.then_inc(self.sems[unit.slot], 16)

    def wait(self, eng, unit):
        if unit.static and unit.no < 0:
            return
        eng.wait_ge(self.sems[unit.slot], (unit.turn + 1) * (16 * self.n))


def settle(eng, ticks):
    eng.sem_inc(ticks, 1)


def run_steps(eng, tasks, count, depth):
    peel = -(-(depth + 2) // LOOP) * LOOP
    if count <= peel:
        for s in range(count + depth):
            for lag, task in tasks:
                if 0 <= s - lag < count:
                    task(Unit(0, s - lag))
        return
    assert count % LOOP == 0
    for s in range(peel):
        for lag, task in tasks:
            if s - lag >= 0:
                task(Unit(0, s - lag))
    with eng.Fori(peel // LOOP, count // LOOP) as i:
        for k in range(LOOP):
            for lag, task in tasks:
                task(Unit(i, k - lag))
    for s in range(count, count + depth):
        for lag, task in tasks:
            if s - lag < count:
                task(Unit(0, s - lag))


class Bank:

    def __init__(self, users, count):
        self.users, self.count = users, count
        self.at = {u[0]: i for i, u in enumerate(users)}

    def wait(self, eng, name, unit):
        n = self.at[name]
        step = unit.off + self.users[n][1]
        for m in range(n - 1, n - 1 - 8 * len(self.users), -1):
            _, lag, freed, k = self.users[m % len(self.users)]
            before = Unit(unit.base, step + m // len(self.users) - lag)
            if unit.static and not 0 <= before.off < self.count:
                continue
            freed.wait(eng, before, k)
            return


class Kit:

    def __init__(self, nc, ctx, stage, whole=None):
        self.nc, self.ctx, self.stage, self.whole, self.sems = nc, ctx, stage, whole or self, []

    def sb(self, name, shape, dt):
        return self.ctx.enter_context(self.nc.sbuf_tensor(f"{self.stage}_{name}", shape, dt))

    def ps(self, name):
        return self.ctx.enter_context(self.nc.psum_tensor(f"{self.stage}_{name}", [P, 512], F32))

    def sem(self, name):
        self.whole.sems.append(self.nc.alloc_semaphore(name=f"{self.stage}_{name}"))
        return self.whole.sems[-1]

    def end_phase(self):
        self.nc.clear_and_free_semaphores(self.sems)
        self.nc.all_engine_barrier()

    def sig(self, name, per=1):
        return Sig(self.sem(name), per)

    def dsig(self, name, n=1):
        return DmaSig([self.sem(f"{name}_a"), self.sem(f"{name}_b")], n)


def three_passes(eng, out, l_hi, l_lo, r_hi, r_lo, start, stop):
    eng.matmul(out, l_hi, r_hi, start=start, stop=False)
    eng.matmul(out, l_hi, r_lo, start=False, stop=False)
    return eng.matmul(out, l_lo, r_hi, start=False, stop=stop)


def together(nc, *programs):
    with nc.Block() as block:
        for name in ("sync", "tensor", "scalar", "vector", "gpsimd"):
            def run(eng, parts=[p[name] for p in programs if name in p]):
                for part in parts:
                    part(eng)
            {"sync": block.sync, "tensor": block.tensor, "scalar": block.scalar, "vector": block.vector,
             "gpsimd": block.gpsimd}[name](run)


def constants(k):
    c = {"ident": k.sb("ident", [P, P], F32), "identb": k.sb("identb", [P, P], BF16),
         "ident16": k.sb("ident16", [P, P], F16)}
    sel1 = k.sb("sel1", [P, HEADS, 1], BF16)
    c["sel"] = k.sb("sel", [P, HEADS, P], BF16)
    c["ones10"] = k.sb("ones10", [2, D], F16)
    c["ones6"] = k.sb("ones6", [2, D], F16)
    c["minus_half"] = k.sb("minus_half", [P, PAIR], F32)
    s, s_sel = k.sem("s_const"), k.sem("s_sel")
    zeroed = [c["ident"][:, :], c["identb"][:, :], c["ident16"][:, :], sel1[:, :, :]]
    c["s_ident"], c["ident_ready"] = s, len(zeroed) + 1

    def gpsimd(g):
        for t in zeroed:
            g.memset(t, 0.0).then_inc(s, 1)
        g.wait_ge(s, len(zeroed))
        for m in ("ident", "identb", "ident16"):
            g.affine_select(out=c[m][:, :], in_=c[m][:, :], compare_op=ALU.not_equal, fill=1.0, base=0,
                            pattern=[[-1, P]], channel_multiplier=1).then_inc(s, 1)
        n = 0
        for g0 in (0, 64):
            for part in range(PARTS):
                g.affine_select(out=sel1[:, :, 0], in_=sel1[:, :, 0], compare_op=ALU.not_equal, fill=1.0,
                                base=-(g0 + 16 * part), pattern=[[-1, HEADS]], channel_multiplier=1).then_inc(s_sel, 1)
                n += 1
                g.wait_ge(s_sel, n)
        g.memset(c["ones10"][:, :], p2(LN_X))
        g.memset(c["ones6"][:, :], p2(CTX_X))
        g.memset(c["minus_half"][:, :], -0.5)

    def vector(v):
        v.wait_ge(s_sel, 2 * PARTS)
        v.tensor_copy(c["sel"][:, :, :], sel1[:, :, :].to_broadcast([P, HEADS, P]))

    return c, {"gpsimd": gpsimd}, {"vector": vector}


def weight_buffers(k, mats, rows):
    out = {}
    for name, w, tr in mats:
        n_out, n_in = w.shape if tr else w.shape[::-1]
        out[name] = tuple(k.sb(f"{name}_{x}", [P, n_in // P, n_out], F16) for x in ("hi", "lo"))
    for name, b in rows:
        out[name] = k.sb(f"{name}_rows", [2, b.shape[0] * b.shape[1]], F16)
    return out


def prepare_weights(kk, c, out, mats, rows):
    loads, turned, plain, biases, parts_of = [], [], [], [], {}
    bank = [kk.ps(f"prep_ps{i}") for i in range(2)]
    for name, w, tr in mats:
        r, n = w.shape
        hi, lo = out[name]
        raw = kk.sb(f"{name}_raw", [P, r // P, n], F32)
        loads.append((raw[:, :, :], w.rearrange("(b p) n -> p b n", p=P)))
        if tr:
            for ib in range(n // P):
                for ob in range(0, r // P, 4):
                    nb = min(4, r // P - ob)
                    at = slice(ob * P, (ob + nb) * P)
                    turned.append(([raw[:, ob + j, ib * P:(ib + 1) * P] for j in range(nb)], hi[:, ib, at],
                                   lo[:, ib, at]))
        else:
            plain.append((raw[:, :, :], hi[:, :, :], lo[:, :, :]))
    for name, b in rows:
        r, n = b.shape
        raw, parts = kk.sb(f"{name}_rawrow", [r, n], F32), kk.sb(f"{name}_parts", [r, 2, n], F16)
        loads.append((raw[:, :], b))
        biases.append((raw[:, :], parts[:, 0, :], parts[:, 1, :]))
        parts_of[name] = parts
    s_ld, s_t, s_hi, s_lo, s_row = (kk.sem(f"prep_{x}") for x in ("ld", "t", "hi", "lo", "row"))

    def jobs():
        for n, (blocks, hi, lo) in enumerate(turned):
            yield bank[n % 2][:, 0:len(blocks) * P], hi, lo, n + 1
        for src, hi, lo in plain + biases:
            yield src, hi, lo, 0
    count = len(turned) + len(plain) + len(biases)

    def sync(sp):
        for to, src in loads:
            sp.dma_start(to, src).then_inc(s_ld, 16)

    def place_rows(g):
        g.wait_ge(s_lo, count)
        moves = 0
        for name, b in rows:
            r, n = b.shape
            for i in range(2):
                for j in range(r):
                    g.dma_start(out[name][i:i + 1, j * n:(j + 1) * n], parts_of[name][j:j + 1, i, :]).then_inc(s_row, 16)
                    moves += 1
        g.wait_ge(s_row, 16 * moves)

    def tensor(pe):
        pe.wait_ge(c["s_ident"], c["ident_ready"])
        pe.wait_ge(s_ld, 16 * len(loads))
        for n, (blocks, hi, lo) in enumerate(turned):
            if n >= 2:
                pe.wait_ge(s_lo, n - 1)
            for j, x in enumerate(blocks):
                m = pe.transpose(bank[n % 2][:, j * P:(j + 1) * P], x, c["ident"][:, :])
            m.then_inc(s_t, 1)

    def scalar(act):
        act.wait_ge(s_ld, 16 * len(loads))
        for src, hi, lo, t in jobs():
            if t:
                act.wait_ge(s_t, t)
            act.activation(hi, src, ACT.Copy, scale=p2(W_X)).then_inc(s_hi, 1)

    def vector(v):
        v.wait_ge(s_ld, 16 * len(loads))
        for n, (src, hi, lo, t) in enumerate(jobs()):
            v.wait_ge(s_hi, n + 1)
            v.scalar_tensor_tensor(out=lo, in0=src, scalar=p2(W_X), in1=hi, op0=ALU.mult,
                                   op1=ALU.subtract).then_inc(s_lo, 1)

    return {"sync": sync, "tensor": tensor, "scalar": scalar, "vector": vector}, place_rows


class Norm:

    def __init__(self, k, name, c, ticks_v, ticks_g):
        self.c, self.ticks_v, self.ticks_g = c, ticks_v, ticks_g
        self.st = [k.sb(f"{name}_st{i}", [P, PAIR, 6], F32) for i in range(2)]
        self.mv = [k.sb(f"{name}_mv{i}", [P, PAIR, 2], F32) for i in range(2)]
        self.ve = [k.sb(f"{name}_ve{i}", [P, PAIR], F32) for i in range(2)]
        self.rs = [k.sb(f"{name}_rs{i}", [P, PAIR], F32) for i in range(2)]
        self.xn = [k.sb(f"{name}_xn{i}", [P, PAIR, D], F32) for i in range(2)]
        self.s_st = k.sig(f"{name}_s_st", PAIR)
        self.s_mv = k.sig(f"{name}_s_mv", PAIR)
        self.s_ve = k.sig(f"{name}_s_ve")
        self.s_rs = k.sig(f"{name}_s_rs")
        self.s_xn = k.sig(f"{name}_s_xn", PAIR)

    def stats(self, v, u, x):
        s = u.slot
        self.s_rs.wait(v, u.back(2))
        for a in range(PAIR):
            v.bn_stats(self.st[s][:, a, :], x[:, a, :]).then_inc(self.s_st.sem, 1)
        for a in range(PAIR):
            self.s_st.wait(v, u, a + 1)
            settle(v, self.ticks_v)
            v.bn_aggr(self.mv[s][:, a, :], self.st[s][:, a, :]).then_inc(self.s_mv.sem, 1)

    def rstd(self, g, u):
        s = u.slot
        self.s_mv.wait(g, u)
        self.s_xn.wait(g, u.back(2))
        settle(g, self.ticks_g)
        g.tensor_scalar(self.ve[s][:, :], self.mv[s][:, :, 1], EPS, p2(-2 * LN_X), ALU.add,
                        ALU.mult).then_inc(self.s_ve.sem, 1)
        self.s_ve.wait(g, u)
        g.tensor_tensor(self.rs[s][:, :], self.ve[s][:, :], self.c["minus_half"][:, :],
                        ALU.pow).then_inc(self.s_rs.sem, 1)

    def apply(self, v, u, x):
        s = u.slot
        self.s_rs.wait(v, u)
        for a in range(PAIR):
            v.tensor_scalar(self.xn[s][:, a, :], x[:, a, :], self.mv[s][:, a, 0:1],
                            self.rs[s][:, a:a + 1], ALU.subtract, ALU.mult).then_inc(self.s_xn.sem, 1)


def transpose_pair(pe, bank, x, ident):
    for kb in range(KB):
        for a in range(PAIR):
            at = (kb * PAIR + a) * P
            m = pe.transpose(bank[:, at:at + P], x[:, a, kb * P:(kb + 1) * P], ident)
    return m


def slot_of(buffers, u):
    return buffers[u.slot if len(buffers) == 2 else u.slot4]


def v4(t):
    return t.rearrange("p (b n) -> p b n", b=KB)


def attention(nc, k0, c, w, io, n_seq, first, glog_top=None, idx_d=None):
    units = n_seq // PAIR
    exp_scale = p2(-2 * QK_X) * (DK ** -0.5 if first else D ** -0.5)
    x_in, x_out, h_out = (io["x"], io["x1"], io["h"]) if first else (io["x2"], io["x3"], io["h3"])
    with ExitStack() as ctx:
        k = Kit(nc, ctx, f"{k0.stage}_loop", k0.whole)
        two = lambda name, shape, dt: [k.sb(f"{name}{i}", shape, dt) for i in range(2)]
        four = lambda name, shape, dt: [k.sb(f"{name}{i}", shape, dt) for i in range(4)]
        xin = two("xin", [P, PAIR, D], F32)
        cin = two("cin", [P, PAIR, D], F32)
        xr = two("xr", [P, PAIR, D], F32)
        xT = two("xT", [P, 2, KB, PAIR * S], F16)
        cT = four("cT", [P, 2, KB, PAIR * S], F16)
        qk = two("qk", [P, 4, KB, PAIR * S], F16)
        qS = four("qS", [P, QB, PAIR * S], F16)
        kS = four("kS", [P, QB, PAIR * S], F16)
        vx = four("vx", [P, PAIR, HEADS, 2 * DK], F32)
        mx = two("mx", [P, PAIR, HEADS], F32)
        nm = two("nm", [P, PAIR, HEADS], F32)
        MAX = F16 if first else BF16
        m3 = two("m3", [P, PAIR, P], MAX)
        mT = two("mT", [P, PAIR, S], MAX)
        pt = [k.sb(f"pt{i}", [P, CH, S], F32) for i in range(4)]
        yE = two("yE", [P, PAIR, 512], F32)
        rec = two("rec", [P, PAIR, HEADS], F32)
        yn = two("yn", [P, PAIR, D], F32)
        yT = two("yT", [P, 2, KB, PAIR * S], F16)
        x1 = two("x1", [P, PAIR, D], F32)
        hT = two("hT", [P, 2, KB, PAIR * S], F16)
        gl = two("gl", [P, PAIR, EXP], F32)
        g8 = two("g8", [P, PAIR, EXP], F32)
        i8 = k.sb("i8", [P, EXP], U32)
        qkd = [nc.dram_tensor(f"qk_scratch{int(first)}{i}", (4, D, PAIR * S), F16, kind="Internal").ap() for i in range(2)]
        md = [nc.dram_tensor(f"max_scratch{int(first)}{i}", (PARTS * HEADS, PAIR * S), F16, kind="Internal").ap()
              for i in range(2)]
        ring3 = [k.ps(f"ring{i}") for i in range(3)]
        score_bank = [k.ps(f"score{i}") for i in range(2)]
        score_t_bank = [k.ps(f"scoreT{i}") for i in range(2)]
        av_bank = k.ps("av")

        tag = "a" if first else "b"
        s_fill, s_ones = k.sem("s_fill"), k.sem("s_ones")
        ticks_v, ticks_g, ticks_s = (k.sem(f"ticks_{e}") for e in "vgs")
        ln0, ln1 = (Norm(k, f"{n}{tag}", c, ticks_v, ticks_g) for n in ("ln0", "ln1"))
        d_x, d_c, d_xr = k.dsig("d_x"), k.dsig("d_c"), k.dsig("d_xr")
        d_q, d_k, d_x1, d_h = k.dsig("d_q"), k.dsig("d_k"), k.dsig("d_x1"), k.dsig("d_h")
        d_m, d_mp = k.dsig("d_m"), k.dsig("d_mp", 2)
        d_stq, d_stk = k.dsig("d_stq", 6), k.dsig("d_stk", 6)
        d_ct = k.dsig("d_ct")
        g = lambda name, per=1: k.sig(name, per)
        s_tx, s_tc, s_xh, s_xl, s_ch, s_cl = g("s_tx"), g("s_tc"), g("s_xh"), g("s_xl"), g("s_ch"), g("s_cl")
        s_q, s_k, s_v, s_qh, s_ql, s_kh, s_kl, s_ve = (g(n) for n in "s_q s_k s_v s_qh s_ql s_kh s_kl s_vev".split())
        NC = PAIR * CHUNKS
        DEPTH = 7
        s_s, s_mx, s_st, s_e, s_av = (g(n, NC) for n in "s_s s_mx s_st s_e s_av".split())
        s_ye, s_yt, s_rec, s_yn = (g(n, PAIR) for n in "s_ye s_yt s_rec s_yn".split())
        s_m3, s_mt, s_mte = g("s_m3", 6 if first else 7), g("s_mt"), g("s_mte")
        s_y2, s_yh, s_yl, s_o, s_x1, s_t1, s_hh, s_hl = (g(n) for n in "s_y2 s_yh s_yl s_o s_x1 s_t1 s_hh s_hl".split())
        s_g, s_gl, s_g8, s_gt = g("s_g"), g("s_gl"), g("s_g8", PAIR), g("s_gt")
        s_idx, s_idxd = k.sem("s_idx"), k.sem("s_idxd")
        AV = (0, "av")
        if first:
            t_first = 2
            plan = [[AV, (2, "q")], [AV, (6, "t_y"), (2, "k"), (4, "t_max")], [AV], [(1, "t_x"), (7, "t_1"), (6, "o"), AV],
                    [AV, (5, "y0")], [AV, (2, "v")], [AV, (1, "t_c")], [(7, "gate"), AV, (5, "y1")]]
            shared = (("t_y", "t_1", "y0", "y1"), ("k", "o", "v", "gate"), ("q", "t_max", "t_x", "t_c"))
        else:
            t_first = 5
            plan = [[AV, (6, "o")], [AV, (5, "y0"), (2, "q"), (4, "t_max")], [AV], [AV, (1, "t_x")],
                    [AV, (5, "y1"), (6, "t_1")], [AV], [AV, (5, "t_y")], [AV]]
            shared = (("y0", "y1", "t_y"), ("o", "t_max", "t_x", "t_1"), ("q",))
        read = {"y0": (s_yn, 1), "y1": (s_yn, 2), "t_y": (s_yl, 1), "o": (s_x1, 1), "t_max": (s_mte, 1),
                "t_x": (s_xl, 1), "t_1": (s_hl, 1), "q": (s_ql, 1), "k": (s_kl, 1), "v": (s_ve, 1),
                "t_c": (s_cl, 1), "gate": (s_gl, 1)}
        ring, bank_of = {}, {}
        for i, products in enumerate(shared):
            bank = Bank([(name, lag, *read[name]) for part in plan for lag, name in part if name in products], units)
            for name in products:
                ring[name], bank_of[name] = ring3[i], bank

        def lag_t(n):
            return 4 if n < t_first else 5

        xv = x_in.rearrange("(u a) s d -> u s a d", a=PAIR)
        cv = io["ctx"].rearrange("(u a) s d -> u s a d", a=PAIR)
        x1v = x_out.rearrange("(u a) s d -> u s a d", a=PAIR)

        with nc.Block() as block:
            @block.sync
            def _(sp):
                def load(u):
                    s = u.slot
                    ln0.s_xn.wait(sp, u.back(2))
                    d_x.inc(sp.dma_start(xin[s][:, :, :], xv[u.no]), u)
                    (s_tc if first else s_ve).wait(sp, u.back(2))
                    d_c.inc(sp.dma_start(cin[s][:, :, :], cv[u.no]), u)

                def store_x1(u):
                    s_x1.wait(sp, u)
                    d_x1.inc(sp.dma_start(x1v[u.no], x1[u.slot][:, :, :]), u)

                def store_h(u):
                    s_hl.wait(sp, u)
                    s_hh.wait(sp, u)
                    d_h.inc(sp.dma_start(h_out[u.no], hT[u.slot][:, :, :, :]), u)

                def reload_x(u):
                    s_x1.wait(sp, u.back(2))
                    d_xr.inc(sp.dma_start(xr[u.slot][:, :, :], xv[u.no]), u)

                def store_ct(u):
                    s_cl.wait(sp, u)
                    s_ch.wait(sp, u)
                    d_ct.inc(sp.dma_start(io["ct"][u.no].rearrange("w (b p) n -> p w b n", p=P),
                                          cT[u.slot4][:, :, :, :]), u)

                def store_q(u):
                    s_ql.wait(sp, u)
                    settle(sp, ticks_s)
                    d_stq.wait(sp, u.back(2))
                    d_q.inc(sp.dma_start(scratch(u, 0), qk[u.slot][:, 0:2, :, :]), u)

                def store_k(u):
                    s_kl.wait(sp, u)
                    d_stk.wait(sp, u.back(2))
                    d_k.inc(sp.dma_start(scratch(u, 2), qk[u.slot][:, 2:4, :, :]), u)

                def scratch(u, at):
                    return qkd[u.slot][at:at + 2].rearrange("w (b p) n -> p w b n", p=P)

                def stack(u, done, dst, parts):
                    for hh in range(2):
                        for i, part in enumerate(parts):
                            src = part.rearrange("(b h d) n -> h d b n", h=2, d=DK)[hh]
                            at = 64 * hh + DK * i
                            done.inc(sp.dma_start(dst[u.slot4][at:at + DK, :, :], src), u)

                def stack_q(u):
                    d_q.wait(sp, u)
                    s_st.wait(sp, u.back(4))
                    hi, lo = qkd[u.slot][0], qkd[u.slot][1]
                    stack(u, d_stq, qS, (hi, hi, lo))

                def stack_k(u):
                    if first:
                        if u.static and u.no < len(kS):
                            sp.wait_ge(s_fill, len(m3) + 2 * (u.no + 1))
                        d_k.wait(sp, u)
                        hi, lo = qkd[u.slot][2], qkd[u.slot][3]
                    else:
                        hi, lo = io["ct"][u.no][0], io["ct"][u.no][1]
                    s_st.wait(sp, u.back(4))
                    stack(u, d_stk, kS, (hi, lo, hi))

                def store_max(u):
                    s_mte.wait(sp, u)
                    settle(sp, ticks_s)
                    d_mp.wait(sp, u.back(2))
                    d_m.inc(sp.dma_start(md[u.slot][:, :], mT[u.slot][0:PARTS * HEADS, :, :]), u)

                def place_max(u):
                    d_m.wait(sp, u)
                    for hh in range(2):
                        src = md[u.slot].rearrange("(i h b) n -> h i b n", i=PARTS, h=2)[hh]
                        at = 64 * hh + 3 * DK
                        d_mp.inc(sp.dma_start(qS[u.slot4][at:at + PARTS, :, :], src), u)

                if first:
                    tasks = [(2, store_ct), (0, load), (2, store_q), (4, store_max), (2, store_k), (4, place_max),
                             (5, reload_x), (2, stack_q), (2, stack_k), (6, store_x1), (7, store_h)]
                else:
                    tasks = [(2, stack_k), (0, load), (6, store_x1), (2, store_q), (5, reload_x), (2, stack_q),
                             (6, store_h)]
                run_steps(sp, tasks, units, DEPTH)
                for s in range(2):
                    last = Unit(0, units - 2 + s)
                    d_x1.wait(sp, last)
                    d_h.wait(sp, last)
                    if first:
                        d_ct.wait(sp, last)
                if first:
                    sp.wait_ge(s_idx, 1)
                    sp.dma_start(idx_d, i8[0:n_seq, 0:2]).then_inc(s_idxd, 16)
                    sp.wait_ge(s_idxd, 16)

            @block.gpsimd
            def _(p):
                def fill(t, value, n):
                    p.memset(t, value).then_inc(s_fill, 1)
                    p.wait_ge(s_fill, n)
                for n, t in enumerate(m3):
                    fill(t[:, :, :], 0.0, n + 1)

                def maxima(u):
                    s = u.slot
                    s_mx.wait(p, u)
                    s_mt.wait(p, u.back(2))
                    settle(p, ticks_g)
                    part = [m3[s][:, :, 16 * i:16 * i + 16] for i in range(PARTS)]
                    n = [0]

                    def then(ins):
                        n[0] += 1
                        ins.then_inc(s_m3.sem, 1)
                        if n[0] < s_m3.per:
                            s_m3.wait(p, u, n[0])
                            settle(p, ticks_g)
                    then(p.tensor_scalar(nm[s][:, :, :], mx[s][:, :, :], -p2(-M_X) if first else -1.0, None, ALU.mult))
                    then(p.tensor_copy(part[0], nm[s][:, :, :]))
                    then(p.tensor_tensor(nm[s][:, :, :], nm[s][:, :, :], part[0], ALU.subtract))
                    then(p.tensor_copy(part[1], nm[s][:, :, :]))
                    then(p.tensor_tensor(nm[s][:, :, :], nm[s][:, :, :], part[1], ALU.subtract))
                    then(p.tensor_copy(part[2], nm[s][:, :, :]))
                    if not first:
                        then(p.tensor_copy(m3[s][:, :, 64:112], m3[s][:, :, 0:48]))

                def ctx_as_v(u):
                    d_c.wait(p, u)
                    s_av.wait(p, u.back(4))
                    settle(p, ticks_g)
                    p.tensor_copy(vx[u.slot4][:, :, :, 0:DK],
                                  cin[u.slot][:, :, :].rearrange("p a (h d) -> p a h d", d=DK)).then_inc(s_ve.sem, 1)

                def rstd0(u):
                    ln0.rstd(p, u)
                    if first and u.static and u.no < len(kS):
                        ln0.s_rs.wait(p, u)
                        for n, at in enumerate((32, 96), len(m3) + 2 * u.no + 1):
                            fill(kS[u.no][at:at + 32, :, :], p2(M_X), n)

                def rstd1(u):
                    ln1.rstd(p, u)

                tasks = [(0, rstd0), (6, rstd1)] if first else [(6, rstd1), (2, ctx_as_v), (0, rstd0)]
                run_steps(p, [(4, maxima)] + tasks, units, DEPTH)

            @block.tensor
            def _(pe):
                ident = c["ident"][:, :]

                def free(name, u):
                    bank_of[name].wait(pe, name, u)

                def t_x(u):
                    ln0.s_xn.wait(pe, u)
                    free("t_x", u)
                    transpose_pair(pe, ring["t_x"], ln0.xn[u.slot], ident).then_inc(s_tx.sem, 1)

                def t_c(u):
                    d_c.wait(pe, u)
                    free("t_c", u)
                    transpose_pair(pe, ring["t_c"], cin[u.slot], ident).then_inc(s_tc.sem, 1)

                def project(u, bank, src, name, bias, ones):
                    hi, lo = w[name]
                    x = src(u)
                    for mb in range(KB):
                        o = bank[:, mb * 256:(mb + 1) * 256]
                        for kb in range(KB):
                            three_passes(pe, o, hi[:, kb, mb * P:(mb + 1) * P], lo[:, kb, mb * P:(mb + 1) * P],
                                         x[:, 0, kb, :], x[:, 1, kb, :], kb == 0, False)
                        m = pe.matmul(o, w[bias][:, mb * P:(mb + 1) * P], ones[:, :], start=False, stop=True)
                    return m

                def fold_q(u):
                    s_xl.wait(pe, u)
                    free("q", u)
                    hi, lo = w["wa"]
                    x = xT[u.slot]
                    for kb in range(KB):
                        m = three_passes(pe, ring["q"][:, kb * 256:(kb + 1) * 256], hi[:, 0, :], lo[:, 0, :],
                                         x[:, 0, kb, :], x[:, 1, kb, :], True, True)
                    m.then_inc(s_q.sem, 1)

                def project_rows(u, bank, src, name, bias, ones):
                    hi, lo = w[name]
                    x = src(u)
                    for a in range(PAIR):
                        o = bank[:, a * D:(a + 1) * D]
                        at = slice(a * S, (a + 1) * S)
                        for kb in range(KB):
                            three_passes(pe, o, x[:, 0, kb, at], x[:, 1, kb, at], hi[:, kb, :], lo[:, kb, :],
                                         kb == 0, False)
                        m = pe.matmul(o, ones[:, 0:S], w[bias][:, :], start=False, stop=True)
                    return m

                def q(u):
                    s_xl.wait(pe, u)
                    free("q", u)
                    project(u, ring["q"], lambda u: xT[u.slot], "wq", "bq", c["ones10"]).then_inc(s_q.sem, 1)

                def kk(u):
                    s_cl.wait(pe, u)
                    free("k", u)
                    project(u, ring["k"], lambda u: cT[u.slot4], "wk", "bk", c["ones6"]).then_inc(s_k.sem, 1)

                def vv(u):
                    s_cl.wait(pe, u)
                    free("v", u)
                    project_rows(u, ring["v"], lambda u: cT[u.slot4], "wv", "bv", c["ones6"]).then_inc(s_v.sem, 1)

                def score(n):
                    a, ch = n // CHUNKS, n % CHUNKS
                    hh, g4 = ch // 2, ch % 2
                    rows = slice(64 * hh, 64 * hh + 3 * DK)
                    at = slice(a * S, (a + 1) * S)

                    def go(u):
                        if n == 0:
                            d_stq.wait(pe, u)
                            d_stk.wait(pe, u)
                        s_mx.wait(pe, u, n - 1)
                        for j in range(CH):
                            b = 4 * g4 + j
                            m = pe.matmul(score_bank[n % 2][:, j * S:(j + 1) * S], qS[u.slot4][rows, b, at],
                                          kS[u.slot4][rows, b, at], start=first or j == 0, stop=first,
                                          skip_group_check=not first)
                        if not first:
                            m = pe.matmul(score_bank[n % 2][:, :], c["identb"][:, :], w["mask"][:, :], start=False, stop=True,
                                          skip_group_check=True)
                        m.then_inc(s_s.sem, 1)
                    return go

                def t_max(u):
                    s_m3.wait(pe, u)
                    free("t_max", u)
                    o = ring["t_max"][:, 0:S].bitcast(MAX)
                    for a in range(PAIR):
                        m = pe.transpose(o[:, a * S:(a + 1) * S], m3[u.slot][:, a, :], c["ident16" if first else "identb"][:, :])
                    m.then_inc(s_mt.sem, 1)

                def score_t(n):
                    a, ch = n // CHUNKS, n % CHUNKS
                    hh, g4 = ch // 2, ch % 2
                    rows = slice(64 * hh, 64 * hh + 3 * DK)
                    at = slice(a * S, (a + 1) * S)

                    def go(u):
                        s_e.wait(pe, u, n - 1)
                        (d_mp if first else s_mte).wait(pe, u)
                        o = score_t_bank[n % 2][:, :].rearrange("p (j n) -> p j n", j=CH)
                        if first:
                            rows_m = slice(64 * hh, 64 * hh + 3 * DK + PARTS)
                            for j in range(CH):
                                b = 4 * g4 + j
                                m = pe.matmul(o[:, j, :], kS[u.slot4][rows_m, b, at], qS[u.slot4][rows_m, b, at],
                                              start=True, stop=True)
                            m.then_inc(s_st.sem, 1)
                            return
                        for j in range(CH):
                            b = 4 * g4 + j
                            pe.matmul(o[:, j, :], kS[u.slot4][rows, b, at], qS[u.slot4][rows, b, at], start=j == 0,
                                      stop=False, skip_group_check=True)
                        pe.matmul(score_t_bank[n % 2][:, :], c["identb"][:, :], w["maskT"][:, :], start=False, stop=False,
                                  skip_group_check=True)
                        for j in range(CH):
                            m = pe.matmul(o[:, j, :], c["sel"][rows, 8 * hh + 4 * g4 + j, :], mT[u.slot][rows, a, :],
                                          start=False, stop=j == CH - 1, skip_group_check=True)
                        m.then_inc(s_st.sem, 1)
                    return go

                def av(n):
                    a, ch = n // CHUNKS, n % CHUNKS
                    hh, g4 = ch // 2, ch % 2

                    def go(u):
                        s_e.wait(pe, u, n + 1)
                        if n == 0 and u.static and u.no == 0:
                            pe.wait_ge(s_ones, len(vx))
                        if n == 0:
                            s_ve.wait(pe, u)
                        if ch == 0:
                            s_ye.wait(pe, u, a)
                        for j in range(CH):
                            head = 2 * (4 * g4 + j) + hh
                            m = pe.matmul(av_bank[32 * j:32 * j + 32, ch * S:(ch + 1) * S], vx[u.slot4][:, a, head, :],
                                          pt[n % 4][:, j, :], start=True, stop=True)
                        m.then_inc(s_av.sem, 1)
                    return go

                def y_rows(a):
                    def go(u):
                        s_ye.wait(pe, u, a + 1)
                        free(f"y{a}", u)
                        for ch in range(CHUNKS):
                            at = slice(ch * P, (ch + 1) * P)
                            m = pe.transpose(ring["y0"][:, at], yE[u.slot][:, a, at], ident)
                        m.then_inc(s_yt.sem, 1)
                    return go

                def t_y(u):
                    s_yn.wait(pe, u)
                    free("t_y", u)
                    transpose_pair(pe, ring["t_y"], yn[u.slot], ident).then_inc(s_y2.sem, 1)

                def o(u):
                    s_yl.wait(pe, u)
                    free("o", u)
                    project_rows(u, ring["o"], lambda u: yT[u.slot], "wo", "bo", c["ones6"]).then_inc(s_o.sem, 1)

                def t_1(u):
                    ln1.s_xn.wait(pe, u)
                    free("t_1", u)
                    transpose_pair(pe, ring["t_1"], ln1.xn[u.slot], ident).then_inc(s_t1.sem, 1)

                def gate(u):
                    s_hl.wait(pe, u)
                    free("gate", u)
                    hi, lo = w["wg"]
                    for a in range(PAIR):
                        out = ring["gate"][:, a * EXP:(a + 1) * EXP]
                        at = slice(a * S, (a + 1) * S)
                        for kb in range(KB):
                            three_passes(pe, out, hT[u.slot][:, 0, kb, at], hT[u.slot][:, 1, kb, at], hi[:, kb, :],
                                         lo[:, kb, :], kb == 0, False)
                        m = pe.matmul(out, c["ones10"][:, 0:S], w["bg"][:, :], start=False, stop=True)
                    m.then_inc(s_g.sem, 1)

                make = {"t_x": t_x, "t_c": t_c, "q": q if first else fold_q, "k": kk, "v": vv, "t_max": t_max,
                        "y0": y_rows(0), "y1": y_rows(1), "t_y": t_y, "o": o, "t_1": t_1, "gate": gate}
                tasks = []
                for part in range(NC):
                    n = (part + t_first) % NC
                    before = (n - 1) % NC
                    after_scores = (4 if before < t_first - 1 else 5, av(before))
                    tasks.append((lag_t(n), score_t(n)))
                    tasks += [after_scores if item == AV else (item[0], make[item[1]]) for item in plan[part]]
                    tasks.append((3, score(part)))
                run_steps(pe, tasks, units, DEPTH)

            @block.scalar
            def _(act):

                def hi_part(done, src, dst, after, freed, scale):
                    def go(u):
                        after.wait(act, u)
                        for f, ago in freed:
                            f.wait(act, u.back(ago))
                        act.activation(slot_of(dst, u)[:, 0, :, :], v4(src), ACT.Copy, scale=scale).then_inc(done.sem, 1)
                    return go

                hi_x = hi_part(s_xh, ring["t_x"][:, :], xT, s_tx, [(s_q, 2)], 1.0)
                hi_c = first and hi_part(s_ch, ring["t_c"][:, :], cT, s_tc, [(s_v, 4), (d_ct, 4)], p2(CTX_X))
                hi_y = hi_part(s_yh, ring["t_y"][:, :], yT, s_y2, [(s_o, 2)], p2(Y_X))
                hi_h = hi_part(s_hh, ring["t_1"][:, :], hT, s_t1, [(s_g, 2)] * first + [(d_h, 2)], 1.0)

                def hi_q(u):
                    s_q.wait(act, u)
                    d_q.wait(act, u.back(2))
                    act.activation(qk[u.slot][:, 0, :, :], v4(ring["q"][:, :]), ACT.Copy,
                                   scale=p2(QK_X - LN_X - W_X)).then_inc(s_qh.sem, 1)

                def hi_k(u):
                    s_k.wait(act, u)
                    d_k.wait(act, u.back(2))
                    act.activation(qk[u.slot][:, 2, :, :], v4(ring["k"][:, :]), ACT.Copy,
                                   scale=p2(QK_X - CTX_X - W_X)).then_inc(s_kh.sem, 1)

                def copy_v(u):
                    s_v.wait(act, u)
                    s_av.wait(act, u.back(4))
                    act.activation(vx[u.slot4][:, :, :, 0:DK],
                                   ring["v"][:, :].rearrange("p (a h d) -> p a h d", a=PAIR, d=DK), ACT.Copy,
                                   scale=p2(-CTX_X - W_X)).then_inc(s_ve.sem, 1)

                def copy_max(u):
                    s_mt.wait(act, u)
                    (d_m if first else s_st).wait(act, u.back(2))
                    act.activation(mT[u.slot][:, :, :], ring["t_max"][:, 0:S].bitcast(MAX).rearrange("p (a n) -> p a n", a=PAIR),
                                   ACT.Copy).then_inc(s_mte.sem, 1)

                def expo(n):
                    def go(u):
                        s_st.wait(act, u, n + 1)
                        s_av.wait(act, u, n - 3)
                        act.activation(pt[n % 4][:, :, :], score_t_bank[n % 2][:, :].rearrange("p (j n) -> p j n", j=CH),
                                       ACT.Exp, scale=exp_scale).then_inc(s_e.sem, 1)
                    return go

                def copy_y(a):
                    def go(u):
                        s_av.wait(act, u, CHUNKS * (a + 1))
                        s_yt.wait(act, u.back(2), a + 1)
                        act.activation(yE[u.slot][:, a, :], av_bank[:, :], ACT.Copy).then_inc(s_ye.sem, 1)
                    return go

                def copy_gate(u):
                    s_g.wait(act, u)
                    s_g8.wait(act, u.back(2))
                    act.activation(gl[u.slot][:, :, :], ring["gate"][:, 0:PAIR * EXP].rearrange("p (a n) -> p a n", a=PAIR),
                                   ACT.Copy, scale=p2(-LN_X - W_X)).then_inc(s_gl.sem, 1)

                if first:
                    items = [[(2, hi_q)], [(6, hi_y), (2, hi_k), (4, copy_max)], [(5, copy_y(0))], [(1, hi_x), (7, hi_h)],
                             [], [(2, copy_v)], [(5, copy_y(1)), (1, hi_c)], [(7, copy_gate)]]
                else:
                    items = [[], [(2, hi_q), (4, copy_max)], [], [(5, copy_y(1)), (1, hi_x)], [(6, hi_h)], [],
                             [(5, hi_y)], [(4, copy_y(0))]]
                tasks = []
                for part in range(NC):
                    n = (part + t_first) % NC
                    tasks += [(lag_t(n), expo(n))] + items[part]
                run_steps(act, tasks, units, DEPTH)

            @block.vector
            def _(v):
                for t in vx:
                    v.memset(t[:, :, :, DK:2 * DK], 1.0).then_inc(s_ones, 1)

                def lo_part(done, src, dst, w0, after, freed, scale):
                    def go(u):
                        after.wait(v, u)
                        for f, ago in freed:
                            f.wait(v, u.back(ago))
                        v.scalar_tensor_tensor(out=slot_of(dst, u)[:, w0 + 1, :, :], in0=v4(src), scalar=scale,
                                               in1=slot_of(dst, u)[:, w0, :, :], op0=ALU.mult,
                                               op1=ALU.subtract).then_inc(done.sem, 1)
                    return go

                lo_x = lo_part(s_xl, ring["t_x"][:, :], xT, 0, s_xh, [(s_q, 2)], 1.0)
                lo_c = first and lo_part(s_cl, ring["t_c"][:, :], cT, 0, s_ch, [(s_v, 4), (d_ct, 4)], p2(CTX_X))
                lo_q = lo_part(s_ql, ring["q"][:, :], qk, 0, s_qh, [(d_q, 2)], p2(QK_X - LN_X - W_X))
                lo_k = first and lo_part(s_kl, ring["k"][:, :], qk, 2, s_kh, [(d_k, 2)], p2(QK_X - CTX_X - W_X))
                lo_y = lo_part(s_yl, ring["t_y"][:, :], yT, 0, s_yh, [(s_o, 2)], p2(Y_X))
                lo_h = lo_part(s_hl, ring["t_1"][:, :], hT, 0, s_hh, [(s_g, 2)] * first + [(d_h, 2)], 1.0)

                def norm0_stats(u):
                    d_x.wait(v, u)
                    ln0.stats(v, u, xin[u.slot])

                def norm0(u):
                    s_tx.wait(v, u.back(2))
                    ln0.apply(v, u, xin[u.slot])

                def add_x(u):
                    s_o.wait(v, u)
                    d_xr.wait(v, u)
                    d_x1.wait(v, u.back(2))
                    v.scalar_tensor_tensor(out=x1[u.slot][:, :, :],
                                           in0=ring["o"][:, :].rearrange("p (a n) -> p a n", a=PAIR),
                                           scalar=p2(-Y_X - W_X), in1=xr[u.slot][:, :, :], op0=ALU.mult,
                                           op1=ALU.add).then_inc(s_x1.sem, 1)

                def norm1_stats(u):
                    s_x1.wait(v, u)
                    ln1.stats(v, u, x1[u.slot])

                def norm1(u):
                    s_t1.wait(v, u.back(2))
                    ln1.apply(v, u, x1[u.slot])

                def row_max(n):
                    a, ch = n // CHUNKS, n % CHUNKS

                    def go(u):
                        s_s.wait(v, u, n + 1)
                        if n == 0:
                            s_m3.wait(v, u.back(2))
                        v.tensor_reduce(mx[u.slot][:, a, CH * ch:CH * ch + CH],
                                        score_bank[n % 2][:, :].rearrange("p (j n) -> p j n", j=CH), AX.X,
                                        ALU.max).then_inc(s_mx.sem, 1)
                    return go

                def norm_y(a):
                    def go(u):
                        s_yt.wait(v, u, a + 1)
                        s_y2.wait(v, u.back(2))
                        y = ring["y0"][:, :].rearrange("p (h n) -> p h n", n=2 * DK)
                        v.reciprocal(rec[u.slot][:, a, :], y[:, :, DK]).then_inc(s_rec.sem, 1)
                        s_rec.wait(v, u, a + 1)
                        r = rec[u.slot][:, a, :].rearrange("p (hh b) -> p hh b", hh=2).unsqueeze(3)
                        v.tensor_tensor(yn[u.slot][:, a, :].rearrange("p (b hh d) -> p hh b d", hh=2, d=DK),
                                        y[:, :, 0:DK].rearrange("p (hh b) d -> p hh b d", hh=2),
                                        r.to_broadcast([P, 2, QB, DK]), ALU.mult).then_inc(s_yn.sem, 1)
                    return go

                def top(u):
                    s_gl.wait(v, u)
                    s_gt.wait(v, u.back(2))
                    settle(v, ticks_v)
                    for a in range(PAIR):
                        v.max(g8[u.slot][:, a, :], gl[u.slot][:, a, :]).then_inc(s_g8.sem, 1)
                    s_g8.wait(v, u)
                    if u.static and u.no == 0:
                        v.max_index(i8[:, :], g8[0][:, 0, :], gl[0][:, 0, :]).then_inc(s_idx, 1)
                    v.tensor_copy(glog_top[:, bass.ts(u.no, PAIR), :], g8[u.slot][:, :, 0:2]).then_inc(s_gt.sem, 1)

                if first:
                    items = [[(7, norm1)], [(2, lo_q), (6, lo_y)], [(2, lo_k)], [(1, lo_x), (7, lo_h), (0, norm0_stats), (6, add_x)],
                             [(6, norm1_stats), (5, norm_y(0))], [(0, norm0)], [],
                             [(1, lo_c), (5, norm_y(1))], [(7, top)]]
                else:
                    items = [[(6, add_x)], [(6, norm1_stats), (5, norm_y(0))], [(2, lo_q), (6, norm1)], [(1, lo_x)],
                             [(5, norm_y(1))], [(6, lo_h), (0, norm0_stats)], [], [(5, lo_y), (0, norm0)], []]
                tasks = []
                for part in range(NC):
                    tasks += items[part] + [(3, row_max(part))]
                tasks += items[NC]
                run_steps(v, tasks, units, DEPTH)


def gates(kk, top, gate, n_seq):
    e, d = kk.sb("gate_e", [P, n_seq], F32), kk.sb("gate_d", [P, n_seq], F32)
    s = kk.sem("s_gate")

    def vector(v):
        v.tensor_tensor(d[:, :], top[:, :, 1], top[:, :, 0], ALU.subtract).then_inc(s, 1)
        v.wait_ge(s, 2)
        v.tensor_scalar(d[:, :], e[:, :], 1.0, None, ALU.add).then_inc(s, 1)
        v.wait_ge(s, 3)
        v.reciprocal(d[:, :], d[:, :]).then_inc(s, 1)
        v.wait_ge(s, 4)
        v.tensor_scalar(gate[:, :, 0], d[:, :], p2(-H_X - W_X), None, ALU.mult).then_inc(s, 1)
        v.wait_ge(s, 5)
        v.tensor_tensor(gate[:, :, 1], gate[:, :, 0], e[:, :], ALU.mult)

    def scalar(act):
        act.wait_ge(s, 1)
        act.activation(e[:, :], d[:, :], ACT.Exp).then_inc(s, 1)

    return {"vector": vector, "scalar": scalar}


def expert_buffers(k, n_seq):
    return {"w1_hi": k.sb("w1_hi", [P, EXP, KB, HID], F16), "w1_lo": k.sb("w1_lo", [P, EXP, KB, HID], F16),
            "w2": k.sb("w2", [P, EXP, HB, 2, D], F16),
            "b1": k.sb("b1T", [P, EXP * HB], F32),
            "idx": k.sb("idx", [1, n_seq // PAIR + 1, 8], U32)}


def prepare_experts(kk, c, w, io, idx_d):
    SLOTS, HALVES = 4, 2
    jobs = []
    for e in range(EXP):
        for i in range(HALVES):
            at = slice(i * KB // HALVES, (i + 1) * KB // HALVES)
            jobs.append((io["L0_ffn_W1"][e].rearrange("(b p) n -> p b n", p=P)[:, at, :],
                         w["w1_hi"][:, e, at, :], w["w1_lo"][:, e, at, :]))
            at = slice(i * HB // HALVES, (i + 1) * HB // HALVES)
            jobs.append((io["L0_ffn_W2"][e].rearrange("(b p) n -> p b n", p=P)[:, at, :],
                         w["w2"][:, e, at, 0, :], w["w2"][:, e, at, 1, :]))
    raw = [kk.sb(f"expert_raw{i}", [P, KB * HID // HALVES], F32) for i in range(SLOTS)]
    b1r = kk.sb("b1_raw", [EXP * HB, P], F32)
    listed = kk.sb("experts_listed", [1, idx_d.shape[0] // PAIR, 2 * PAIR], U32)
    bank = kk.ps("b1_ps")
    s_ld = [kk.sem(f"expert_ld{i}") for i in range(SLOTS)]
    s_hi, s_lo, s_b, s_t, s_i = (kk.sem(f"expert_{x}") for x in ("hi", "lo", "b", "t", "i"))

    def view(i):
        return raw[i % SLOTS][:, :].rearrange("p (b n) -> p b n", b=jobs[i][1].shape[1])

    def sync(sp):
        sp.dma_start(b1r[:, :], io["L0_ffn_b1"].rearrange("e (b p) -> (e b) p", p=P)).then_inc(s_b, 16)
        sp.dma_start(listed[:, :, :], idx_d.rearrange("(o u a) n -> o u (a n)", o=1, a=PAIR)).then_inc(s_i, 16)
        for i, (src, hi, lo) in enumerate(jobs):
            if i >= SLOTS:
                sp.wait_ge(s_lo, i - SLOTS + 1)
            sp.dma_start(view(i), src).then_inc(s_ld[i % SLOTS], 16)

    def tensor(pe):
        pe.wait_ge(s_b, 16)
        pe.transpose(bank[:, 0:EXP * HB], b1r[:, :], c["ident"][0:EXP * HB, 0:EXP * HB]).then_inc(s_t, 1)

    def scalar(act):
        for i, (src, hi, lo) in enumerate(jobs):
            act.wait_ge(s_ld[i % SLOTS], 16 * (i // SLOTS + 1))
            act.activation(hi, view(i), ACT.Copy, scale=p2(W_X)).then_inc(s_hi, 1)

    def vector(v):
        v.wait_ge(s_t, 1)
        v.tensor_copy(w["b1"][:, :], bank[:, 0:EXP * HB])
        v.wait_ge(s_i, 16)
        idx, units = w["idx"], listed.shape[1]
        v.memset(idx[:, 0:1, 0:2], 0)
        v.tensor_scalar(idx[:, 0:units, 2:6], listed[:, :, :], EXP - 1, None, ALU.min)
        v.tensor_scalar(idx[:, 1:units + 1, 0:2], listed[:, :, 2:4], EXP - 1, None, ALU.min)
        for i, (src, hi, lo) in enumerate(jobs):
            v.wait_ge(s_hi, i + 1)
            v.scalar_tensor_tensor(out=lo, in0=view(i), scalar=p2(W_X), in1=hi, op0=ALU.mult,
                                   op1=ALU.subtract).then_inc(s_lo, 1)

    return {"sync": sync, "tensor": tensor, "scalar": scalar, "vector": vector}


def read_experts(nc, eng, idx, row, cols):
    at = idx[0:1, bass.ds(row, 1), cols].rearrange("p o n -> p (o n)")
    _, values = nc.values_load_multi_w_load_instructions(at, engines=[eng.engine], min_val=0, max_val=EXP - 1,
                                                         skip_runtime_bounds_check_because="VectorE has clamped them")
    return values


def experts(nc, k0, c, w, io, n_seq, gate):
    units = n_seq // PAIR
    NC = PAIR * 2 * 2
    with ExitStack() as ctx:
        k = Kit(nc, ctx, f"{k0.stage}_loop", k0.whole)
        two = lambda name, shape, dt: [k.sb(f"{name}{i}", shape, dt) for i in range(2)]
        hT = two("moe_h", [P, 2, KB, PAIR * S], F16)
        x1 = two("moe_x1", [P, PAIR, D], F32)
        x2 = two("moe_x2", [P, PAIR, D], F32)
        sums = [k.sb(f"moe_t{i}", [P, PAIR, D], F32) for i in range(3)]
        NH = 4
        hf = [k.sb(f"hf{i}", [P, 4, S], F32) for i in range(NH)]
        hh = [k.sb(f"hh{i}", [P, 4, S], F16) for i in range(NH)]
        hl = [k.sb(f"hl{i}", [P, 4, S], F16) for i in range(NH)]
        hid_bank = [k.ps(f"hid{i}") for i in range(4)]
        y_bank = [[k.ps(f"moe_y{a}{ex}") for ex in range(2)] for a in range(PAIR)]
        d_h, d_x, d_o = k.dsig("m_h"), k.dsig("m_x"), k.dsig("m_o")
        s_m1, s_ge, s_hi, s_lo, s_m2 = (k.sig(f"m_{n}", NC) for n in "m1 ge hi lo m2".split())
        s_t, s_x2 = k.sig("m_t", 3 * PAIR), k.sig("m_x2", PAIR)
        x1v = io["x1"].rearrange("(u a) s d -> u s a d", a=PAIR)
        x2v = io["x2"].rearrange("(u a) s d -> u s a d", a=PAIR)

        with nc.Block() as block:
            @block.sync
            def _(sp):
                def load(u):
                    s_m1.wait(sp, u.back(2))
                    d_h.inc(sp.dma_start(hT[u.slot][:, :, :, :], io["h"][u.no]), u)
                    s_t.wait(sp, u.back(2))
                    d_x.inc(sp.dma_start(x1[u.slot][:, :, :], x1v[u.no]), u)

                def store(u):
                    s_x2.wait(sp, u)
                    d_o.inc(sp.dma_start(x2v[u.no], x2[u.slot][:, :, :]), u)
                run_steps(sp, [(0, load), (3, store)], units, 3)
                for s in range(2):
                    d_o.wait(sp, Unit(0, units - 2 + s))

            @block.tensor
            def _(pe):
                e_now, e_before = {}, {}

                def read(u):
                    values = read_experts(nc, pe, w["idx"], u.no, slice(0, 6))
                    e_before.update({2: values[0], 3: values[1]})
                    e_now.update(enumerate(values[2:]))

                def read_last(u):
                    if u.static and u.no == units - 1:
                        values = read_experts(nc, pe, w["idx"], units, slice(0, 2))
                        e_before.update({2: values[0], 3: values[1]})

                def up(n):
                    a, ex, half = n // 4, n // 2 % 2, n % 2

                    def go(u):
                        if n == 0:
                            d_h.wait(pe, u)
                        at = slice(a * S, (a + 1) * S)
                        e = e_now[2 * a + ex]
                        for j in range(4):
                            cols = slice((4 * half + j) * P, (4 * half + j + 1) * P)
                            for kb in range(KB):
                                m = three_passes(pe, hid_bank[n % 4][:, j * S:(j + 1) * S],
                                                 w["w1_hi"][:, bass.ds(e, 1), kb, cols].rearrange("p o n -> p (o n)"),
                                                 w["w1_lo"][:, bass.ds(e, 1), kb, cols].rearrange("p o n -> p (o n)"),
                                                 hT[u.slot][:, 0, kb, at], hT[u.slot][:, 1, kb, at], kb == 0,
                                                 kb == KB - 1)
                        m.then_inc(s_m1.sem, 1)
                    return go

                def down(n, table):
                    a, ex, half = n // 4, n // 2 % 2, n % 2

                    def go(u):
                        s_lo.wait(pe, u, n + 1)
                        if n % 4 == 0:
                            s_x2.wait(pe, u.back(1), a + 1)
                        e = table[2 * a + ex]
                        o = y_bank[a][ex]
                        for j in range(4):
                            row = w["w2"][:, bass.ds(e, 1), 4 * half + j, :, :].rearrange("p o t n -> p (o t n)")
                            pe.matmul(o[:, :], hh[n % NH][:, j, :], row, start=half == 0 and j == 0, stop=False,
                                      skip_group_check=True)
                            m = pe.matmul(o[:, 0:D], hl[n % NH][:, j, :], row[:, 0:D], start=False, stop=False,
                                          skip_group_check=True)
                        if half == 1:
                            m = pe.matmul(o[:, 0:D], c["ones6"][:, 0:S], w["b2"][:, bass.ds(e * D, D)], start=False,
                                          stop=True, skip_group_check=True)
                        m.then_inc(s_m2.sem, 1)
                    return go

                tasks = [(1, read), (2, read_last)]
                for n in range(NC):
                    tasks.append((1, up(n)))
                    tasks.append((1, down(n - 3, e_now)) if n >= 3 else (2, down(n + NC - 3, e_before)))
                run_steps(pe, tasks, units, 3)

            @block.scalar
            def _(act):
                e_now = {}

                def read(u):
                    e_now.update(enumerate(read_experts(nc, act, w["idx"], u.no, slice(2, 6))))

                def gelu(n):
                    a, ex, half = n // 4, n // 2 % 2, n % 2

                    def go(u):
                        s_m1.wait(act, u, n + 1)
                        s_lo.wait(act, u, n + 1 - NH)
                        e = e_now[2 * a + ex]
                        for j in range(4):
                            i = act.activation(hf[n % NH][:, j, :], hid_bank[n % 4][:, j * S:(j + 1) * S], ACT.Gelu,
                                               bias=w["b1"][:, bass.ds(e * HB + (4 * half + j), 1)],
                                               scale=p2(-LN_X - W_X))
                        i.then_inc(s_ge.sem, 1)
                    return go
                run_steps(act, [(1, read)] + [(1, gelu(n)) for n in range(NC)], units, 3)

            @block.vector
            def _(v):
                def split(n):
                    def go(u):
                        s_ge.wait(v, u, n + 1)
                        s_m2.wait(v, u, n + 1 - NH)
                        v.tensor_scalar(hh[n % NH][:, :, :], hf[n % NH][:, :, :], p2(H_X), None, ALU.mult)\
                         .then_inc(s_hi.sem, 1)
                        s_hi.wait(v, u, n + 1)
                        v.scalar_tensor_tensor(out=hl[n % NH][:, :, :], in0=hf[n % NH][:, :, :], scalar=p2(H_X),
                                               in1=hh[n % NH][:, :, :], op0=ALU.mult, op1=ALU.subtract)\
                         .then_inc(s_lo.sem, 1)
                    return go

                def add(a):
                    def go(u):
                        s_m2.wait(v, u, 4 * (a + 1))
                        if a == 0:
                            d_x.wait(v, u)
                            d_o.wait(v, u.back(2))
                        at = x1[u.slot][:, a, :]
                        for i in range(4):
                            ex, part = i // 2, i % 2
                            to, done = (sums[i][:, a, :], s_t) if i < 3 else (x2[u.slot][:, a, :], s_x2)
                            v.scalar_tensor_tensor(out=to, in0=y_bank[a][ex][:, part * D:(part + 1) * D],
                                                   scalar=gate[:, bass.ds(u.no * PAIR + a, 1), ex], in1=at,
                                                   op0=ALU.mult, op1=ALU.add).then_inc(done.sem, 1)
                            if i < 3:
                                s_t.wait(v, u, 3 * a + i + 1)
                            at = to
                    return go

                tasks = []
                for n in range(NC):
                    tasks.append((1, split(n)))
                    if n == 2:
                        tasks.append((2, add(1)))
                    if n == NC - 1:
                        tasks.append((1, add(0)))
                run_steps(v, tasks, units, 3)


def shared_head_buffers(k):
    return {"wa": (k.sb("wa_hi", [P, 1, P], F16), k.sb("wa_lo", [P, 1, P], F16)),
            "wo": (k.sb("wo2_hi", [P, KB, D], F16), k.sb("wo2_lo", [P, KB, D], F16)),
            "mask": k.sb("mask4", [P, CH * S], BF16), "maskT": k.sb("maskT4", [P, CH * S], BF16)}


def prepare_shared_heads(kk, c, w, io):
    masked = -1e20 * p2(2 * QK_X)
    bd = [kk.sb(f"bd{i}", [P, P], F32) for i in range(3)]
    wo = kk.sb("wo_raw2", [P, KB, D], F32)
    woT = kk.sb("woT2", [P, KB, D], F32)
    mi = kk.sb("mask_int", [P, S], I32)
    b1, b2, b3, b4 = (kk.ps(f"sh_ps{i}") for i in range(4))
    s_z, s_ld, s_mk, s_pe, s_v, s_a = (kk.sem(f"sh_{x}") for x in ("z", "ld", "mk", "pe", "v", "a"))

    def gpsimd(g):
        for t in bd:
            g.memset(t[:, :], 0.0).then_inc(s_z, 1)
        g.dma_start(mi[:, :], io["mask"].rearrange("a b s n -> (a b s) n")).then_inc(s_mk, 16)
        g.dma_start(wo[:, :, :], io["L1_xattn_Wo"].rearrange("(b p) n -> p b n", p=P)).then_inc(s_ld, 16)
        g.wait_ge(s_z, 3)
        for t, name in zip(bd, ("Wq", "Wk", "Wv")):
            for h in range(P // DK):
                at = slice(h * DK, (h + 1) * DK)
                g.dma_start(t[at, at], io[f"L1_xattn_{name}"]).then_inc(s_ld, 16)

    def tensor(pe):
        pe.wait_ge(s_ld, 16 * (3 * (P // DK) + 1))
        pe.matmul(b1[:, 0:P], bd[0][:, :], bd[1][:, :], start=True, stop=True).then_inc(s_pe, 1)
        for ib in range(KB):
            for ob in range(KB):
                m = pe.transpose(b2[:, ib * D + ob * P:ib * D + (ob + 1) * P], wo[:, ob, ib * P:(ib + 1) * P],
                                 c["ident"][:, :])
        m.then_inc(s_pe, 1)
        pe.wait_ge(s_v, 1)
        for ib in range(KB):
            m = pe.matmul(b3[:, ib * D:(ib + 1) * D], bd[2][:, :], woT[:, ib, :], start=True, stop=True)
        m.then_inc(s_pe, 1)
        pe.wait_ge(s_v, 1 + CH)
        pe.transpose(b4[:, 0:S // 2].bitcast(BF16), w["mask"][:, 0:S], c["identb"][:, :]).then_inc(s_pe, 1)

    def scalar(act):
        act.wait_ge(s_pe, 1)
        act.activation(w["wa"][0][:, 0, :], b1[:, 0:P], ACT.Copy, scale=p2(W_X)).then_inc(s_a, 1)
        act.wait_ge(s_pe, 3)
        act.activation(w["wo"][0][:, :, :], v4(b3[:, :]), ACT.Copy, scale=p2(W_X)).then_inc(s_a, 1)

    def vector(v):
        v.wait_ge(s_pe, 2)
        v.tensor_copy(woT[:, :, :], v4(b2[:, :])).then_inc(s_v, 1)
        v.wait_ge(s_mk, 16)
        for j in range(CH):
            v.tensor_scalar(w["mask"][:, j * S:(j + 1) * S], mi[:, :], 0.0, masked, ALU.is_equal,
                            ALU.mult).then_inc(s_v, 1)
        v.wait_ge(s_a, 1)
        v.scalar_tensor_tensor(out=w["wa"][1][:, 0, :], in0=b1[:, 0:P], scalar=p2(W_X), in1=w["wa"][0][:, 0, :],
                               op0=ALU.mult, op1=ALU.subtract)
        v.wait_ge(s_a, 2)
        v.scalar_tensor_tensor(out=w["wo"][1][:, :, :], in0=v4(b3[:, :]), scalar=p2(W_X),
                               in1=w["wo"][0][:, :, :], op0=ALU.mult, op1=ALU.subtract)
        v.wait_ge(s_pe, 4)
        for j in range(CH):
            v.tensor_copy(w["maskT"][:, j * S:(j + 1) * S], b4[:, 0:S // 2].bitcast(BF16))

    return {"tensor": tensor, "scalar": scalar, "vector": vector, "gpsimd": gpsimd}


F_X = 4


def spiking(nc, k0, c, w, io, n_seq):
    units = n_seq // PAIR
    NC = HB // 2
    STEPS, BETA = 5, 0.9
    with ExitStack() as ctx:
        k = Kit(nc, ctx, f"{k0.stage}_loop", k0.whole)
        two = lambda name, shape, dt: [k.sb(f"{name}{i}", shape, dt) for i in range(2)]
        hT = two("sp_h", [P, 2, KB, PAIR * S], F16)
        x3 = two("sp_x3", [P, PAIR, D], F32)
        out = two("sp_out", [P, PAIR, D], F32)
        y = two("sp_y", [P, PAIR, D], F32)
        mem, pot, cnt = (k.sb(f"sp_{n}", [P, PAIR, D], F32) for n in ("mem", "pot", "cnt"))
        r = [k.sb(f"sp_r{i}", [P, 2, PAIR * S], F32) for i in range(4)]
        q = [k.sb(f"sp_q{i}", [P, 2, PAIR * S], F32) for i in range(4)]
        fh = [k.sb(f"sp_fh{i}", [P, 2, PAIR * S], F16) for i in range(4)]
        fl = [k.sb(f"sp_fl{i}", [P, 2, PAIR * S], F16) for i in range(4)]
        hid_bank = [k.ps(f"sp_hid{i}") for i in range(4)]
        y_bank = [k.ps(f"sp_yb{i}") for i in range(2)]
        d_h, d_x, d_o = k.dsig("p_h"), k.dsig("p_x"), k.dsig("p_o")
        s_m1, s_r, s_q, s_hi, s_m2 = (k.sig(f"p_{n}", NC) for n in "m1 r q hi m2".split())
        V_LOW = NC // 2
        s_lov, s_log = k.sig("p_lov", V_LOW), k.sig("p_log", NC - V_LOW)
        s_y, s_out = k.sig("p_y"), k.sig("p_out")
        s_sp = k.sig("p_sp", 1 + 3 * (STEPS - 1))
        x3v = io["x3"].rearrange("(u a) s d -> u s a d", a=PAIR)
        outv = io["out"].rearrange("(u a) s d -> u s a d", a=PAIR)

        def wait_low(eng, u, n):
            if n < V_LOW:
                s_lov.wait(eng, u, n + 1)
            else:
                s_log.wait(eng, u, n - V_LOW + 1)

        def low_part(eng, u, n):
            s_hi.wait(eng, u, n + 1)
            s_q.wait(eng, u, n + 1)
            done = s_lov if n < V_LOW else s_log
            eng.tensor_tensor(fl[n][:, :, :], q[n][:, :, :], fh[n][:, :, :], ALU.subtract).then_inc(done.sem, 1)

        with nc.Block() as block:
            @block.sync
            def _(sp):
                def load(u):
                    s_m1.wait(sp, u.back(2))
                    d_h.inc(sp.dma_start(hT[u.slot][:, :, :, :], io["h3"][u.no]), u)

                def load_x(u):
                    s_out.wait(sp, u.back(2))
                    d_x.inc(sp.dma_start(x3[u.slot][:, :, :], x3v[u.no]), u)

                def store(u):
                    s_out.wait(sp, u)
                    d_o.inc(sp.dma_start(outv[u.no], out[u.slot][:, :, :]), u)
                run_steps(sp, [(0, load), (1, load_x), (3, store)], units, 3)
                for s in range(2):
                    d_o.wait(sp, Unit(0, units - 2 + s))

            @block.tensor
            def _(pe):
                def up(n):
                    def go(u):
                        if n == 0:
                            d_h.wait(pe, u)
                        s_r.wait(pe, u, n - 3)
                        hi, lo = w["wf"]
                        for j in range(2):
                            cols = slice((2 * n + j) * P, (2 * n + j + 1) * P)
                            for kb in range(KB):
                                m = three_passes(pe, hid_bank[n % 4][:, j * 256:(j + 1) * 256], hi[:, kb, cols], lo[:, kb, cols],
                                                 hT[u.slot][:, 0, kb, :], hT[u.slot][:, 1, kb, :], kb == 0, kb == KB - 1)
                        m.then_inc(s_m1.sem, 1)
                    return go

                def down(n):
                    def go(u):
                        wait_low(pe, u, n)
                        if n == 0:
                            s_y.wait(pe, u.back(2))
                        hi, lo = w["wp"]
                        for j in range(2):
                            for a in range(PAIR):
                                o = y_bank[u.slot][:, a * D:(a + 1) * D]
                                at = slice(a * S, (a + 1) * S)
                                hb = 2 * n + j
                                st, sto = hb == 0 and a == 0, hb == HB - 1 and a == PAIR - 1
                                for i, (l, rr) in enumerate(((fh, hi), (fh, lo), (fl, hi))):
                                    m = pe.matmul(o, l[n % 4][:, j, at], rr[:, hb, :], start=st and i == 0,
                                                  stop=sto and i == 2, skip_group_check=True)
                        m.then_inc(s_m2.sem, 1)
                    return go
                tasks = []
                for n in range(NC):
                    tasks.append((1, up(n)))
                    tasks.append((1, down(n - 2)) if n >= 2 else (2, down(n + NC - 2)))
                run_steps(pe, tasks, units, 3)

            @block.scalar
            def _(act):
                def relu(n):
                    def go(u):
                        s_m1.wait(act, u, n + 1)
                        s_q.wait(act, u.back(1), n + 1)
                        act.activation(r[n][:, :, :], v4(hid_bank[n][:, :]), ACT.Relu,
                                       scale=p2(F_X // 2 - LN_X - W_X)).then_inc(s_r.sem, 1)
                    return go

                def square(n):
                    def go(u):
                        s_r.wait(act, u, n + 1)
                        s_m2.wait(act, u.back(1), n + 1)
                        act.activation(fh[n][:, :, :], r[n][:, :, :], ACT.Square).then_inc(s_hi.sem, 1)
                    return go

                def copy_y(u):
                    s_m2.wait(act, u)
                    s_out.wait(act, u.back(2))
                    act.activation(y[u.slot][:, :, :], y_bank[u.slot][:, :].rearrange("p (a n) -> p a n", a=PAIR), ACT.Copy,
                                   scale=p2(-F_X - W_X)).then_inc(s_y.sem, 1)
                tasks = []
                for n in range(NC):
                    tasks += [(1, relu(n)), (1, square(n))]
                    if n == 1:
                        tasks.append((2, copy_y))
                run_steps(act, tasks, units, 3)

            @block.gpsimd
            def _(g):
                def sq(n):
                    def go(u):
                        s_r.wait(g, u, n + 1)
                        wait_low(g, u.back(1), n)
                        g.tensor_tensor(q[n][:, :, :], r[n][:, :, :], r[n][:, :, :], ALU.mult).then_inc(s_q.sem, 1)
                    return go
                def low(n):
                    return lambda u: low_part(g, u, n)

                tasks = []
                for n in range(NC):
                    tasks += [(1, sq(n))] + ([(1, low(n))] if n >= V_LOW else [])
                run_steps(g, tasks, units, 3)

            @block.vector
            def _(v):
                def decay(step):
                    def go(u):
                        yy = y[u.slot][:, :, :]
                        if step == 2:
                            s_y.wait(v, u)
                            s_out.wait(v, u.back(1))
                            v.tensor_scalar(cnt[:, :, :], yy, 1.0, None, ALU.is_gt).then_inc(s_sp.sem, 1)
                        s_sp.wait(v, u, 1 + 3 * (step - 2))
                        v.scalar_tensor_tensor(out=pot[:, :, :], in0=yy if step == 2 else mem[:, :, :], scalar=BETA,
                                               in1=yy, op0=ALU.mult, op1=ALU.add).then_inc(s_sp.sem, 1)
                    return go

                def fire(step):
                    def go(u):
                        m = y[u.slot][:, :, :] if step == 2 else mem[:, :, :]
                        at = 2 + 3 * (step - 2)
                        s_sp.wait(v, u, at)
                        v.scalar_tensor_tensor(out=mem[:, :, :], in0=m, scalar=1.0, in1=pot[:, :, :], op0=ALU.is_gt,
                                               op1=ALU.subtract, reverse1=True).then_inc(s_sp.sem, 1)
                        s_sp.wait(v, u, at + 1)
                        v.scalar_tensor_tensor(out=cnt[:, :, :], in0=mem[:, :, :], scalar=1.0, in1=cnt[:, :, :],
                                               op0=ALU.is_gt, op1=ALU.add).then_inc(s_sp.sem, 1)
                    return go

                def add_spikes(u):
                    d_x.wait(v, u)
                    d_o.wait(v, u.back(2))
                    s_sp.wait(v, u)
                    v.scalar_tensor_tensor(out=out[u.slot][:, :, :], in0=cnt[:, :, :], scalar=1.0 / STEPS,
                                           in1=x3[u.slot][:, :, :], op0=ALU.mult, op1=ALU.add).then_inc(s_out.sem, 1)

                def low(n):
                    return lambda u: low_part(v, u, n)

                run_steps(v, [(3, decay(4)), (1, low(0)), (3, fire(4)), (3, decay(5)), (1, low(1)), (3, fire(5)),
                              (3, add_spikes), (2, decay(2)), (2, fire(2)), (2, decay(3)), (2, fire(3))], units, 3)


def build(nc, io, n_seq=128):
    with ExitStack() as ctx:
        k = Kit(nc, ctx, "all")
        for name in ("x1", "x2", "x3"):
            io[name] = nc.dram_tensor(f"{name}_scratch", (n_seq, S, D), F32, kind="Internal").ap()
        for name in ("h", "h3"):
            io[name] = nc.dram_tensor(f"{name}_scratch", (n_seq // PAIR, P, 2, KB, PAIR * S), F16, kind="Internal").ap()
        io["ct"] = nc.dram_tensor("ct_scratch", (n_seq // PAIR, 2, D, PAIR * S), F16, kind="Internal").ap()
        idx_d = nc.dram_tensor("idx_scratch", (n_seq, 2), U32, kind="Internal").ap()
        top = k.sb("top", [P, n_seq, 2], F32)
        gate = k.sb("gate", [P, n_seq, 2], F32)
        c, make_constants, make_selectors = constants(k)
        late_mats = [("wf", io["L1_ffn_W_fc"], True), ("wp", io["L1_ffn_W_proj"], True)]
        late_rows = [("bo", io["L1_xattn_bo"]), ("b2", io["L0_ffn_b2"])]
        w_late = weight_buffers(k, late_mats, late_rows)
        w_late.update(shared_head_buffers(k))
        with ExitStack() as c1:
            k1 = Kit(nc, c1, "phase1")
            mats = [("wq", io["L0_xattn_w_q"], True), ("wk", io["L0_xattn_w_k"], True), ("wv", io["L0_xattn_w_v"], True),
                    ("wo", io["L0_xattn_w_o"], True), ("wg", io["L0_ffn_Wg"], False)]
            biases = [("bq", io["L0_xattn_b_q"]), ("bk", io["L0_xattn_b_k"]), ("bv", io["L0_xattn_b_v"]),
                      ("bo", io["L0_xattn_b_o"]), ("bg", io["L0_ffn_bg"])]
            w = weight_buffers(k1, mats, biases)
            with ExitStack() as tmp:
                split, place_rows = prepare_weights(Kit(nc, tmp, "prep1", k1), c, w, mats, biases)
                together(nc, make_constants, split, make_selectors, {"sync": place_rows})
            attention(nc, k1, c, w, io, n_seq, True, top, idx_d)
            k1.end_phase()
        with ExitStack() as c2:
            k2 = Kit(nc, c2, "phase2")
            w = expert_buffers(k2, n_seq)
            w["b2"] = w_late["b2"]
            with ExitStack() as tmp:
                kk = Kit(nc, tmp, "prep2", k2)
                split, place_rows = prepare_weights(kk, c, w_late, late_mats, late_rows)
                together(nc, gates(kk, top, gate, n_seq), split, prepare_shared_heads(kk, c, w_late, io),
                         prepare_experts(kk, c, w, io, idx_d), {"gpsimd": place_rows})
            experts(nc, k2, c, w, io, n_seq, gate)
            k2.end_phase()
        with ExitStack() as c3:
            k3 = Kit(nc, c3, "phase3")
            attention(nc, k3, c, w_late, io, n_seq, False)
            k3.end_phase()
        with ExitStack() as c4:
            k4 = Kit(nc, c4, "phase4")
            spiking(nc, k4, c, w_late, io, n_seq)


_ROWS = ("L0_xattn_b_q", "L0_xattn_b_k", "L0_xattn_b_v", "L0_xattn_b_o", "L0_ffn_bg", "L1_xattn_bo")


def kernel(**inputs):
    import numpy as _np
    import concourse.bacc as _bacc
    from concourse.bass_utils import run_bass_kernel_spmd as _run

    nc = _bacc.Bacc("TRN2", target_bir_lowering=False, num_devices=1)
    arrays, io = {}, {}
    short = {"ctx_1024": "ctx", "mask_1x1xSxS2_ik1": "mask"}
    for name, value in inputs.items():
        a = _np.ascontiguousarray(value)
        if name in _ROWS:
            a = a.reshape(1, -1)
        key = short.get(name, name)
        arrays[f"in_{key}"] = a
        io[key] = nc.dram_tensor(f"in_{key}", a.shape, mybir.dt.from_np(a.dtype), kind="ExternalInput").ap()
    n_seq = io["x"].shape[0]
    io["out"] = nc.dram_tensor("out_x", tuple(io["x"].shape), F32, kind="ExternalOutput").ap()
    build(nc, io, n_seq)
    r = _run(nc, [arrays], core_ids=[0])
    return r.results[0]["out_x"]
```
